# Optimizing a Trainium2 kernel written in Bass

```python
import numpy as np
import jax
import jax.numpy as jnp

def _softmax(x, axis=-1):
    return jax.nn.softmax(x, axis=axis)

def _gelu(x):
    return jax.nn.gelu(x, approximate=True)

def _silu(x):
    return jax.nn.silu(x)

def _sigmoid(x):
    return jax.nn.sigmoid(x)

def _layernorm(x, axis=-1, eps=1e-05):
    m = jnp.mean(x, axis=axis, keepdims=True)
    v = jnp.var(x, axis=axis, keepdims=True)
    return (x - m) / jnp.sqrt(v + eps)

def _scatter_add(tgt, idx, src, axis=0):
    return tgt.at[idx].add(src)

def _segment_sum(src, seg, n):
    return jax.ops.segment_sum(src, seg, n)
kernel_name = 'mk_decoder_postln_d1_seqx_r8_298195'

def setup_inputs(seed: int=0):
    np.random.seed(seed)
    _w = jnp.asarray

    def _rec_inputs():
        import jax
        import jax.numpy as jnp
        _rk = jax.random.key(seed)
        x = -0.0002928 + 1 * jax.random.normal(jax.random.fold_in(_rk, 1), (64, 64, 256), jnp.float32)
        _lenS = 64 - jax.random.randint(jax.random.fold_in(_rk, 7), (64,), 0, max(1, 64 // 4) + 1, jnp.int32)
        _lenS2 = 64 - jax.random.randint(jax.random.fold_in(_rk, 8), (64,), 0, max(1, 64 // 4) + 1, jnp.int32)
        _ctx_512P = jax.random.normal(jax.random.fold_in(_rk, 11), (64, 16, 64), jnp.float32)
        _ctx_512c = jax.random.dirichlet(jax.random.fold_in(_rk, 511), 0.3 * jnp.ones((16,), jnp.float32), (64, 64))
        _ctx_512t = jnp.einsum('bsk,bkd->bsd', _ctx_512c, _ctx_512P)
        _ctx_512t = _ctx_512t * jax.lax.rsqrt(jnp.mean(jnp.square(_ctx_512t)) + 1e-12) * 0.953939
        ctx_512 = 0.000227908 + 0.99994 * (_ctx_512t + 0.3 * jax.random.normal(jax.random.fold_in(_rk, 611), (64, 64, 64), jnp.float32))
        return (x, ctx_512)
    x, ctx_512 = _rec_inputs()

    def _L0_attn_setup():
        import jax, jax.numpy as jnp
        import numpy as np
        HIDDEN = 256
        NUM_HEADS = 16
        HEAD_DIM = 128
        WINDOW_SIZE = 64
        NUM_GLOBAL = 16
        SCALING = HEAD_DIM ** (-0.5)

        def _sliding_mask(q_len: int, kv_len: int) -> jnp.ndarray:
            q_pos = jnp.arange(q_len)[:, None]
            kv_pos = jnp.arange(kv_len)[None, :]
            half_window = WINDOW_SIZE // 2
            local = jnp.abs(q_pos - kv_pos) < half_window
            glob = (q_pos < NUM_GLOBAL) | (kv_pos < NUM_GLOBAL)
            mask = local | glob
            return jnp.where(mask, 0.0, -jnp.inf).astype(jnp.float32)
        key = jax.random.key(seed)
        ks = jax.random.split(key, 5)
        std = HIDDEN ** (-0.5)
        hidden_states = jax.random.normal(ks[0], (1, 512, HIDDEN), dtype=jnp.float32)
        Wq = jax.random.normal(ks[1], (HIDDEN, NUM_HEADS * HEAD_DIM), dtype=jnp.float32) * std
        Wk = jax.random.normal(ks[2], (HIDDEN, NUM_HEADS * HEAD_DIM), dtype=jnp.float32) * std
        Wv = jax.random.normal(ks[3], (HIDDEN, NUM_HEADS * HEAD_DIM), dtype=jnp.float32) * std
        Wo = jax.random.normal(ks[4], (NUM_HEADS * HEAD_DIM, HIDDEN), dtype=jnp.float32) * std
        return {'hidden_states': hidden_states, 'Wq': Wq, 'Wk': Wk, 'Wv': Wv, 'Wo': Wo}
    _L0_attn_all = _L0_attn_setup()
    _L0_attn_in = {k: v for k, v in _L0_attn_all.items() if k in ('Wq', 'Wk', 'Wv', 'Wo')}
    del _L0_attn_all

    def _L0_xattn_setup():
        import jax, jax.numpy as jnp
        import numpy as np
        B, S, L = (2, 128, 128)
        DIM_Q, H, K, D_C, D_CQ, R = (256, 16, 128, 64, 192, 64)

        def _rope_tables(seq_len, dim, dtype):
            inv_freq = 1.0 / 10000.0 ** (jnp.arange(0, dim, 2, dtype=dtype) / dim)
            t = jnp.arange(seq_len, dtype=dtype)
            freqs = t[:, None] * inv_freq[None, :]
            sin = jnp.repeat(jnp.sin(freqs), 2, axis=-1)
            cos = jnp.repeat(jnp.cos(freqs), 2, axis=-1)
            return (sin, cos)

        def _rotate_half(x):
            h = x.shape[-1] // 2
            return jnp.concatenate([-x[..., h:], x[..., :h]], axis=-1)
        key = jax.random.key(seed)
        ks = jax.random.split(key, 8)
        s_in = 1.0 / np.sqrt(DIM_Q)
        s_k = 1.0 / np.sqrt(K)
        s_cq = 1.0 / np.sqrt(D_CQ)
        s_c = 1.0 / np.sqrt(D_C)
        return {'hidden_q': jax.random.normal(ks[0], (B, S, DIM_Q), jnp.float32), 'kv_c': jax.random.normal(ks[1], (B, L, D_C), jnp.float32), 'Wq': jax.random.normal(ks[2], (H * K, DIM_Q), jnp.float32) * s_in, 'w_kc_q': jax.random.normal(ks[3], (H, K, D_CQ), jnp.float32) * s_k, 'w_kc_kv': jax.random.normal(ks[4], (H, K, D_C), jnp.float32) * s_k, 'W_qr': jax.random.normal(ks[5], (H, D_CQ, R), jnp.float32) * s_cq / np.sqrt(R), 'W_kr': jax.random.normal(ks[6], (H, D_C, R), jnp.float32) * s_c, 'Wo': jax.random.normal(ks[7], (DIM_Q, H * K), jnp.float32) * s_k}
    _L0_xattn_all = _L0_xattn_setup()
    _L0_xattn_in = {k: v for k, v in _L0_xattn_all.items() if k in ('Wq', 'w_kc_q', 'w_kc_kv', 'W_qr', 'W_kr', 'Wo')}
    del _L0_xattn_all

    def _L0_ffn_setup():
        import jax, jax.numpy as jnp
        import numpy as np
        E = 16
        K = 2
        D = 256
        I = 176
        CAP = 128
        VOCAB = 16160
        key = jax.random.key(seed)
        ks = jax.random.split(key, 11)
        B, S = (4, 128)
        sd = 1.0 / np.sqrt(D)
        si = 1.0 / np.sqrt(I)
        return {'x': jax.random.normal(ks[0], (B, S, D), jnp.float32), 'input_ids': jax.random.randint(ks[1], (B, S), 0, VOCAB, dtype=jnp.int64), 'gate_w': jax.random.normal(ks[2], (E, D), jnp.float32) * sd, 'gate_b': jax.random.normal(ks[3], (E,), jnp.float32) * 0.01, 'W1': jax.random.normal(ks[4], (E, I, D), jnp.float32) * sd, 'W3': jax.random.normal(ks[5], (E, I, D), jnp.float32) * sd, 'W2': jax.random.normal(ks[6], (E, D, I), jnp.float32) * si, 'Ws1': jax.random.normal(ks[7], (I, D), jnp.float32) * sd, 'Ws3': jax.random.normal(ks[8], (I, D), jnp.float32) * sd, 'Ws2': jax.random.normal(ks[9], (D, I), jnp.float32) * si}
    _L0_ffn_all = _L0_ffn_setup()
    _L0_ffn_in = {k: v for k, v in _L0_ffn_all.items() if k in ('input_ids', 'gate_w', 'gate_b', 'W1', 'W3', 'W2', 'Ws1', 'Ws3', 'Ws2')}
    del _L0_ffn_all
    return {'x': x, 'ctx_512': ctx_512, 'L0_attn_Wq': _L0_attn_in['Wq'], 'L0_attn_Wk': _L0_attn_in['Wk'], 'L0_attn_Wv': _L0_attn_in['Wv'], 'L0_attn_Wo': _L0_attn_in['Wo'], 'L0_xattn_Wq': _L0_xattn_in['Wq'], 'L0_xattn_w_kc_q': _L0_xattn_in['w_kc_q'], 'L0_xattn_w_kc_kv': _L0_xattn_in['w_kc_kv'], 'L0_xattn_W_qr': _L0_xattn_in['W_qr'], 'L0_xattn_W_kr': _L0_xattn_in['W_kr'], 'L0_xattn_Wo': _L0_xattn_in['Wo'], 'L0_ffn_input_ids': _L0_ffn_in['input_ids'], 'L0_ffn_gate_w': _L0_ffn_in['gate_w'], 'L0_ffn_gate_b': _L0_ffn_in['gate_b'], 'L0_ffn_W1': _L0_ffn_in['W1'], 'L0_ffn_W3': _L0_ffn_in['W3'], 'L0_ffn_W2': _L0_ffn_in['W2'], 'L0_ffn_Ws1': _L0_ffn_in['Ws1'], 'L0_ffn_Ws3': _L0_ffn_in['Ws3'], 'L0_ffn_Ws2': _L0_ffn_in['Ws2']}

def reference(x, ctx_512, L0_attn_Wq, L0_attn_Wk, L0_attn_Wv, L0_attn_Wo, L0_xattn_Wq, L0_xattn_w_kc_q, L0_xattn_w_kc_kv, L0_xattn_W_qr, L0_xattn_W_kr, L0_xattn_Wo, L0_ffn_input_ids, L0_ffn_gate_w, L0_ffn_gate_b, L0_ffn_W1, L0_ffn_W3, L0_ffn_W2, L0_ffn_Ws1, L0_ffn_Ws3, L0_ffn_Ws2):
    import jax
    import jax.numpy as jnp

    def _L0_attn_ref(hidden_states, Wq, Wk, Wv, Wo):
        import jax, jax.numpy as jnp
        import numpy as np
        HIDDEN = 256
        NUM_HEADS = 16
        HEAD_DIM = 128
        WINDOW_SIZE = 64
        NUM_GLOBAL = 16
        SCALING = HEAD_DIM ** (-0.5)

        def _sliding_mask(q_len: int, kv_len: int) -> jnp.ndarray:
            q_pos = jnp.arange(q_len)[:, None]
            kv_pos = jnp.arange(kv_len)[None, :]
            half_window = WINDOW_SIZE // 2
            local = jnp.abs(q_pos - kv_pos) < half_window
            glob = (q_pos < NUM_GLOBAL) | (kv_pos < NUM_GLOBAL)
            mask = local | glob
            return jnp.where(mask, 0.0, -jnp.inf).astype(jnp.float32)
        bsz, q_len, _ = hidden_states.shape
        q = (hidden_states @ Wq).reshape(bsz, q_len, NUM_HEADS, HEAD_DIM).transpose(0, 2, 1, 3)
        k = (hidden_states @ Wk).reshape(bsz, q_len, NUM_HEADS, HEAD_DIM).transpose(0, 2, 1, 3)
        v = (hidden_states @ Wv).reshape(bsz, q_len, NUM_HEADS, HEAD_DIM).transpose(0, 2, 1, 3)
        mask = _sliding_mask(q_len, q_len)[None, None]
        scores = jnp.einsum('bhqd,bhkd->bhqk', q, k) * SCALING + mask
        attn = jax.nn.softmax(scores.astype(jnp.float32), axis=-1).astype(q.dtype)
        out = jnp.einsum('bhqk,bhkd->bhqd', attn, v)
        out = out.transpose(0, 2, 1, 3).reshape(bsz, q_len, NUM_HEADS * HEAD_DIM)
        return out @ Wo

    def _L0_xattn_ref(hidden_q, kv_c, Wq, w_kc_q, w_kc_kv, W_qr, W_kr, Wo):
        import jax, jax.numpy as jnp
        import numpy as np
        B, S, L = (2, 128, 128)
        DIM_Q, H, K, D_C, D_CQ, R = (256, 16, 128, 64, 192, 64)

        def _rope_tables(seq_len, dim, dtype):
            inv_freq = 1.0 / 10000.0 ** (jnp.arange(0, dim, 2, dtype=dtype) / dim)
            t = jnp.arange(seq_len, dtype=dtype)
            freqs = t[:, None] * inv_freq[None, :]
            sin = jnp.repeat(jnp.sin(freqs), 2, axis=-1)
            cos = jnp.repeat(jnp.cos(freqs), 2, axis=-1)
            return (sin, cos)

        def _rotate_half(x):
            h = x.shape[-1] // 2
            return jnp.concatenate([-x[..., h:], x[..., :h]], axis=-1)
        b, s, _ = hidden_q.shape
        l = kv_c.shape[1]
        q_hk = (hidden_q @ Wq.T).reshape(b, s, H, K)
        q_big = jnp.einsum('bshk,hkq->bshq', q_hk, w_kc_q)
        sin, cos = _rope_tables(l, D_C, kv_c.dtype)
        kv_rope = kv_c * cos[None] + _rotate_half(kv_c) * sin[None]
        q_r = jnp.einsum('bshq,hqr->bhsr', q_big, W_qr)
        k_r = jnp.einsum('bld,hdr->bhlr', kv_rope, W_kr)
        scores = jnp.einsum('bhsr,bhlr->bhsl', q_r, k_r)
        attn = jax.nn.softmax(scores, axis=-1)
        ctx_c = jnp.einsum('bhsl,bld->bhsd', attn, kv_rope)
        ctx_lat = jnp.einsum('bhsd,hkd->bshk', ctx_c, w_kc_kv)
        out = ctx_lat.reshape(b, s, H * K) @ Wo.T
        return out

    def _L0_ffn_ref(x, input_ids, gate_w, gate_b, W1, W3, W2, Ws1, Ws3, Ws2):
        import jax, jax.numpy as jnp
        import numpy as np
        E = 16
        K = 2
        D = 256
        I = 176
        CAP = 128
        VOCAB = 16160
        shape = x.shape
        xt = x.reshape(-1, D)
        T = xt.shape[0]
        logits = xt.astype(jnp.float32) @ gate_w.astype(jnp.float32).T
        scores = jnp.sqrt(jax.nn.softplus(logits))
        _, idx = jax.lax.top_k(scores + gate_b, K)
        w = jnp.take_along_axis(scores, idx, axis=1)
        w = w / jnp.sum(w, axis=1, keepdims=True)
        e = idx.reshape(-1)
        onehot = jax.nn.one_hot(e, E, dtype=jnp.int32)
        pos = jnp.sum(onehot * (jnp.cumsum(onehot, axis=0) - 1), axis=1)
        valid = pos < CAP
        posc = jnp.where(valid, pos, 0)
        x_pairs = jnp.repeat(xt, K, axis=0)
        x_pairs = jnp.where(valid[:, None], x_pairs, 0.0)
        buf = jnp.zeros((E, CAP, D), xt.dtype).at[e, posc].add(x_pairs)
        g = jnp.einsum('ecd,eid->eci', buf, W1).astype(jnp.float32)
        u = jnp.einsum('ecd,eid->eci', buf, W3).astype(jnp.float32)
        h = (jax.nn.silu(g) * u).astype(xt.dtype)
        out = jnp.einsum('eci,edi->ecd', h, W2)
        y_pairs = out[e, posc] * (w.reshape(-1) * valid)[:, None]
        y = y_pairs.reshape(T, K, D).sum(axis=1)
        gs = jax.nn.silu((xt @ Ws1.T).astype(jnp.float32))
        us = (xt @ Ws3.T).astype(jnp.float32)
        shared = (gs * us).astype(xt.dtype) @ Ws2.T
        return (y + shared).astype(x.dtype).reshape(shape)
    x = _layernorm(x + _L0_attn_ref(x, L0_attn_Wq, L0_attn_Wk, L0_attn_Wv, L0_attn_Wo), axis=-1)
    x = _layernorm(x + _L0_xattn_ref(x, ctx_512, L0_xattn_Wq, L0_xattn_w_kc_q, L0_xattn_w_kc_kv, L0_xattn_W_qr, L0_xattn_W_kr, L0_xattn_Wo), axis=-1)
    x = _layernorm(x + _L0_ffn_ref(x, L0_ffn_input_ids, L0_ffn_gate_w, L0_ffn_gate_b, L0_ffn_W1, L0_ffn_W3, L0_ffn_W2, L0_ffn_Ws1, L0_ffn_Ws3, L0_ffn_Ws2), axis=-1)
    return x

_drawn_inputs = setup_inputs


def setup_inputs(seed=0):
    import zlib

    import numpy as np

    out = dict(_drawn_inputs(seed))
    spreads = {}
    factors = {}
    for name, (base, spread) in spreads.items():
        noise = np.random.default_rng([zlib.crc32(name.encode()), seed]).standard_normal(out[name].shape)
        drawn = base * np.exp(spread * noise) if base else spread * noise
        out[name] = jnp.asarray(drawn.astype(out[name].dtype))
    for name, factor in factors.items():
        out[name] = (out[name] * factor).astype(out[name].dtype)
    return out
```

```python
from contextlib import ExitStack

import concourse.bass as bass
from concourse import mybir

F32 = mybir.dt.float32
F32R = mybir.dt.float32r
ALU = mybir.AluOpType
ACT = mybir.ActivationFunctionType
AX = mybir.AxisListType

P = 128
BATCH, SEQ, DIM = 64, 64, 256
TOKENS = BATCH * SEQ
HEADS, HEAD_DIM = 16, 128
WINDOW, GLOBAL = 64, 16
KC = DIM // P
UNIT = 256
UNITS = TOKENS // UNIT
PAIRS = UNIT // P
UB = UNIT // SEQ
HS = 8
STEPS = HEADS // HS
HP = HS // 2
EPS = 1e-5
MASKED = -1e30


def local_attention(nc, x, xT, Wq, Wk, WvT, Wo, out):
    SCALE = float(HEAD_DIM) ** -0.5
    STAGE = 1024
    W_LOADS = 2 * KC * 2048 // STAGE
    B_LOADS = HEADS // 2
    RING = 4
    JOBS = PAIRS * 2 * KC

    with ExitStack() as ctx:
        def sb(name, shape, dt=F32):
            return ctx.enter_context(nc.sbuf_tensor("a_" + name, shape, dt))

        def ps(name, shape):
            return ctx.enter_context(nc.psum_tensor("a_" + name, shape, F32))

        def sem(name):
            return ctx.enter_context(nc.semaphore("a_" + name))

        stage = sb("stage", [P, 3, STAGE])
        wqk_hi = sb("wqk_hi", [P, 2, KC, 2048], F32R)
        wqk_lo = sb("wqk_lo", [P, 2, KC, 2048], F32R)
        wvo = sb("wvo", [P, HEADS * KC, 2, DIM], F32R)
        ident = sb("ident", [P, P])
        mask = sb("mask", [P, SEQ])
        x_res = sb("x_res", [P, PAIRS, DIM])
        x_raw = sb("x_raw", [P, UB, DIM])
        x_hi = sb("x_hi", [P, UB, DIM], F32R)
        x_lo = sb("x_lo", [P, UB, DIM], F32R)
        xT_raw = sb("xT_raw", [P, KC, UNIT])
        xT_hi = sb("xT_hi", [P, KC, UNIT], F32R)
        xT_lo = sb("xT_lo", [P, KC, UNIT], F32R)
        qk = sb("qk", [P, HS, 2, UNIT])
        s_sb = sb("s_sb", [P, PAIRS, HS, SEQ])
        row_max = sb("row_max", [P, PAIRS, HS])
        row_sum = sb("row_sum", [P, PAIRS, HS])
        inv_sum = sb("inv_sum", [P, PAIRS, HS])
        pT_hi = sb("pT_hi", [P, PAIRS, 2, HP, SEQ], F32R)
        pT_lo = sb("pT_lo", [P, PAIRS, 2, HP, SEQ], F32R)
        mix_hi = sb("mix_hi", [P, RING, HP, P], F32R)
        mix_lo = sb("mix_lo", [P, RING, HP, P], F32R)
        y = sb("y", [P, PAIRS, DIM])
        stats = sb("stats", [P, PAIRS, 6])
        mean_var = sb("mean_var", [P, PAIRS, 2])
        rstd = sb("rstd", [P, PAIRS, 1])
        power = sb("power", [P, 1])

        ps_s = ps("ps_s", [P, PAIRS, HS, SEQ])
        ps_qk = ps("ps_qk", [P, 2, 2, UNIT])
        ps_mix = ps("ps_mix", [P, 2, 512])
        ps_out = ps("ps_out", [P, PAIRS, 2, DIM])

        staged = [sem(f"staged{n}") for n in range(3)]
        xT_in = sem("xT_in")
        xd_in = sem("xd_in")
        xr_in = sem("xr_in")
        stored = sem("stored")
        w_hi = sem("w_hi")
        w_lo = sem("w_lo")
        fold_filled = sem("fold_filled")
        fold_hi = sem("fold_hi")
        fold_lo = sem("fold_lo")
        consts = sem("consts")
        xT_hi_done = sem("xT_hi_done")
        xT_lo_done = sem("xT_lo_done")
        x_hi_done = sem("x_hi_done")
        x_lo_done = sem("x_lo_done")
        qk_filled = sem("qk_filled")
        qk_copied = sem("qk_copied")
        s_filled = sem("s_filled")
        masked = sem("masked")
        maxed = sem("maxed")
        shifted = sem("shifted")
        exped = sem("exped")
        summed = sem("summed")
        inverted = sem("inverted")
        normed = sem("normed")
        t_filled = sem("t_filled")
        pT_hi_done = sem("pT_hi_done")
        pT_lo_done = sem("pT_lo_done")
        mix_filled = sem("mix_filled")
        mix_hi_done = sem("mix_hi_done")
        mix_lo_done = sem("mix_lo_done")
        proj_done = sem("proj_done")
        left_added = sem("left_added")
        right_added = sem("right_added")
        stats_done = sem("stats_done")
        stats_seen = sem("stats_seen")
        moments_done = sem("moments_done")
        var_done = sem("var_done")
        rstd_done = sem("rstd_done")
        y_done = sem("y_done")

        def staged_count(n):
            return sum(16 if m < W_LOADS else 32 for m in range(n % 3, n + 1, 3))

        block = ctx.enter_context(nc.Block())

        xT_v = xT.rearrange("(c p) t -> p c t", p=P)
        x_pairs = x.rearrange("(n p) d -> p n d", p=P)
        x_batches = x.rearrange("(b t) d -> t b d", t=SEQ)
        out_pairs = out.rearrange("(n p) d -> p n d", p=P)
        WvT_v = WvT.rearrange("(h k) d -> k h d", k=P)
        Wo_v = Wo.rearrange("(h k) d -> k h d", k=P)

        @block.sync
        def _(sp):
            def load_xT(u):
                if not (isinstance(u, int) and u == 0):
                    sp.wait_ge(xT_lo_done, u)
                sp.dma_start(xT_raw[:, :, :], xT_v[:, :, bass.ds(u * UNIT, UNIT)]).then_inc(xT_in, 16)

            def load_xd(u):
                if not (isinstance(u, int) and u == 0):
                    sp.wait_ge(x_lo_done, u)
                for e in range(2):
                    sp.dma_start(x_raw[64 * e:64 * e + 64, :, :], x_batches[:, bass.ds(u * UB, UB), :]) \
                        .then_inc(xd_in, 16)

            def load_xres(u):
                if not (isinstance(u, int) and u == 0):
                    sp.wait_ge(left_added, PAIRS * u)
                sp.dma_start(x_res[:, :, :], x_pairs[:, bass.ds(u * PAIRS, PAIRS), :]).then_inc(xr_in, 16)

            def store(u):
                sp.wait_ge(y_done, PAIRS * (u + 1))
                sp.dma_start(out_pairs[:, bass.ds(u * PAIRS, PAIRS), :], y[:, :, :]).then_inc(stored, 16)

            load_xT(0)
            n = 0
            for c in range(KC):
                for w in (Wq, Wk):
                    for half in range(2):
                        if n >= 3:
                            sp.wait_ge(w_lo, n - 2)
                        sp.dma_start(stage[:, n % 3, :], w[c * P:(c + 1) * P, half * STAGE:(half + 1) * STAGE]) \
                            .then_inc(staged[n % 3], 16)
                        n += 1
            for g in range(B_LOADS):
                if n - 3 < W_LOADS:
                    sp.wait_ge(w_lo, n - 2)
                else:
                    sp.wait_ge(fold_filled, n - 2 - W_LOADS)
                dst = stage[:, n % 3, :].rearrange("p (h w d) -> p h w d", h=2, w=2)
                sp.dma_start(dst[:, :, 0, :], WvT_v[:, 2 * g:2 * g + 2, :]).then_inc(staged[n % 3], 16)
                sp.dma_start(dst[:, :, 1, :], Wo_v[:, 2 * g:2 * g + 2, :]).then_inc(staged[n % 3], 16)
                n += 1
            load_xd(0)
            load_xres(0)
            load_xT(1)
            load_xd(1)
            with sp.Fori(1, UNITS - 1) as u:
                load_xT(u + 1)
                store(u - 1)
                load_xres(u)
                load_xd(u + 1)
            store(UNITS - 2)
            load_xres(UNITS - 1)
            store(UNITS - 1)
            sp.wait_ge(stored, 16 * UNITS)

        @block.gpsimd
        def _(pool):
            pool.memset(ident[:, :], 0.0).then_inc(consts, 1)
            pool.memset(power[:, :], -0.5).then_inc(consts, 1)
            pool.memset(mask[:, :], 0.0).then_inc(consts, 1)
            pool.wait_ge(consts, 3)
            pool.affine_select(out=ident[:, :], in_=ident[:, :], compare_op=ALU.not_equal, fill=1.0,
                               base=0, pattern=[[-1, P]], channel_multiplier=1).then_inc(consts, 1)
            n = 4
            for b in range(2):
                half = mask[b * SEQ:(b + 1) * SEQ, :]
                for sign in (1, -1):
                    pool.affine_select(out=half, in_=half, compare_op=ALU.is_ge, fill=MASKED,
                                       base=WINDOW // 2 - 1, pattern=[[sign, SEQ]],
                                       channel_multiplier=-sign).then_inc(consts, 1)
                    n += 1
                    pool.wait_ge(consts, n)
                pool.memset(mask[b * SEQ:(b + 1) * SEQ, 0:GLOBAL], 0.0).then_inc(consts, 1)
                pool.affine_select(out=half[:, GLOBAL:SEQ], in_=half[:, GLOBAL:SEQ], compare_op=ALU.is_ge, fill=0.0,
                                   base=-GLOBAL, pattern=[[0, SEQ - GLOBAL]],
                                   channel_multiplier=1).then_inc(consts, 1)
                n += 2
            pool.wait_ge(consts, n)

            def split_xT(u):
                pool.wait_ge(xT_hi_done, u + 1)
                pool.tensor_tensor(xT_lo[:, :, :], xT_raw[:, :, :], xT_hi[:, :, :].bitcast(F32), ALU.subtract) \
                    .then_inc(xT_lo_done, 1)

            def split_x(u):
                pool.wait_ge(x_hi_done, u + 1)
                pool.tensor_tensor(x_lo[:, :, :], x_raw[:, :, :], x_hi[:, :, :].bitcast(F32), ALU.subtract) \
                    .then_inc(x_lo_done, 1)

            def inverse_deviation(u):
                for p in range(PAIRS):
                    pool.wait_ge(var_done, PAIRS * u + p + 1)
                    pool.tensor_tensor(rstd[:, p, :], mean_var[:, p, 1:2], power[:, :], ALU.pow) \
                        .then_inc(rstd_done, 1)

            split_xT(0)
            split_x(0)
            split_xT(1)
            with pool.Fori(1, UNITS - 1) as u:
                split_x(u)
                inverse_deviation(u - 1)
                split_xT(u + 1)
            split_x(UNITS - 1)
            inverse_deviation(UNITS - 2)
            inverse_deviation(UNITS - 1)

        @block.tensor
        def _(pe):
            def scores(s, first):
                pe.wait_ge(qk_copied, HS * (s + 1))
                for p in range(PAIRS):
                    if not first:
                        pe.wait_ge(masked, PAIRS * (s - 1) + p + 1)
                    for hh in range(HS):
                        for b in range(2):
                            t = p * P + b * SEQ
                            last = pe.matmul(ps_s[b * SEQ:(b + 1) * SEQ, p, hh, :], qk[:, hh, 0, t:t + SEQ],
                                             qk[:, hh, 1, t:t + SEQ], start=True, stop=True)
                    last.then_inc(s_filled, 1)

            def turn(s, first):
                for p in range(PAIRS):
                    pe.wait_ge(normed, PAIRS * s + p + 1)
                    if first:
                        pe.wait_ge(fold_lo, B_LOADS * 2)
                    else:
                        pe.wait_ge(mix_lo_done, JOBS * s - 1 + p)
                    for hp in range(HP):
                        last = pe.transpose(ps_mix[:, p, hp * P:(hp + 1) * P], s_sb[:, p, 2 * hp:2 * hp + 2, :],
                                            ident[:, :])
                    last.then_inc(t_filled, 1)

            def mix(s, unit, j):
                p, e, c = j // (2 * KC), j // KC % 2, j % KC
                if j == 0:
                    pe.wait_ge(x_lo_done, unit + 1)
                if j < 2:
                    pe.wait_ge(pT_lo_done, PAIRS * s + j + 1)
                else:
                    if j == JOBS // 2:
                        pe.wait_ge(pT_lo_done, PAIRS * s + 2)
                    pe.wait_ge(mix_lo_done, JOBS * s + j - 1)
                rows = slice(64 * e, 64 * e + 64)
                for b in range(2):
                    cols = slice(c * P, (c + 1) * P)
                    hi, lo = x_hi[rows, 2 * p + b, cols], x_lo[rows, 2 * p + b, cols]
                    for n, (w, v) in enumerate(((hi, pT_hi), (hi, pT_lo), (lo, pT_hi))):
                        last = pe.matmul(ps_mix[:, j % 2, b * 256:(b + 1) * 256], w, v[rows, p, b, :, :],
                                         start=(n == 0), stop=(n == 2))
                last.then_inc(mix_filled, 1)

            def output(s, unit, half, j, first):
                p, e, c = j // (2 * KC), j // KC % 2, j % KC
                pe.wait_ge(mix_lo_done, JOBS * s + j + 1)
                if half == 0 and j % (2 * KC) == 0 and not first:
                    pe.wait_ge(right_added, PAIRS * (unit - 1) + p + 1)
                for hp in range(HP):
                    k = (HS * half + 2 * hp + e) * KC + c
                    start = half == 0 and j % (2 * KC) == 0 and hp == 0
                    stop = half == STEPS - 1 and j % (2 * KC) == 2 * KC - 1 and hp == HP - 1
                    pe.matmul(ps_out[:, p, :, :], mix_hi[:, j % RING, hp, :], wvo[:, k, :, :],
                              start=start, stop=False)
                    last = pe.matmul(ps_out[:, p, 0, :], mix_lo[:, j % RING, hp, :], wvo[:, k, 0, :],
                                     start=False, stop=stop)
                last.then_inc(proj_done, 1)

            def step(unit, half, first, last):
                s = unit * STEPS + half
                scores(s, first and half == 0)
                ahead = not (last and half == STEPS - 1)
                nh = (half + 1) % STEPS

                def next_projection(hh):
                    if ahead:
                        if nh == 0 and hh == 0:
                            pe.wait_ge(xT_lo_done, unit + 2)
                        project(s + 1, nh, hh, False)

                for hh in range(HS - 1):
                    next_projection(hh)
                turn(s, first and half == 0)
                next_projection(HS - 1)
                for j in range(JOBS + 2):
                    if j < JOBS:
                        mix(s, unit, j)
                    if j >= 2:
                        output(s, unit, half, j - 2, first)

            def project(s, half, hh, first):
                if not (first and hh < 2):
                    pe.wait_ge(qk_copied, HS * s + hh - 1)
                h = HS * half + hh
                for i in range(2):
                    dst = ps_qk[:, hh % 2, i, :]
                    n = 0
                    for c in range(KC):
                        hi = wqk_hi[:, i, c, h * P:(h + 1) * P]
                        lo = wqk_lo[:, i, c, h * P:(h + 1) * P]
                        for w, v in ((hi, xT_hi), (hi, xT_lo), (lo, xT_hi)):
                            last = pe.matmul(dst, w, v[:, c, :], start=(n == 0), stop=(n == 3 * KC - 1))
                            n += 1
                last.then_inc(qk_filled, 1)

            pe.wait_ge(consts, 12)
            pe.wait_ge(w_lo, W_LOADS)
            pe.wait_ge(xT_lo_done, 1)
            for hh in range(HS):
                project(0, 0, hh, True)
            for g in range(B_LOADS):
                pe.wait_ge(staged[(W_LOADS + g) % 3], staged_count(W_LOADS + g))
                w = stage[:, (W_LOADS + g) % 3, :].rearrange("p (h w d) -> p h w d", h=2, w=2)
                for hh in range(2):
                    if g >= 1:
                        pe.wait_ge(fold_lo, 2 * g - 1 + hh)
                    for c in range(KC):
                        last = pe.matmul(ps_mix[:, hh, c * DIM:(c + 1) * DIM], w[:, hh, 0, c * P:(c + 1) * P],
                                         w[:, hh, 1, :], start=True, stop=True)
                last.then_inc(fold_filled, 1)
            for half in range(STEPS):
                step(0, half, True, False)
            with pe.Fori(1, UNITS - 1) as u:
                for half in range(STEPS):
                    step(u, half, False, False)
            for half in range(STEPS):
                step(UNITS - 1, half, False, True)

        @block.scalar
        def _(act):
            def copy_qk(s, hh, first):
                act.wait_ge(qk_filled, HS * s + hh + 1)
                if not first and hh == 0:
                    act.wait_ge(s_filled, PAIRS * s)
                nc.scalar.activation(qk[:, hh, :, :], ps_qk[:, hh % 2, :, :], ACT.Copy).then_inc(qk_copied, 1)

            def exponent(s, p):
                act.wait_ge(shifted, PAIRS * s + p + 1)
                nc.scalar.activation(s_sb[:, p, :, :], s_sb[:, p, :, :], ACT.Exp, scale=SCALE).then_inc(exped, 1)

            def probs_hi(s, p, first):
                act.wait_ge(t_filled, PAIRS * s + p + 1)
                if not first and p == 0:
                    act.wait_ge(mix_filled, JOBS * s)
                src = ps_mix[:, p, :].rearrange("k (h b q) -> k b h q", h=HP, b=2)
                nc.scalar.activation(pT_hi[:, p, :, :, :], src, ACT.Copy).then_inc(pT_hi_done, 1)

            def mixed_hi(s, j, first):
                act.wait_ge(mix_filled, JOBS * s + j + 1)
                if not (first and j < RING):
                    act.wait_ge(proj_done, JOBS * s + j - RING + 1)
                src = ps_mix[:, j % 2, :].rearrange("d (b h q) -> d h b q", b=2, h=HP)
                nc.scalar.activation(mix_hi[:, j % RING, :, :].rearrange("d h (b q) -> d h b q", b=2), src,
                                     ACT.Copy).then_inc(mix_hi_done, 1)

            def xT_split(u, first=False):
                act.wait_ge(xT_in, 16 * (u + 1))
                if not first:
                    act.wait_ge(qk_filled, HEADS * u)
                nc.scalar.activation(xT_hi[:, :, :], xT_raw[:, :, :], ACT.Copy).then_inc(xT_hi_done, 1)

            def x_split(u, first=False):
                act.wait_ge(xd_in, 32 * (u + 1))
                if not first:
                    act.wait_ge(mix_filled, STEPS * JOBS * u)
                nc.scalar.activation(x_hi[:, :, :], x_raw[:, :, :], ACT.Copy).then_inc(x_hi_done, 1)

            def step(u, half, first=False, last=False):
                s = u * STEPS + half
                first, ahead = first and half == 0, not (last and half == STEPS - 1)

                def nxt(*hs):
                    for hh in hs:
                        if ahead:
                            copy_qk(s + 1, hh, False)
                nxt(0, 1)
                if half == 0 and not first:
                    x_split(u)
                exponent(s, 0)
                nxt(2, 3, 4)
                exponent(s, 1)
                nxt(5, 6)
                probs_hi(s, 0, first)
                probs_hi(s, 1, first)
                nxt(7)
                for j in range(JOBS):
                    mixed_hi(s, j, first)
                if half == 0 and not last:
                    xT_split(u + 1)

            xT_split(0, True)
            for n in range(W_LOADS):
                act.wait_ge(staged[n % 3], staged_count(n))
                c, i, half = n // 4, n // 2 % 2, n % 2
                nc.scalar.activation(wqk_hi[:, i, c, half * STAGE:(half + 1) * STAGE], stage[:, n % 3, :],
                                     ACT.Copy).then_inc(w_hi, 1)
            for hh in range(HS):
                copy_qk(0, hh, True)
            for h in range(HEADS):
                act.wait_ge(fold_filled, h // 2 + 1)
                src = ps_mix[:, h % 2, :].rearrange("p (c d) -> p c d", c=KC)
                nc.scalar.activation(wvo[:, h * KC:(h + 1) * KC, 0, :], src, ACT.Copy).then_inc(fold_hi, 1)
            x_split(0, True)
            for half in range(STEPS):
                step(0, half, first=True)
            with act.Fori(1, UNITS - 1) as u:
                for half in range(STEPS):
                    step(u, half)
            for half in range(STEPS):
                step(UNITS - 1, half, last=True)

        @block.vector
        def _(dve):
            mask_b = mask[:, :].unsqueeze(1).to_broadcast([P, HS, SEQ])

            def softmax_start(s, p):
                n = PAIRS * s + p + 1
                dve.wait_ge(s_filled, n)
                if not (isinstance(s, int) and s == 0):
                    dve.wait_ge(t_filled, n - PAIRS)
                dve.tensor_tensor(s_sb[:, p, :, :], ps_s[:, p, :, :], mask_b, ALU.add).then_inc(masked, 1)
                dve.wait_ge(masked, n)
                dve.tensor_reduce(row_max[:, p, :], s_sb[:, p, :, :], AX.X, ALU.max).then_inc(maxed, 1)
                dve.wait_ge(maxed, n)
                dve.tensor_tensor(s_sb[:, p, :, :], s_sb[:, p, :, :],
                                  row_max[:, p, :].unsqueeze(2).to_broadcast([P, HS, SEQ]),
                                  ALU.subtract).then_inc(shifted, 1)

            def softmax_end(s, p):
                n = PAIRS * s + p + 1
                dve.wait_ge(exped, n)
                dve.tensor_reduce(row_sum[:, p, :], s_sb[:, p, :, :], AX.X, ALU.add).then_inc(summed, 1)
                dve.wait_ge(summed, n)
                dve.reciprocal(inv_sum[:, p, :], row_sum[:, p, :]).then_inc(inverted, 1)
                dve.wait_ge(inverted, n)
                dve.tensor_tensor(s_sb[:, p, :, :], s_sb[:, p, :, :],
                                  inv_sum[:, p, :].unsqueeze(2).to_broadcast([P, HS, SEQ]),
                                  ALU.mult).then_inc(normed, 1)

            def probs_lo(s, p):
                dve.wait_ge(pT_hi_done, PAIRS * s + p + 1)
                src = ps_mix[:, p, :].rearrange("k (h b q) -> k b h q", h=HP, b=2)
                dve.tensor_tensor(pT_lo[:, p, :, :, :], src, pT_hi[:, p, :, :, :].bitcast(F32), ALU.subtract) \
                    .then_inc(pT_lo_done, 1)

            def mixed_lo(s, j):
                dve.wait_ge(mix_hi_done, JOBS * s + j + 1)
                src = ps_mix[:, j % 2, :].rearrange("d (b h q) -> d h b q", b=2, h=HP)
                hi = mix_hi[:, j % RING, :, :].rearrange("d h (b q) -> d h b q", b=2).bitcast(F32)
                lo = mix_lo[:, j % RING, :, :].rearrange("d h (b q) -> d h b q", b=2)
                dve.tensor_tensor(lo, src, hi, ALU.subtract).then_inc(mix_lo_done, 1)

            def residual(unit, p, first):
                n = PAIRS * unit + p + 1
                if p == 0:
                    dve.wait_ge(xr_in, 16 * (unit + 1))
                    dve.wait_ge(proj_done, STEPS * JOBS * (unit + 1))
                    if not first:
                        dve.wait_ge(stored, 16 * unit)
                dve.tensor_tensor(y[:, p, :], ps_out[:, p, 0, :], x_res[:, p, :], ALU.add).then_inc(left_added, 1)
                dve.wait_ge(left_added, n)
                dve.tensor_tensor(y[:, p, :], ps_out[:, p, 1, :], y[:, p, :], ALU.add).then_inc(right_added, 1)
                dve.wait_ge(right_added, n)
                dve.bn_stats(stats[:, p, :], y[:, p, :]).then_inc(stats_done, 1)
                dve.wait_ge(stats_done, n)
                dve.sem_inc(stats_seen, 1)
                dve.bn_aggr(mean_var[:, p, :], stats[:, p, :]).then_inc(moments_done, 1)
                dve.wait_ge(moments_done, n)
                dve.tensor_scalar(mean_var[:, p, 1:2], mean_var[:, p, 1:2], EPS, None, ALU.add).then_inc(var_done, 1)

            def normalise(unit, p):
                dve.wait_ge(rstd_done, PAIRS * unit + p + 1)
                dve.tensor_scalar(y[:, p, :], y[:, p, :], mean_var[:, p, 0:1], rstd[:, p, 0:1],
                                  ALU.subtract, ALU.mult).then_inc(y_done, 1)

            def step(unit, half, first):
                s = unit * STEPS + half
                softmax_start(s, 0)
                softmax_start(s, 1)
                if half == 0 and not first:
                    residual(unit - 1, 0, first=isinstance(unit, int) and unit == 1)
                softmax_end(s, 0)
                softmax_end(s, 1)
                if half == 0 and not first:
                    residual(unit - 1, 1, first=False)
                    normalise(unit - 1, 0)
                    normalise(unit - 1, 1)
                probs_lo(s, 0)
                probs_lo(s, 1)
                for j in range(JOBS):
                    mixed_lo(s, j)

            for n in range(W_LOADS):
                dve.wait_ge(w_hi, n + 1)
                c, i, half = n // 4, n // 2 % 2, n % 2
                cols = slice(half * STAGE, (half + 1) * STAGE)
                dve.tensor_tensor(wqk_lo[:, i, c, cols], stage[:, n % 3, :], wqk_hi[:, i, c, cols].bitcast(F32),
                                  ALU.subtract).then_inc(w_lo, 1)
            for h in range(HEADS):
                dve.wait_ge(fold_hi, h + 1)
                src = ps_mix[:, h % 2, :].rearrange("p (c d) -> p c d", c=KC)
                dve.tensor_tensor(wvo[:, h * KC:(h + 1) * KC, 1, :], src,
                                  wvo[:, h * KC:(h + 1) * KC, 0, :].bitcast(F32), ALU.subtract).then_inc(fold_lo, 1)
            dve.wait_ge(consts, 12)
            for half in range(STEPS):
                step(0, half, True)
            with dve.Fori(1, UNITS) as u:
                for half in range(STEPS):
                    step(u, half, False)
            for p in range(PAIRS):
                residual(UNITS - 1, p, first=False)
            for p in range(PAIRS):
                normalise(UNITS - 1, p)


def latent_attention(nc, x, kv, rope, Wq, w_kc_qT, W_qrT, W_krT, w_kc_kv, WoT, out):
    LATENT, Q_RANK = 64, 192
    QR = Q_RANK - P
    HALL = HEADS // 2

    with ExitStack() as ctx:
        def sb(name, shape, dt=F32):
            return ctx.enter_context(nc.sbuf_tensor("l_" + name, shape, dt))

        def sem(name):
            return ctx.enter_context(nc.semaphore("l_" + name))

        wq = sb("wq", [P, HEADS, DIM])
        kcq_a = sb("kcq_a", [P, HEADS, P])
        kcq_b = sb("kcq_b", [QR, HEADS, P])
        qrT = sb("qrT", [64, HEADS, Q_RANK])
        krT = sb("krT", [64, HEADS, LATENT])
        kckv = sb("kckv", [P, HEADS, LATENT])
        woT = sb("woT", [P, HEADS, DIM])
        r1_a = sb("r1_a", [P, HEADS, LATENT])
        r1_b = sb("r1_b", [QR, HEADS, LATENT])
        r2 = sb("r2", [P, HEADS, LATENT])
        wm_hi = sb("wm_hi", [P, KC, HALL, P], F32R)
        wm_lo = sb("wm_lo", [P, KC, HALL, P], F32R)
        wn = sb("wn", [P, HALL, 2, DIM], F32R)
        ident = sb("ident", [P, P])
        power = sb("power", [P, 1])
        tables = sb("tables", [P, 2, LATENT])
        x_nat = sb("x_nat", [P, PAIRS, DIM])
        x_res = sb("x_res", [P, PAIRS, DIM])
        xT_hi = sb("xT_hi", [P, PAIRS, KC, P], F32R)
        xT_lo = sb("xT_lo", [P, PAIRS, KC, P], F32R)
        kv_in = sb("kv_in", [P, UB, LATENT])
        kv_cos = sb("kv_cos", [P, UB, LATENT])
        kv_sin = sb("kv_sin", [P, UB, LATENT])
        kv2 = sb("kv2", [P, UB, P])
        kv2_hi = sb("kv2_hi", [P, UB, P], F32R)
        kv2_lo = sb("kv2_lo", [P, UB, P], F32R)
        kv2T = sb("kv2T", [P, UB, P])
        qm = sb("qm", [P, HP, UNIT])
        s_sb = sb("s_sb", [P, STEPS, PAIRS, HS, SEQ])
        row_max = sb("row_max", [P, STEPS, PAIRS, HS])
        row_sum = sb("row_sum", [P, STEPS, PAIRS, HS])
        inv_sum = sb("inv_sum", [P, STEPS, PAIRS, HS])
        pT_hi = sb("pT_hi", [P, PAIRS, 2, HP, SEQ], F32R)
        pT_lo = sb("pT_lo", [P, PAIRS, 2, HP, SEQ], F32R)
        mix_hi = sb("mix_hi", [P, PAIRS, HP, P], F32R)
        mix_lo = sb("mix_lo", [P, PAIRS, HP, P], F32R)
        y = sb("y", [P, PAIRS, DIM])
        stats = sb("stats", [P, PAIRS, 6])
        mean_var = sb("mean_var", [P, PAIRS, 2])
        rstd = sb("rstd", [P, PAIRS, 1])

        banks = ctx.enter_context(nc.psum_tensor("l_banks", [P, 8, 512], F32))
        ps_s = banks[:, 0:2, :].rearrange("p n (h k) -> p n h k", k=SEQ)
        ps_front = banks[:, 2:4, :]
        ps_mix = banks[:, 4:6, :]
        ps_out = banks[:, 6:8, :].rearrange("p n (w d) -> p n w d", w=2)

        w_in = sem("w_in")
        x_in = sem("x_in")
        kv_in_done = sem("kv_in_done")
        xr_in = sem("xr_in")
        stored = sem("stored")
        r1_filled = sem("r1_filled")
        r1_copied = sem("r1_copied")
        r2_filled = sem("r2_filled")
        r2_copied = sem("r2_copied")
        wm_filled = sem("wm_filled")
        wm_hi_done = sem("wm_hi_done")
        wm_lo_done = sem("wm_lo_done")
        wn_filled = sem("wn_filled")
        wn_hi_done = sem("wn_hi_done")
        wn_lo_done = sem("wn_lo_done")
        consts = sem("consts")
        xT_filled = sem("xT_filled")
        xT_hi_done = sem("xT_hi_done")
        xT_lo_done = sem("xT_lo_done")
        cos_done = sem("cos_done")
        sin_done = sem("sin_done")
        rotated = sem("rotated")
        kvT_filled = sem("kvT_filled")
        kvT_copied = sem("kvT_copied")
        kv_hi_done = sem("kv_hi_done")
        kv_lo_done = sem("kv_lo_done")
        qm_filled = sem("qm_filled")
        qm_copied = sem("qm_copied")
        s_filled = sem("s_filled")
        maxed = sem("maxed")
        shifted = sem("shifted")
        exped = sem("exped")
        summed = sem("summed")
        inverted = sem("inverted")
        normed = sem("normed")
        t_filled = sem("t_filled")
        pT_hi_done = sem("pT_hi_done")
        pT_lo_done = sem("pT_lo_done")
        mix_filled = sem("mix_filled")
        mix_hi_done = sem("mix_hi_done")
        mix_lo_done = sem("mix_lo_done")
        proj_done = sem("proj_done")
        left_added = sem("left_added")
        right_added = sem("right_added")
        stats_done = sem("stats_done")
        stats_seen = sem("stats_seen")
        moments_done = sem("moments_done")
        var_done = sem("var_done")
        rstd_done = sem("rstd_done")
        y_done = sem("y_done")

        block = ctx.enter_context(nc.Block())

        x_pairs = x.rearrange("(n p) d -> p n d", p=P)
        kv_batches = kv.rearrange("b t d -> t b d")
        out_pairs = out.rearrange("(n p) d -> p n d", p=P)
        W_DMAS = 9

        @block.sync
        def _(sp):
            def load_x(u, first=False):
                if not first:
                    sp.wait_ge(xT_filled, u)
                sp.dma_start(x_nat[:, :, :], x_pairs[:, bass.ds(u * PAIRS, PAIRS), :]).then_inc(x_in, 16)

            def load_kv(u, first=False):
                if not first:
                    sp.wait_ge(cos_done, u)
                    sp.wait_ge(sin_done, u)
                for e in range(2):
                    sp.dma_start(kv_in[64 * e:64 * e + 64, :, :], kv_batches[:, bass.ds(u * UB, UB), :]) \
                        .then_inc(kv_in_done, 16)

            def load_xres(u, first=False):
                if not first:
                    sp.wait_ge(left_added, PAIRS * u)
                sp.dma_start(x_res[:, :, :], x_pairs[:, bass.ds(u * PAIRS, PAIRS), :]).then_inc(xr_in, 16)

            def store(u):
                sp.wait_ge(y_done, PAIRS * (u + 1))
                sp.dma_start(out_pairs[:, bass.ds(u * PAIRS, PAIRS), :], y[:, :, :]).then_inc(stored, 16)

            sp.dma_start(qrT[:, :, :], W_qrT.rearrange("h r q -> r h q")).then_inc(w_in, 16)
            sp.dma_start(krT[:, :, :], W_krT.rearrange("h r d -> r h d")).then_inc(w_in, 16)
            sp.dma_start(kcq_a[:, :, :], w_kc_qT[:, 0:P, :].rearrange("h q k -> q h k")).then_inc(w_in, 16)
            sp.dma_start(kcq_b[:, :, :], w_kc_qT[:, P:Q_RANK, :].rearrange("h q k -> q h k")).then_inc(w_in, 16)
            sp.dma_start(wq[:, :, :], Wq.rearrange("(h k) d -> k h d", k=P)).then_inc(w_in, 16)
            sp.dma_start(kckv[:, :, :], w_kc_kv.rearrange("h k d -> k h d")).then_inc(w_in, 16)
            sp.dma_start(woT[:, :, :], WoT.rearrange("(h k) d -> k h d", k=P)).then_inc(w_in, 16)
            for e in range(2):
                sp.dma_start(tables[64 * e:64 * e + 64, :, :], rope.rearrange("w t d -> t w d")).then_inc(w_in, 16)
            load_x(0, True)
            load_kv(0, True)
            load_xres(0, True)
            load_x(1)
            load_kv(1)
            with sp.Fori(1, UNITS - 1) as u:
                load_x(u + 1)
                load_kv(u + 1)
                store(u - 1)
                load_xres(u)
            store(UNITS - 2)
            load_xres(UNITS - 1)
            store(UNITS - 1)
            sp.wait_ge(stored, 16 * UNITS)

        @block.gpsimd
        def _(pool):
            def rotate(u, first=False):
                pool.wait_ge(kv_in_done, 32 * (u + 1))
                pool.tensor_tensor(kv_cos[:, :, :], kv_in[:, :, :],
                                   tables[:, 0, :].unsqueeze(1).to_broadcast([P, UB, LATENT]), ALU.mult) \
                    .then_inc(cos_done, 1)
                swapped = kv_in[:, :, :].rearrange("p b (w d) -> p b w d", w=2)
                sines = tables[:, 1, :].rearrange("p (w d) -> p w d", w=2)
                turned = kv_sin[:, :, :].rearrange("p b (w d) -> p b w d", w=2)
                for w in range(2):
                    last = pool.tensor_tensor(turned[:, :, w, :], swapped[:, :, 1 - w, :],
                                              sines[:, w, :].unsqueeze(1).to_broadcast([P, UB, LATENT // 2]), ALU.mult)
                last.then_inc(sin_done, 1)
                pool.wait_ge(cos_done, u + 1)
                pool.wait_ge(sin_done, u + 1)
                if not first:
                    pool.wait_ge(kvT_filled, u)
                    pool.wait_ge(kv_lo_done, u)
                for e in range(2):
                    rows, cols = slice(64 * e, 64 * e + 64), slice(64 * e, 64 * e + 64)
                    pool.tensor_tensor(kv2[rows, :, cols], kv_cos[rows, :, :], kv_sin[rows, :, :], ALU.add) \
                        .then_inc(rotated, 1)
                    pool.wait_ge(rotated, 2 * u + e + 1)

            def split_kv(u):
                pool.wait_ge(kv_hi_done, u + 1)
                pool.tensor_tensor(kv2_lo[:, :, :], kv2[:, :, :], kv2_hi[:, :, :].bitcast(F32), ALU.subtract) \
                    .then_inc(kv_lo_done, 1)

            def normalise_probs(s, half):
                for p in range(PAIRS):
                    pool.wait_ge(inverted, PAIRS * s + p + 1)
                    pool.tensor_tensor(s_sb[:, half, p, :, :], s_sb[:, half, p, :, :],
                                       inv_sum[:, half, p, :].unsqueeze(2).to_broadcast([P, HS, SEQ]), ALU.mult) \
                        .then_inc(normed, 1)

            def inverse_deviation(u):
                for p in range(PAIRS):
                    pool.wait_ge(var_done, PAIRS * u + p + 1)
                    pool.tensor_tensor(rstd[:, p, :], mean_var[:, p, 1:2], power[:, :], ALU.pow).then_inc(rstd_done, 1)

            pool.memset(ident[:, :], 0.0).then_inc(consts, 1)
            pool.memset(power[:, :], -0.5).then_inc(consts, 1)
            pool.memset(kv2[:, :, :], 0.0).then_inc(consts, 1)
            pool.wait_ge(consts, 3)
            pool.affine_select(out=ident[:, :], in_=ident[:, :], compare_op=ALU.not_equal, fill=1.0,
                               base=0, pattern=[[-1, P]], channel_multiplier=1).then_inc(consts, 1)
            pool.wait_ge(w_in, 16 * W_DMAS)
            rotate(0, True)
            split_kv(0)
            rotate(1)
            normalise_probs(0, 0)
            normalise_probs(1, 1)
            with pool.Fori(1, UNITS - 1) as u:
                normalise_probs(u * STEPS, 0)
                split_kv(u)
                rotate(u + 1)
                inverse_deviation(u - 1)
                normalise_probs(u * STEPS + 1, 1)
            normalise_probs((UNITS - 1) * STEPS, 0)
            split_kv(UNITS - 1)
            inverse_deviation(UNITS - 2)
            normalise_probs((UNITS - 1) * STEPS + 1, 1)
            inverse_deviation(UNITS - 1)

        @block.tensor
        def _(pe):
            def turn_inputs(u, first=False):
                pe.wait_ge(x_in, 16 * (u + 1))
                if not first:
                    pe.wait_ge(qm_copied, 4 * u - 1)
                for p in range(PAIRS):
                    for c in range(KC):
                        k = (p * KC + c) * P
                        last = pe.transpose(ps_front[:, 0, k:k + P], x_nat[:, p, c * P:(c + 1) * P], ident[:, :])
                last.then_inc(xT_filled, 1)
                pe.wait_ge(rotated, 2 * (u + 1))
                if not first:
                    pe.wait_ge(qm_copied, 4 * u)
                for b in range(UB):
                    last = pe.transpose(ps_front[:, 1, b * P:(b + 1) * P], kv2[:, b, :], ident[:, :])
                last.then_inc(kvT_filled, 1)

            def project(s, unit, half):
                for j in range(2):
                    if half == 0 and j == 0:
                        pe.wait_ge(xT_lo_done, unit + 1)
                    elif half == 0:
                        pe.wait_ge(kvT_copied, unit + 1)
                    else:
                        pe.wait_ge(qm_copied, 2 * s - 1 + j)
                    for i in range(2):
                        dst = ps_front[:, j, i * UNIT:(i + 1) * UNIT]
                        n = 0
                        for c in range(KC):
                            hi = wm_hi[:, c, half * HP + 2 * j + i, :]
                            lo = wm_lo[:, c, half * HP + 2 * j + i, :]
                            for w, v in ((hi, xT_hi), (hi, xT_lo), (lo, xT_hi)):
                                last = pe.matmul(dst, w, v[:, :, c, :], start=(n == 0), stop=(n == 3 * KC - 1))
                                n += 1
                    last.then_inc(qm_filled, 1)

            def scores(s, first=False):
                pe.wait_ge(qm_copied, 2 * (s + 1))
                for p in range(PAIRS):
                    if not first:
                        pe.wait_ge(shifted, PAIRS * (s - 1) + p + 1)
                    for hp in range(HP):
                        for b in range(2):
                            t = p * P + b * SEQ
                            last = pe.matmul(ps_s[b * SEQ:(b + 1) * SEQ, p, 2 * hp:2 * hp + 2, :], qm[:, hp, t:t + SEQ],
                                             kv2T[:, 2 * p + b, :], start=True, stop=True)
                    last.then_inc(s_filled, 1)

            def turn(s, half, first=False):
                for p in range(PAIRS):
                    pe.wait_ge(normed, PAIRS * s + p + 1)
                    if not first:
                        pe.wait_ge(mix_lo_done, PAIRS * (s - 1) + p + 1)
                    for hp in range(HP):
                        last = pe.transpose(ps_mix[:, p, hp * P:(hp + 1) * P],
                                            s_sb[:, half, p, 2 * hp:2 * hp + 2, :], ident[:, :])
                    last.then_inc(t_filled, 1)

            def mix(s, unit, half):
                if half == 0:
                    pe.wait_ge(kv_lo_done, unit + 1)
                for p in range(PAIRS):
                    pe.wait_ge(pT_lo_done, PAIRS * s + p + 1)
                    for b in range(2):
                        hi, lo = kv2_hi[:, 2 * p + b, :], kv2_lo[:, 2 * p + b, :]
                        for n, (w, v) in enumerate(((hi, pT_hi), (hi, pT_lo), (lo, pT_hi))):
                            last = pe.matmul(ps_mix[:, p, b * 256:(b + 1) * 256], w, v[:, p, b, :, :],
                                             start=(n == 0), stop=(n == 2))
                    last.then_inc(mix_filled, 1)

            def output(s, unit, half, first=False):
                for p in range(PAIRS):
                    pe.wait_ge(mix_lo_done, PAIRS * s + p + 1)
                    if half == 0 and not first:
                        pe.wait_ge(right_added, PAIRS * (unit - 1) + p + 1)
                    for hp in range(HP):
                        k = half * HP + hp
                        pe.matmul(ps_out[:, p, :, :], mix_hi[:, p, hp, :], wn[:, k, :, :], start=(k == 0), stop=False)
                        last = pe.matmul(ps_out[:, p, 0, :], mix_lo[:, p, hp, :], wn[:, k, 0, :],
                                         start=False, stop=(k == HALL - 1))
                    last.then_inc(proj_done, 1)

            def back(s, unit, half, first, project_ahead=None):
                turn(s, half, first)
                if project_ahead:
                    project_ahead()
                mix(s, unit, half)
                output(s, unit, half, first)

            pe.wait_ge(w_in, 16 * W_DMAS)
            pe.wait_ge(consts, 4)
            for h in range(HEADS):
                at = slice(h % 8 * LATENT, (h % 8 + 1) * LATENT)
                pe.matmul(banks[:, h // 8, at], qrT[:, h, 0:P], krT[:, h, :], start=True, stop=True)
                last = pe.matmul(banks[0:QR, 2 + h // 8, at], qrT[:, h, P:Q_RANK], krT[:, h, :], start=True, stop=True)
            last.then_inc(r1_filled, 1)
            pe.wait_ge(r1_copied, 2)
            for h in range(HEADS):
                at = slice(h % 8 * LATENT, (h % 8 + 1) * LATENT)
                pe.matmul(banks[:, 4 + h // 8, at], kcq_a[:, h, :], r1_a[:, h, :], start=True, stop=False)
                last = pe.matmul(banks[:, 4 + h // 8, at], kcq_b[:, h, :], r1_b[:, h, :], start=False, stop=True)
            last.then_inc(r2_filled, 1)
            pe.wait_ge(r2_copied, 1)
            for c in range(KC):
                for h in range(HEADS):
                    at = slice(h % 8 * LATENT, (h % 8 + 1) * LATENT)
                    last = pe.matmul(banks[:, 2 * c + h // 8, at], wq[:, h, c * P:(c + 1) * P], r2[:, h, :],
                                     start=True, stop=True)
            last.then_inc(wm_filled, 1)
            for h in range(HEADS):
                rows = slice(h % 2 * 64, h % 2 * 64 + 64)
                last = pe.matmul(banks[rows, 4 + h // 4, h // 2 % 2 * DIM:(h // 2 % 2 + 1) * DIM], kckv[:, h, :],
                                 woT[:, h, :], start=True, stop=True)
            last.then_inc(wn_filled, 1)
            pe.wait_ge(wm_lo_done, 1)
            pe.wait_ge(wn_lo_done, 1)

            turn_inputs(0, True)
            project(0, 0, 0)
            scores(0, True)
            project(1, 0, 1)
            scores(1)
            turn_inputs(1)
            back(0, 0, 0, True, lambda: project(2, 1, 0))
            with pe.Fori(1, UNITS - 1) as u:
                s = u * STEPS
                scores(s)
                back(s - 1, u - 1, 1, False, lambda: project(s + 1, u, 1))
                scores(s + 1)
                turn_inputs(u + 1)
                back(s, u, 0, False, lambda: project(s + 2, u + 1, 0))
            s = (UNITS - 1) * STEPS
            scores(s)
            back(s - 1, UNITS - 2, 1, False, lambda: project(s + 1, UNITS - 1, 1))
            scores(s + 1)
            back(s, UNITS - 1, 0, False)
            back(s + 1, UNITS - 1, 1, False)

        @block.scalar
        def _(act):
            def inputs_hi(u):
                act.wait_ge(xT_filled, u + 1)
                nc.scalar.activation(xT_hi[:, :, :, :], ps_front[:, 0, :], ACT.Copy).then_inc(xT_hi_done, 1)
                act.wait_ge(kvT_filled, u + 1)
                nc.scalar.activation(kv2T[:, :, :], ps_front[:, 1, :], ACT.Copy).then_inc(kvT_copied, 1)

            def copy_qm(s):
                for j in range(2):
                    act.wait_ge(qm_filled, 2 * s + j + 1)
                    nc.scalar.activation(qm[:, 2 * j:2 * j + 2, :], ps_front[:, j, :], ACT.Copy).then_inc(qm_copied, 1)

            def exponents(s, half):
                for p in range(PAIRS):
                    act.wait_ge(shifted, PAIRS * s + p + 1)
                    nc.scalar.activation(s_sb[:, half, p, :, :], s_sb[:, half, p, :, :], ACT.Exp).then_inc(exped, 1)

            def probs_hi(s):
                for p in range(PAIRS):
                    act.wait_ge(t_filled, PAIRS * s + p + 1)
                    src = ps_mix[:, p, :].rearrange("k (h b q) -> k b h q", h=HP, b=2)
                    nc.scalar.activation(pT_hi[:, p, :, :, :], src, ACT.Copy).then_inc(pT_hi_done, 1)

            def mixed_hi(s, first=False):
                for p in range(PAIRS):
                    act.wait_ge(mix_filled, PAIRS * s + p + 1)
                    if not first:
                        act.wait_ge(proj_done, PAIRS * (s - 1) + p + 1)
                    src = ps_mix[:, p, :].rearrange("d (b h q) -> d h b q", b=2, h=HP)
                    nc.scalar.activation(mix_hi[:, p, :, :].rearrange("d h (b q) -> d h b q", b=2), src, ACT.Copy) \
                        .then_inc(mix_hi_done, 1)

            def kv_split(u, first=False):
                act.wait_ge(rotated, 2 * (u + 1))
                if not first:
                    act.wait_ge(mix_filled, STEPS * PAIRS * u)
                nc.scalar.activation(kv2_hi[:, :, :], kv2[:, :, :], ACT.Copy).then_inc(kv_hi_done, 1)

            act.wait_ge(r1_filled, 1)
            nc.scalar.activation(r1_a[:, :, :], banks[:, 0:2, :], ACT.Copy).then_inc(r1_copied, 1)
            nc.scalar.activation(r1_b[:, :, :], banks[0:QR, 2:4, :], ACT.Copy).then_inc(r1_copied, 1)
            act.wait_ge(r2_filled, 1)
            nc.scalar.activation(r2[:, :, :], banks[:, 4:6, :], ACT.Copy).then_inc(r2_copied, 1)
            act.wait_ge(wm_filled, 1)
            nc.scalar.activation(wm_hi[:, :, :, :], banks[:, 0:4, :], ACT.Copy).then_inc(wm_hi_done, 1)
            act.wait_ge(wn_filled, 1)
            nc.scalar.activation(wn[:, :, 0, :], banks[:, 4:8, :].rearrange("p n (k d) -> p (n k) d", k=2),
                                 ACT.Copy).then_inc(wn_hi_done, 1)

            kv_split(0, True)
            inputs_hi(0)
            copy_qm(0)
            copy_qm(1)
            exponents(0, 0)
            inputs_hi(1)
            exponents(1, 1)
            probs_hi(0)
            copy_qm(2)
            mixed_hi(0, True)
            with act.Fori(1, UNITS - 1) as u:
                s = u * STEPS
                exponents(s, 0)
                probs_hi(s - 1)
                copy_qm(s + 1)
                mixed_hi(s - 1)
                kv_split(u)
                inputs_hi(u + 1)
                exponents(s + 1, 1)
                probs_hi(s)
                copy_qm(s + 2)
                mixed_hi(s)
            s = (UNITS - 1) * STEPS
            exponents(s, 0)
            probs_hi(s - 1)
            copy_qm(s + 1)
            mixed_hi(s - 1)
            kv_split(UNITS - 1)
            exponents(s + 1, 1)
            for k in (s, s + 1):
                probs_hi(k)
                mixed_hi(k)

        @block.vector
        def _(dve):
            def inputs_lo(u):
                dve.wait_ge(xT_hi_done, u + 1)
                dve.tensor_tensor(xT_lo[:, :, :, :], ps_front[:, 0, :].rearrange("p (n c t) -> p n c t", n=PAIRS, c=KC),
                                  xT_hi[:, :, :, :].bitcast(F32), ALU.subtract).then_inc(xT_lo_done, 1)

            def softmax_start(s, half):
                for p in range(PAIRS):
                    n = PAIRS * s + p + 1
                    dve.wait_ge(s_filled, n)
                    dve.tensor_reduce(row_max[:, half, p, :], ps_s[:, p, :, :], AX.X, ALU.max).then_inc(maxed, 1)
                    dve.wait_ge(maxed, n)
                    if not (isinstance(s, int) and s < STEPS):
                        dve.wait_ge(t_filled, n - STEPS * PAIRS)
                    dve.tensor_tensor(s_sb[:, half, p, :, :], ps_s[:, p, :, :],
                                      row_max[:, half, p, :].unsqueeze(2).to_broadcast([P, HS, SEQ]),
                                      ALU.subtract).then_inc(shifted, 1)

            def softmax_sum(s, half):
                for p in range(PAIRS):
                    n = PAIRS * s + p + 1
                    dve.wait_ge(exped, n)
                    dve.tensor_reduce(row_sum[:, half, p, :], s_sb[:, half, p, :, :], AX.X, ALU.add) \
                        .then_inc(summed, 1)
                    dve.wait_ge(summed, n)
                    dve.reciprocal(inv_sum[:, half, p, :], row_sum[:, half, p, :]).then_inc(inverted, 1)

            def probs_lo(s):
                for p in range(PAIRS):
                    dve.wait_ge(pT_hi_done, PAIRS * s + p + 1)
                    src = ps_mix[:, p, :].rearrange("k (h b q) -> k b h q", h=HP, b=2)
                    dve.tensor_tensor(pT_lo[:, p, :, :, :], src, pT_hi[:, p, :, :, :].bitcast(F32), ALU.subtract) \
                        .then_inc(pT_lo_done, 1)

            def mixed_lo(s):
                for p in range(PAIRS):
                    dve.wait_ge(mix_hi_done, PAIRS * s + p + 1)
                    src = ps_mix[:, p, :].rearrange("d (b h q) -> d h b q", b=2, h=HP)
                    hi = mix_hi[:, p, :, :].rearrange("d h (b q) -> d h b q", b=2).bitcast(F32)
                    dve.tensor_tensor(mix_lo[:, p, :, :].rearrange("d h (b q) -> d h b q", b=2), src, hi,
                                      ALU.subtract).then_inc(mix_lo_done, 1)

            def residual(unit, first=False):
                dve.wait_ge(xr_in, 16 * (unit + 1))
                dve.wait_ge(proj_done, STEPS * PAIRS * (unit + 1))
                if not first:
                    dve.wait_ge(stored, 16 * unit)
                for p in range(PAIRS):
                    dve.tensor_tensor(y[:, p, :], ps_out[:, p, 0, :], x_res[:, p, :], ALU.add).then_inc(left_added, 1)
                for p in range(PAIRS):
                    dve.wait_ge(left_added, PAIRS * unit + p + 1)
                    dve.tensor_tensor(y[:, p, :], ps_out[:, p, 1, :], y[:, p, :], ALU.add).then_inc(right_added, 1)
                for p in range(PAIRS):
                    n = PAIRS * unit + p + 1
                    dve.wait_ge(right_added, n)
                    dve.bn_stats(stats[:, p, :], y[:, p, :]).then_inc(stats_done, 1)
                    dve.wait_ge(stats_done, n)
                    dve.sem_inc(stats_seen, 1)
                    dve.bn_aggr(mean_var[:, p, :], stats[:, p, :]).then_inc(moments_done, 1)
                    dve.wait_ge(moments_done, n)
                    dve.tensor_scalar(mean_var[:, p, 1:2], mean_var[:, p, 1:2], EPS, None, ALU.add) \
                        .then_inc(var_done, 1)

            def normalise(unit):
                for p in range(PAIRS):
                    dve.wait_ge(rstd_done, PAIRS * unit + p + 1)
                    dve.tensor_scalar(y[:, p, :], y[:, p, :], mean_var[:, p, 0:1], rstd[:, p, 0:1],
                                      ALU.subtract, ALU.mult).then_inc(y_done, 1)

            dve.wait_ge(wm_hi_done, 1)
            dve.tensor_tensor(wm_lo[:, :, :, :].rearrange("p c n k -> p (c n k)"),
                              banks[:, 0:4, :].rearrange("p n k -> p (n k)"),
                              wm_hi[:, :, :, :].rearrange("p c n k -> p (c n k)").bitcast(F32), ALU.subtract) \
                .then_inc(wm_lo_done, 1)
            dve.wait_ge(wn_hi_done, 1)
            dve.tensor_tensor(wn[:, :, 1, :], banks[:, 4:8, :].rearrange("p n (k d) -> p (n k) d", k=2),
                              wn[:, :, 0, :].bitcast(F32), ALU.subtract).then_inc(wn_lo_done, 1)

            inputs_lo(0)
            softmax_start(0, 0)
            softmax_sum(0, 0)
            inputs_lo(1)
            softmax_start(1, 1)
            probs_lo(0)
            softmax_sum(1, 1)
            mixed_lo(0)

            def unit_body(u, ahead=True, first=False):
                s = u * STEPS
                softmax_start(s, 0)
                probs_lo(s - 1)
                softmax_sum(s, 0)
                mixed_lo(s - 1)
                if ahead:
                    inputs_lo(u + 1)
                softmax_start(s + 1, 1)
                residual(u - 1, first)
                probs_lo(s)
                softmax_sum(s + 1, 1)
                normalise(u - 1)
                mixed_lo(s)

            unit_body(1, first=True)
            with dve.Fori(2, UNITS - 1) as u:
                unit_body(u)
            unit_body(UNITS - 1, ahead=False)
            probs_lo(UNITS * STEPS - 1)
            mixed_lo(UNITS * STEPS - 1)
            residual(UNITS - 1)
            normalise(UNITS - 1)


def mixture(nc, x, gateT, gate_b, W1T, W3T, W2T, Ws1T, Ws3T, Ws2T, slots, slots_out, out):
    E, INNER, CAP = 16, 176, 128
    TILES = TOKENS // P
    REST = INNER - P
    W13 = KC * 2 * INNER
    WALL = W13 + 2 * DIM
    FEEDS = TILES + E
    RING = 8
    FAR = float(1 << 20)
    LOW = -1e30

    with ExitStack() as ctx:
        def sb(name, shape, dt=F32):
            return ctx.enter_context(nc.sbuf_tensor("m_" + name, shape, dt))

        def ps(name):
            return ctx.enter_context(nc.psum_tensor("m_" + name, [P, 2, 512], F32))

        def sem(name):
            return ctx.enter_context(nc.semaphore("m_" + name))

        x_all = sb("x_all", [P, TILES, DIM])
        y_all = sb("y_all", [P, TILES, DIM])
        w_raw = sb("w_raw", [P, 2, WALL])
        w_sh = sb("w_sh", [P, 2, WALL], F32R)
        w_ex = sb("w_ex", [P, 4, 2, WALL], F32R)
        gate_raw = sb("gate_raw", [P, KC, E])
        gate = sb("gate", [P, KC, 2, E], F32R)
        bias = sb("bias", [P, E])
        ident = sb("ident", [P, P])
        before = sb("before", [P, P])
        ones = sb("ones", [P, P])
        zeros = sb("zeros", [P, DIM])
        rank = sb("rank", [P, E])
        go_on = sb("go_on", [P, E, TILES])
        power = sb("power", [P, 4])
        x_in = sb("x_in", [P, 2, DIM])
        xT_hi = sb("xT_hi", [P, 2, KC, P], F32R)
        xT_lo = sb("xT_lo", [P, 2, KC, P], F32R)
        act_g = sb("act_g", [P, 2, INNER])
        h = sb("h", [P, 2, 2 * P])
        hT_hi = sb("hT_hi", [P, 2, 2, P], F32R)
        hT_lo = sb("hT_lo", [P, 2, 2, P], F32R)
        y_slot = sb("y_slot", [P, 2, DIM])
        logit = sb("logit", [P, TILES, E])
        t1 = sb("t1", [P, TILES, E])
        t2 = sb("t2", [P, TILES, E])
        t3 = sb("t3", [P, TILES, E])
        t4 = sb("t4", [P, TILES, E])
        t5 = sb("t5", [P, TILES, E])
        score = sb("score", [P, TILES, E])
        pick = sb("pick", [P, TILES, E])
        chosen = sb("chosen", [P, 2, TILES, E])
        top = sb("top", [P, 2, TILES])
        place = sb("place", [P, 2, TILES])
        raw_w = sb("raw_w", [P, 2, TILES])
        total = sb("total", [P, TILES])
        weight = sb("weight", [P, 2, TILES])
        pos = sb("pos", [P, 2, TILES])
        valid = sb("valid", [P, 2, TILES])
        slot = sb("slot", [P, 2, TILES])
        target = sb("target", [P, 2, TILES])
        counts = sb("counts", [P, E, TILES])
        running = sb("running", [P, E, TILES])
        send_at = sb("send_at", [P, 2, TILES], mybir.dt.uint32)
        fetch_at = sb("fetch_at", [P, 2, TILES], mybir.dt.uint32)
        fetched = sb("fetched", [P, RING, DIM])
        stats = sb("stats", [P, 4, 6])
        mean_var = sb("mean_var", [P, 2, 4, 2])
        rstd = sb("rstd", [P, 2, 4])

        ps_x, ps_g, ps_h, ps_y = ps("ps_x"), ps("ps_g"), ps("ps_h"), ps("ps_y")
        ps_logit = ps_y[:, :, :].rearrange("p n (t w e) -> p (n t) w e", w=2, e=E)

        gate_in = sem("gate_in")
        all_in = sem("all_in")
        cleared = sem("cleared")
        x_landed = [sem(f"x_landed{n}") for n in range(2)]
        w_landed = [sem(f"w_landed{n}") for n in range(2)]
        sent = sem("sent")
        slots_stored = [sem(f"slots_stored{n}") for n in range(2)]
        fetched_in = [sem(f"fetched_in{n}") for n in range(RING)]
        stored = sem("stored")
        consts = sem("consts")
        gate_split = sem("gate_split")
        w_hi_done = sem("w_hi_done")
        w_lo_done = sem("w_lo_done")
        x_filled = sem("x_filled")
        xT_hi_done = sem("xT_hi_done")
        xT_lo_done = sem("xT_lo_done")
        logits_filled = sem("logits_filled")
        left_logits = sem("left_logits")
        logits_read = sem("logits_read")
        chosen_done = sem("chosen_done")
        counts_read = sem("counts_read")
        targets_done = sem("targets_done")
        route_act = sem("route_act")
        route = sem("route")
        softplus_part = sem("softplus_part")
        counted = sem("counted")
        g_filled = sem("g_filled")
        g_acted = sem("g_acted")
        h_done = sem("h_done")
        hT_filled = sem("hT_filled")
        hT_hi_done = sem("hT_hi_done")
        hT_lo_done = sem("hT_lo_done")
        y_filled = sem("y_filled")
        shared_left = sem("shared_left")
        y_left = sem("y_left")
        y_right = sem("y_right")
        weighed = sem("weighed")
        stats_done = sem("stats_done")
        stats_seen = sem("stats_seen")
        moments_done = sem("moments_done")
        var_done = sem("var_done")
        rstd_done = sem("rstd_done")
        y_done = sem("y_done")


        block = ctx.enter_context(nc.Block())

        x_tiles = x.rearrange("(n p) d -> p n d", p=P)
        out_tiles = out.rearrange("(n p) d -> p n d", p=P)
        slot_tiles = slots.rearrange("(n p) d -> p n d", p=P)
        slot_out_tiles = slots_out.rearrange("(n p) d -> p n d", p=P)
        PARTS = 4
        PART = TILES // PARTS
        GROUP = 4

        def weight_parts(n, w1, w3, w2):
            w13 = w_raw[:, n, 0:W13].rearrange("p (c w i) -> p c w i", c=KC, w=2)
            return ((w13[:, :, 0, :], w1.rearrange("(c p) i -> p c i", p=P)),
                    (w13[:, :, 1, :], w3.rearrange("(c p) i -> p c i", p=P)),
                    (w_raw[:, n, W13:W13 + DIM], w2[0:P, :]),
                    (w_raw[0:REST, n, W13 + DIM:WALL], w2[P:INNER, :]))

        @block.sync
        def _(sp):
            def load_x(n, i, src, first=False):
                if not first:
                    sp.wait_ge(x_filled, n - 1)
                sp.dma_start(x_in[:, i, :], src).then_inc(x_landed[i], 16)

            def load_weights(e, i):
                if not (isinstance(e, int) and e == 0):
                    sp.wait_ge(w_lo_done, e)
                for dst, src in weight_parts(1 - i, W1T[e], W3T[e], W2T[e]):
                    sp.dma_start(dst, src).then_inc(w_landed[1 - i], 16)

            sp.dma_start(gate_raw[:, :, :], gateT.rearrange("(c p) e -> p c e", p=P)).then_inc(gate_in, 16)
            sp.dma_start(bias[:, :], gate_b.rearrange("(a e) -> a e", a=1).to_broadcast([P, E])).then_inc(gate_in, 16)
            for i in range(2):
                load_x(i, i, x_tiles[:, i, :], True)
            with sp.Fori(1, TILES // 2) as u:
                for i in range(2):
                    load_x(2 * u + i, i, x_tiles[:, 2 * u + i, :])
            for i in range(2):
                load_x(TILES + i, i, x_tiles[:, i, :])
            sp.wait_ge(consts, 7)
            for dst, src in weight_parts(0, Ws1T, Ws3T, Ws2T):
                sp.dma_start(dst, src).then_inc(w_landed[0], 16)
            for k in range(PARTS):
                part = slice(k * PART, (k + 1) * PART)
                sp.dma_start(x_all[:, part, :], x_tiles[:, part, :]).then_inc(all_in, 16)
            sp.dma_start(slot_tiles, zeros[:, :].unsqueeze(1).to_broadcast([P, E, DIM])).then_inc(cleared, 16)
            load_weights(0, 0)
            load_weights(1, 1)
            with sp.Fori(1, TILES // 2) as u:
                for i in range(2):
                    load_x(TILES + 2 * u + i, i, x_tiles[:, 2 * u + i, :])
            for e in range(2, 4):
                load_weights(e, e % 2)
            sp.wait_ge(sent, 16 * 2 * TILES)
            for e in range(3):
                load_x(2 * TILES + e, e % 2, slot_tiles[:, e, :])
            with sp.Fori(1, E // 2 - 1) as u:
                for i in (1, 2):
                    load_x(2 * TILES + 2 * u + i, i % 2, slot_tiles[:, 2 * u + i, :])
                    load_weights(2 * u + i + 1, (i + 1) % 2)
            load_x(2 * TILES + E - 1, 1, slot_tiles[:, E - 1, :])
            with sp.Fori(0, TILES // GROUP) as g:
                sp.wait_ge(y_done, GROUP * g + GROUP)
                sp.dma_start(out_tiles[:, bass.ds(GROUP * g, GROUP), :], y_all[:, bass.ds(GROUP * g, GROUP), :]) \
                    .then_inc(stored, 16)
            sp.wait_ge(stored, 16 * TILES // GROUP)

        @block.gpsimd
        def _(pool):
            pool.memset(ident[:, :], 0.0).then_inc(consts, 1)
            pool.memset(zeros[:, :], 0.0).then_inc(consts, 1)
            pool.memset(ones[:, :], 1.0).then_inc(consts, 1)
            pool.memset(w_raw[:, :, :], 0.0).then_inc(consts, 1)
            pool.memset(h[:, :, :], 0.0).then_inc(consts, 1)
            pool.memset(go_on[:, :, :], 1.0).then_inc(consts, 1)
            pool.memset(power[:, :], -0.5).then_inc(consts, 1)
            pool.wait_ge(consts, 7)
            pool.affine_select(out=ident[:, :], in_=ident[:, :], compare_op=ALU.not_equal, fill=1.0,
                               base=0, pattern=[[-1, P]], channel_multiplier=1).then_inc(consts, 1)
            pool.affine_select(out=before[:, :], in_=ones[:, :], compare_op=ALU.is_ge, fill=0.0,
                               base=-1, pattern=[[1, P]], channel_multiplier=-1).then_inc(consts, 1)
            pool.memset(go_on[:, :, 0:1], 0.0).then_inc(consts, 1)
            for e in range(E):
                pool.memset(rank[:, e:e + 1], float(E - e)).then_inc(consts, 1)

            pool.wait_ge(targets_done, 2)
            pool.wait_ge(cleared, 16)
            pool.wait_ge(all_in, 16 * PARTS)
            for t in range(TILES):
                for k in range(2):
                    pool.indirect_dma_start(
                        out=slots[:, :], out_offset=bass.IndirectOffsetOnAxis(ap=send_at[:, k, t:t + 1], axis=0),
                        in_=x_all[:, t, :], in_offset=None, bounds_check=E * CAP - 1, oob_is_err=False) \
                        .then_inc(sent, 16)

            def inverse_deviation(g):
                pool.wait_ge(var_done, g + 1)
                pool.tensor_tensor(rstd[:, g % 2, :], mean_var[:, g % 2, :, 1], power[:, :], ALU.pow) \
                    .then_inc(rstd_done, 1)

            for i in range(2):
                pool.wait_ge(slots_stored[i], 16 * E // 2)
            for g in range(TILES // GROUP):
                for k in range(2):
                    for i in range(GROUP):
                        r = k * GROUP + i
                        if g >= 1:
                            pool.wait_ge(weighed, RING * (g - 1) + r + 1)
                        pool.indirect_dma_start(
                            out=fetched[:, r, :], out_offset=None, in_=slots_out[:, :],
                            in_offset=bass.IndirectOffsetOnAxis(
                                ap=fetch_at[:, k, GROUP * g + i:GROUP * g + i + 1], axis=0)) \
                            .then_inc(fetched_in[r], 16)
                if g >= 1:
                    inverse_deviation(g - 1)
            inverse_deviation(TILES // GROUP - 1)

        @block.tensor
        def _(pe):
            def turn(n, g, k, first=False):
                i = k % 2
                pe.wait_ge(x_landed[i], 16 * (g + k // 2 + 1))
                if not first:
                    pe.wait_ge(xT_lo_done, n - 1)
                for c in range(KC):
                    last = pe.transpose(ps_x[:, i, c * P:(c + 1) * P], x_in[:, i, c * P:(c + 1) * P], ident[:, :])
                last.then_inc(x_filled, 1)

            def logits(n, i):
                pe.wait_ge(xT_lo_done, n + 1)
                for c in range(KC):
                    pe.matmul(ps_logit[:, n, :, :], xT_hi[:, i, c, :], gate[:, c, :, :], start=(c == 0), stop=False)
                    last = pe.matmul(ps_logit[:, n, 0, :], xT_lo[:, i, c, :], gate[:, c, 0, :],
                                     start=False, stop=(c == KC - 1))
                last.then_inc(logits_filled, 1)

            def up(m, k, expert, first=False):
                i = k % 2
                pe.wait_ge(xT_lo_done, TILES + m + 1)
                if expert:
                    pe.wait_ge(w_lo_done, m - TILES + 2)
                if not first:
                    pe.wait_ge(h_done, m - 1)
                w = w_ex[:, k % 4, :, :] if expert else w_sh
                dst = ps_g[:, i, 0:2 * INNER]
                n = 0
                for c in range(KC):
                    cols = slice(c * 2 * INNER, (c + 1) * 2 * INNER)
                    for v, part in ((xT_hi, 0), (xT_hi, 1), (xT_lo, 0)):
                        last = pe.matmul(dst, v[:, i, c, :], w[:, part, cols], start=(n == 0), stop=(n == 3 * KC - 1))
                        n += 1
                last.then_inc(g_filled, 1)

            def turn_inner(m, k, first=False):
                i = k % 2
                pe.wait_ge(h_done, m + 1)
                if not first:
                    pe.wait_ge(hT_lo_done, m - 1)
                for c in range(2):
                    last = pe.transpose(ps_h[:, i, c * P:(c + 1) * P], h[:, i, c * P:(c + 1) * P], ident[:, :])
                last.then_inc(hT_filled, 1)

            def down(m, k, expert, first=False):
                i = k % 2
                pe.wait_ge(hT_lo_done, m + 1)
                if first:
                    pe.wait_ge(logits_read, 1)
                else:
                    pe.wait_ge(y_right, m - 1)
                w = w_ex[:, k % 4, :, :] if expert else w_sh
                for c, rows in enumerate((P, REST)):
                    cols = slice(W13 + c * DIM, W13 + (c + 1) * DIM)
                    pe.matmul(ps_y[:, i, :], hT_hi[0:rows, i, c, :], w[0:rows, :, cols], start=(c == 0), stop=False)
                    last = pe.matmul(ps_y[:, i, 0:DIM], hT_lo[0:rows, i, c, :], w[0:rows, 0, cols],
                                     start=False, stop=(c == 1))
                last.then_inc(y_filled, 1)

            def feed_group(g, expert, first=False, last=False):
                for k in range(GROUP):
                    m = GROUP * g + k
                    if not (last and k == GROUP - 1):
                        turn(TILES + m + 1, TILES // 2 + 2 * g, k + 1)
                    up(m, k, expert, first and k < 2)
                    if not (first and k == 0):
                        turn_inner(m - 1, k + 3, first and k < 3)
                    if not (first and k < 2):
                        down(m - 2, k + 2, expert and not (first_expert(g) and k < 2), first and k < 4)

            def first_expert(g):
                return isinstance(g, int) and g == TILES // GROUP

            pe.wait_ge(consts, 10 + E)
            pe.wait_ge(gate_split, 2)
            turn(0, 0, 0, True)
            for i in range(2):
                turn(i + 1, 0, i + 1, i == 0)
                logits(i, i)
            with pe.Fori(1, TILES // 2) as u:
                for i in range(2):
                    turn(2 * u + i + 1, u, i + 1)
                    logits(2 * u + i, i)
            pe.wait_ge(chosen_done, 1)
            for n, lhs in enumerate((before, ones)):
                last = pe.matmul(ps_g[:, n, :], lhs[:, :], pick[:, :, :], start=True, stop=True)
            last.then_inc(counted, 1)
            pe.wait_ge(w_lo_done, 1)
            pe.wait_ge(counts_read, 2)
            feed_group(0, False, first=True)
            with pe.Fori(1, TILES // GROUP) as g:
                feed_group(g, False)
            feed_group(TILES // GROUP, True)
            with pe.Fori(TILES // GROUP + 1, FEEDS // GROUP - 1) as g:
                feed_group(g, True)
            feed_group(FEEDS // GROUP - 1, True, last=True)
            turn_inner(FEEDS - 1, 3)
            down(FEEDS - 2, 2, True)
            down(FEEDS - 1, 3, True)

        @block.scalar
        def _(act):
            def x_hi(n, k, routed_before, first=False):
                i = k % 2
                act.wait_ge(x_filled, n + 1)
                if not first:
                    if routed_before:
                        act.wait_ge(logits_filled, n - 1)
                    else:
                        act.wait_ge(g_filled, n - TILES - 1)
                nc.scalar.activation(xT_hi[:, i, :, :], ps_x[:, i, 0:DIM], ACT.Copy).then_inc(xT_hi_done, 1)

            def split_weights(n, i, dst, e, first=False):
                act.wait_ge(w_landed[i], n)
                if e is not None and not first:
                    act.wait_ge(y_filled, TILES + e - 3)
                nc.scalar.activation(dst, w_raw[:, i, :], ACT.Copy).then_inc(w_hi_done, 1)

            def g_act(m, k, first=False):
                i = k % 2
                act.wait_ge(g_filled, m + 1)
                if not first:
                    act.wait_ge(h_done, m - 1)
                nc.scalar.activation(act_g[:, i, :], ps_g[:, i, 0:INNER], ACT.Silu).then_inc(g_acted, 1)

            def h_hi(m, k, first=False):
                i = k % 2
                act.wait_ge(hT_filled, m + 1)
                if not first:
                    act.wait_ge(y_filled, m - 1)
                nc.scalar.activation(hT_hi[:, i, :, :], ps_h[:, i, 0:2 * P], ACT.Copy).then_inc(hT_hi_done, 1)

            def y_copy(m, k, first=False):
                i = k % 2
                act.wait_ge(y_filled, m + 1)
                if not first:
                    act.wait_ge(slots_stored[i], 8 * (m - TILES - i))
                nc.scalar.activation(y_slot[:, i, :], ps_y[:, i, 0:DIM], ACT.Copy).then_inc(y_left, 1)

            def store_expert(m, k):
                act.wait_ge(y_right, m + 1)
                act.dma_start(slot_out_tiles[:, m - TILES, :], y_slot[:, k % 2, :]).then_inc(slots_stored[k % 2], 16)

            def feed_group(g, expert, first=False, last=False):
                at = isinstance(g, int)
                for k in range(GROUP):
                    m = GROUP * g + k
                    if not (last and k == GROUP - 1):
                        x_hi(TILES + m + 1, k + 1, first and k == 0)
                    g_act(m, k, first and k < 2)
                    if not (first and k == 0):
                        h_hi(m - 1, k + 3, first and k < 3)
                    if expert:
                        boundary = at and g == TILES // GROUP
                        if not (boundary and k < 3):
                            store_expert(m - 3, k + 1)
                        if not (boundary and k < 2):
                            y_copy(m - 2, k + 2, boundary)
                        if not (last and k >= 2):
                            split_weights(32 * (m - TILES + 3 - (k + 1) % 2) + 64, (k + 1) % 2,
                                          w_ex[:, (k + 2) % 4, 0, :], m - TILES + 2, boundary and k < 2)

            act.wait_ge(gate_in, 32)
            nc.scalar.activation(gate[:, :, 0, :], gate_raw[:, :, :], ACT.Copy).then_inc(gate_split, 1)
            for n in range(2):
                x_hi(n, n, True, True)
            with act.Fori(1, TILES // 2) as u:
                for i in range(2):
                    x_hi(2 * u + i, i, True)
            act.wait_ge(logits_filled, TILES)
            nc.scalar.activation(logit[:, :, :], ps_logit[:, :, 0, :], ACT.Copy).then_inc(left_logits, 1)
            split_weights(64, 0, w_sh[:, 0, :], None)
            x_hi(TILES, 0, True)
            act.wait_ge(route, 1)
            nc.scalar.activation(t1[:, :, :], logit[:, :, :], ACT.Abs).then_inc(route_act, 1)
            act.wait_ge(route_act, 1)
            nc.scalar.activation(t2[:, :, :], t1[:, :, :], ACT.Exp, scale=-1.0).then_inc(route_act, 1)
            act.wait_ge(route, 2)
            nc.scalar.activation(t4[:, :, :], t3[:, :, :], ACT.Ln).then_inc(route_act, 1)
            split_weights(64, 1, w_ex[:, 0, 0, :], 0, True)
            act.wait_ge(route, 8)
            nc.scalar.activation(score[:, :, :], t5[:, :, :], ACT.Sqrt).then_inc(route_act, 1)
            split_weights(128, 0, w_ex[:, 1, 0, :], 1, True)
            feed_group(0, False, first=True)
            with act.Fori(1, TILES // GROUP) as g:
                feed_group(g, False)
            feed_group(TILES // GROUP, True)
            with act.Fori(TILES // GROUP + 1, FEEDS // GROUP - 1) as g:
                feed_group(g, True)
            feed_group(FEEDS // GROUP - 1, True, last=True)
            h_hi(FEEDS - 1, 3)
            store_expert(FEEDS - 3, 1)
            y_copy(FEEDS - 2, 2)
            store_expert(FEEDS - 2, 2)
            y_copy(FEEDS - 1, 3)
            store_expert(FEEDS - 1, 3)

        @block.vector
        def _(dve):
            def x_lo(n, k):
                i = k % 2
                dve.wait_ge(xT_hi_done, n + 1)
                dve.tensor_tensor(xT_lo[:, i, :, :], ps_x[:, i, 0:DIM].rearrange("p (c t) -> p c t", c=KC),
                                  xT_hi[:, i, :, :].bitcast(F32), ALU.subtract).then_inc(xT_lo_done, 1)

            def weights_lo(n, i, w):
                dve.wait_ge(w_hi_done, n)
                dve.tensor_tensor(w[:, 1, :], w_raw[:, i, :], w[:, 0, :].bitcast(F32), ALU.subtract) \
                    .then_inc(w_lo_done, 1)

            def gated(m, k, first=False):
                i = k % 2
                dve.wait_ge(g_acted, m + 1)
                if not first:
                    dve.wait_ge(hT_filled, m - 1)
                dve.tensor_tensor(h[:, i, 0:INNER], ps_g[:, i, INNER:2 * INNER], act_g[:, i, :], ALU.mult) \
                    .then_inc(h_done, 1)

            def h_lo(m, k):
                i = k % 2
                dve.wait_ge(hT_hi_done, m + 1)
                dve.tensor_tensor(hT_lo[:, i, :, :], ps_h[:, i, 0:2 * P].rearrange("p (c t) -> p c t", c=2),
                                  hT_hi[:, i, :, :].bitcast(F32), ALU.subtract).then_inc(hT_lo_done, 1)

            def add_shared(m, k):
                i = k % 2
                dve.wait_ge(y_filled, m + 1)
                dve.tensor_tensor(y_all[:, m, :], ps_y[:, i, 0:DIM], x_all[:, m, :], ALU.add).then_inc(shared_left, 1)
                dve.wait_ge(shared_left, m + 1)
                dve.tensor_tensor(y_all[:, m, :], ps_y[:, i, DIM:2 * DIM], y_all[:, m, :], ALU.add) \
                    .then_inc(y_right, 1)

            def add_expert(m, k):
                i = k % 2
                dve.wait_ge(y_left, m - TILES + 1)
                dve.tensor_tensor(y_slot[:, i, :], ps_y[:, i, DIM:2 * DIM], y_slot[:, i, :], ALU.add) \
                    .then_inc(y_right, 1)

            def feed_group(g, expert, first=False, last=False):
                boundary = isinstance(g, int) and g == TILES // GROUP
                for k in range(GROUP):
                    m = GROUP * g + k
                    if not (last and k == GROUP - 1):
                        x_lo(TILES + m + 1, k + 1)
                    gated(m, k, first and k < 2)
                    if not (first and k == 0):
                        h_lo(m - 1, k + 3)
                    if not (first and k < 2):
                        if expert and not (boundary and k < 2):
                            add_expert(m - 2, k + 2)
                        else:
                            add_shared(m - 2, k + 2)
                    if expert and not (last and k >= 2):
                        weights_lo(m - TILES + 4, (k + 1) % 2, w_ex[:, (k + 2) % 4, :, :])

            dve.wait_ge(gate_split, 1)
            dve.tensor_tensor(gate[:, :, 1, :], gate_raw[:, :, :], gate[:, :, 0, :].bitcast(F32), ALU.subtract) \
                .then_inc(gate_split, 1)
            with dve.Fori(0, TILES // 2) as u:
                for i in range(2):
                    x_lo(2 * u + i, i)

            done = 0

            def then(instruction):
                nonlocal done
                done += 1
                instruction.then_inc(route, 1)
                dve.wait_ge(route, done)

            def experts(v):
                return v.unsqueeze(2).to_broadcast([P, TILES, E])

            def tiles(v):
                return v.unsqueeze(1).to_broadcast([P, TILES, E])

            dve.wait_ge(left_logits, 1)
            dve.wait_ge(consts, 10 + E)
            then(dve.tensor_tensor(logit[:, :, :], ps_logit[:, :, 1, :], logit[:, :, :], ALU.add))
            dve.sem_inc(logits_read, 1)
            weights_lo(1, 0, w_sh)
            x_lo(TILES, 0)
            dve.wait_ge(route_act, 2)
            then(dve.tensor_scalar(t3[:, :, :], t2[:, :, :], 1.0, None, ALU.add))
            then(dve.tensor_scalar(t5[:, :, :], t3[:, :, :], -1.0, 0.0, ALU.add, ALU.is_equal))
            then(dve.scalar_tensor_tensor(t1[:, :, :], t3[:, :, :], -1.0, t5[:, :, :], ALU.add, ALU.add))
            then(dve.reciprocal(t1[:, :, :], t1[:, :, :]))
            dve.wait_ge(route_act, 3)
            then(dve.tensor_tensor(t4[:, :, :], t4[:, :, :], t1[:, :, :], ALU.mult))
            then(dve.tensor_tensor(t4[:, :, :], t4[:, :, :], t5[:, :, :], ALU.add))
            dve.tensor_tensor(t4[:, :, :], t4[:, :, :], t2[:, :, :], ALU.mult).then_inc(softplus_part, 1)
            dve.wait_ge(softplus_part, 1)
            then(dve.scalar_tensor_tensor(t5[:, :, :], logit[:, :, :], 0.0, t4[:, :, :], ALU.max, ALU.add))
            weights_lo(2, 1, w_ex[:, 0, :, :])
            dve.wait_ge(route_act, 4)
            then(dve.tensor_tensor(pick[:, :, :], score[:, :, :], tiles(bias[:, :]), ALU.add))
            for k in range(2):
                then(dve.tensor_reduce(top[:, k, :], pick[:, :, :], AX.X, ALU.max))
                then(dve.tensor_tensor(t1[:, :, :], pick[:, :, :], experts(top[:, k, :]), ALU.is_equal))
                then(dve.tensor_tensor(t1[:, :, :], t1[:, :, :], tiles(rank[:, :]), ALU.mult))
                then(dve.tensor_reduce(place[:, k, :], t1[:, :, :], AX.X, ALU.max))
                then(dve.tensor_tensor(chosen[:, k, :, :], tiles(rank[:, :]), experts(place[:, k, :]), ALU.is_equal))
                if k == 0:
                    then(dve.scalar_tensor_tensor(pick[:, :, :], chosen[:, k, :, :], LOW, pick[:, :, :],
                                                  ALU.mult, ALU.add))
            then(dve.tensor_tensor(pick[:, :, :], chosen[:, 0, :, :], chosen[:, 1, :, :], ALU.add))
            dve.sem_inc(chosen_done, 1)
            for k in range(2):
                then(dve.tensor_tensor(t1[:, :, :], score[:, :, :], chosen[:, k, :, :], ALU.mult))
                then(dve.tensor_reduce(raw_w[:, k, :], t1[:, :, :], AX.X, ALU.add))
            then(dve.tensor_tensor(total[:, :], raw_w[:, 0, :], raw_w[:, 1, :], ALU.add))
            then(dve.reciprocal(total[:, :], total[:, :]))
            dve.wait_ge(counted, 1)
            dve.tensor_copy(counts[:, :, :].rearrange("p e t -> p t e"),
                            ps_g[:, 1, :].rearrange("p (t e) -> p t e", e=E)).then_inc(counts_read, 1)
            dve.wait_ge(counts_read, 1)
            then(dve.tensor_tensor_scan(running[:, :, :].rearrange("p e t -> p (e t)"),
                                        go_on[:, :, :].rearrange("p e t -> p (e t)"),
                                        counts[:, :, :].rearrange("p e t -> p (e t)"), 0.0, ALU.mult, ALU.add))
            then(dve.tensor_tensor(running[:, :, :], running[:, :, :], counts[:, :, :], ALU.subtract))
            dve.tensor_tensor(t2[:, :, :], ps_g[:, 0, :].rearrange("p (t e) -> p t e", e=E),
                              running[:, :, :].rearrange("p e t -> p t e"), ALU.add).then_inc(counts_read, 1)
            dve.wait_ge(counts_read, 2)
            for k in range(2):
                then(dve.tensor_tensor(t1[:, :, :], t2[:, :, :], chosen[:, k, :, :], ALU.mult))
                then(dve.tensor_reduce(pos[:, k, :], t1[:, :, :], AX.X, ALU.add))
            then(dve.tensor_scalar(valid[:, :, :], pos[:, :, :], float(CAP), None, ALU.is_lt))
            for k in range(2):
                then(dve.tensor_tensor(weight[:, k, :], raw_w[:, k, :], total[:, :], ALU.mult))
            then(dve.tensor_tensor(weight[:, :, :], weight[:, :, :], valid[:, :, :], ALU.mult))
            then(dve.tensor_tensor(pos[:, :, :], pos[:, :, :], valid[:, :, :], ALU.mult))
            then(dve.tensor_scalar(slot[:, :, :], place[:, :, :], -float(CAP), float(E * CAP), ALU.mult, ALU.add))
            then(dve.tensor_tensor(slot[:, :, :], slot[:, :, :], pos[:, :, :], ALU.add))
            then(dve.tensor_scalar(target[:, :, :], valid[:, :, :], -FAR, FAR, ALU.mult, ALU.add))
            then(dve.tensor_tensor(target[:, :, :], target[:, :, :], slot[:, :, :], ALU.add))
            dve.tensor_copy(send_at[:, :, :], target[:, :, :]).then_inc(targets_done, 1)
            dve.tensor_copy(fetch_at[:, :, :], slot[:, :, :]).then_inc(targets_done, 1)

            weights_lo(3, 0, w_ex[:, 1, :, :])
            dve.wait_ge(all_in, 16 * PARTS)
            feed_group(0, False, first=True)
            with dve.Fori(1, TILES // GROUP) as g:
                feed_group(g, False)
            feed_group(TILES // GROUP, True)
            with dve.Fori(TILES // GROUP + 1, FEEDS // GROUP - 1) as g:
                feed_group(g, True)
            feed_group(FEEDS // GROUP - 1, True, last=True)
            h_lo(FEEDS - 1, 3)
            add_expert(FEEDS - 2, 2)
            add_expert(FEEDS - 1, 3)

            def combine(g, parity):
                for k in range(2):
                    for i in range(GROUP):
                        r, t = k * GROUP + i, GROUP * g + i
                        dve.wait_ge(fetched_in[r], 16 * (g + 1))
                        if k == 1:
                            dve.wait_ge(weighed, RING * g + i + 1)
                        dve.scalar_tensor_tensor(y_all[:, t, :], fetched[:, r, :], weight[:, k, bass.ds(t, 1)],
                                                 y_all[:, t, :], ALU.mult, ALU.add).then_inc(weighed, 1)
                dve.wait_ge(weighed, RING * (g + 1))
                dve.sem_inc(stats_seen, 1)
                for i in range(GROUP):
                    dve.bn_stats(stats[:, i, :], y_all[:, GROUP * g + i, :]).then_inc(stats_done, 1)
                dve.wait_ge(stats_done, GROUP * (g + 1))
                dve.sem_inc(stats_seen, 1)
                for i in range(GROUP):
                    last = dve.bn_aggr(mean_var[:, parity, i, :], stats[:, i, :])
                last.then_inc(moments_done, 1)
                dve.wait_ge(moments_done, g + 1)
                dve.tensor_scalar(mean_var[:, parity, :, 1], mean_var[:, parity, :, 1], EPS, None, ALU.add) \
                    .then_inc(var_done, 1)

            def normalise(g, parity):
                dve.wait_ge(rstd_done, g + 1)
                for i in range(GROUP):
                    t = GROUP * g + i
                    dve.tensor_scalar(y_all[:, t, :], y_all[:, t, :], mean_var[:, parity, i, 0:1],
                                      rstd[:, parity, i:i + 1], ALU.subtract, ALU.mult).then_inc(y_done, 1)

            combine(0, 0)
            with dve.Fori(0, TILES // GROUP // 2 - 1) as v:
                for i in range(2):
                    combine(2 * v + i + 1, (i + 1) % 2)
                    normalise(2 * v + i, i)
            combine(TILES // GROUP - 1, 1)
            normalise(TILES // GROUP - 2, 0)
            normalise(TILES // GROUP - 1, 1)


def decoder_layer(nc, a, out):
    def scratch(name, rows):
        return nc.dram_tensor(name, [rows, DIM], F32).ap()

    x1, x2 = scratch("x1", TOKENS), scratch("x2", TOKENS)
    slots, slots_out = scratch("slots", 16 * 128), scratch("slots_out", 16 * 128)
    local_attention(nc, a["x"], a["xT"], a["attn_Wq"], a["attn_Wk"], a["attn_WvT"], a["attn_Wo"], x1)
    latent_attention(nc, x1, a["ctx"], a["rope"], a["xattn_Wq"], a["xattn_w_kc_qT"], a["xattn_W_qrT"],
                     a["xattn_W_krT"], a["xattn_w_kc_kv"], a["xattn_WoT"], x2)
    mixture(nc, x2, a["gate_wT"], a["gate_b"], a["W1T"], a["W3T"], a["W2T"], a["Ws1T"], a["Ws3T"], a["Ws2T"],
            slots, slots_out, out)



def rope_tables():
    import numpy as np
    steps = np.arange(0, 64, 2, dtype=np.float32) / np.float32(64)
    inv_freq = (np.float32(1.0) / np.float32(10000.0) ** steps).astype(np.float32)
    freqs = np.arange(SEQ, dtype=np.float32)[:, None] * inv_freq[None, :]
    cos, sin = np.repeat(np.cos(freqs), 2, axis=-1), np.repeat(np.sin(freqs), 2, axis=-1)
    sin[:, :32] = -sin[:, :32]
    return np.stack([cos, sin]).astype(np.float32)


def kernel(x, ctx_512, L0_attn_Wq, L0_attn_Wk, L0_attn_Wv, L0_attn_Wo, L0_xattn_Wq, L0_xattn_w_kc_q,
           L0_xattn_w_kc_kv, L0_xattn_W_qr, L0_xattn_W_kr, L0_xattn_Wo, L0_ffn_input_ids, L0_ffn_gate_w,
           L0_ffn_gate_b, L0_ffn_W1, L0_ffn_W3, L0_ffn_W2, L0_ffn_Ws1, L0_ffn_Ws3, L0_ffn_Ws2):
    import numpy as np
    import concourse.bacc as bacc
    from concourse.bass_utils import run_bass_kernel_spmd

    def turned(a):
        a = np.asarray(a)
        return np.ascontiguousarray(np.swapaxes(a, -1, -2))

    rows = np.ascontiguousarray(np.asarray(x).reshape(TOKENS, DIM))
    arrays = {
        "x": rows, "xT": turned(rows), "ctx": np.ascontiguousarray(ctx_512), "rope": rope_tables(),
        "attn_Wq": np.ascontiguousarray(L0_attn_Wq), "attn_Wk": np.ascontiguousarray(L0_attn_Wk),
        "attn_WvT": turned(L0_attn_Wv), "attn_Wo": np.ascontiguousarray(L0_attn_Wo),
        "xattn_Wq": np.ascontiguousarray(L0_xattn_Wq), "xattn_w_kc_qT": turned(L0_xattn_w_kc_q),
        "xattn_W_qrT": turned(L0_xattn_W_qr), "xattn_W_krT": turned(L0_xattn_W_kr),
        "xattn_w_kc_kv": np.ascontiguousarray(L0_xattn_w_kc_kv), "xattn_WoT": turned(L0_xattn_Wo),
        "gate_wT": turned(L0_ffn_gate_w), "gate_b": np.ascontiguousarray(L0_ffn_gate_b),
        "W1T": turned(L0_ffn_W1), "W3T": turned(L0_ffn_W3), "W2T": turned(L0_ffn_W2),
        "Ws1T": turned(L0_ffn_Ws1), "Ws3T": turned(L0_ffn_Ws3), "Ws2T": turned(L0_ffn_Ws2),
    }
    nc = bacc.Bacc("TRN2", target_bir_lowering=False, num_devices=1)
    aps = {n: nc.dram_tensor(n, a.shape, mybir.dt.from_np(a.dtype), kind="ExternalInput").ap()
           for n, a in arrays.items()}
    out = nc.dram_tensor("out", [TOKENS, DIM], F32, kind="ExternalOutput").ap()
    decoder_layer(nc, aps, out)
    result = run_bass_kernel_spmd(nc, [arrays], core_ids=[0])
    return result.results[0]["out"].reshape(BATCH, SEQ, DIM)
```

```python
from contextlib import ExitStack

import concourse.bass as bass
from concourse import mybir

F32 = mybir.dt.float32
F32R = mybir.dt.float32r
ALU = mybir.AluOpType
ACT = mybir.ActivationFunctionType
AX = mybir.AxisListType

P = 128
BATCH, SEQ, DIM = 64, 64, 256
TOKENS = BATCH * SEQ
HEADS, HEAD_DIM = 16, 128
WINDOW, GLOBAL = 64, 16
KC = DIM // P
UNIT = 256
UNITS = TOKENS // UNIT
PAIRS = UNIT // P
UB = UNIT // SEQ
HS = 8
STEPS = HEADS // HS
HP = HS // 2
EPS = 1e-5
MASKED = -1e30


def local_attention(nc, x, xT, Wq, Wk, WvT, Wo, out):
    SCALE = float(HEAD_DIM) ** -0.5
    STAGE = 1024
    W_LOADS = 2 * KC * 2048 // STAGE
    B_LOADS = HEADS // 2
    RING = 4
    JOBS = PAIRS * 2 * KC

    with ExitStack() as ctx:
        def sb(name, shape, dt=F32):
            return ctx.enter_context(nc.sbuf_tensor("a_" + name, shape, dt))

        def ps(name, shape):
            return ctx.enter_context(nc.psum_tensor("a_" + name, shape, F32))

        def sem(name):
            return ctx.enter_context(nc.semaphore("a_" + name))

        stage_own = sb("stage", [P, STAGE])
        wqk_hi = sb("wqk_hi", [P, 2, KC, 2048], F32R)
        wqk_lo = sb("wqk_lo", [P, 2, KC, 2048], F32R)
        wvo = sb("wvo", [P, HEADS * KC, 2, DIM], F32R)
        ident = sb("ident", [P, P])
        mask = sb("mask", [P, SEQ])
        y_and_res = sb("y_and_res", [P, 2, PAIRS, DIM])
        y, x_res = y_and_res[:, 0, :, :], y_and_res[:, 1, :, :]
        x_raw = sb("x_raw", [P, UB, DIM])
        x_hl = sb("x_hl", [P, 2, UB, DIM], F32R)
        xT_raw = sb("xT_raw", [P, KC, UNIT])
        xT_hi = sb("xT_hi", [P, KC, UNIT], F32R)
        xT_lo = sb("xT_lo", [P, KC, UNIT], F32R)
        qk = sb("qk", [P, HS, 2, UNIT])
        s_sb = sb("s_sb", [P, PAIRS, HS, SEQ])
        row_max = sb("row_max", [P, PAIRS, HS])
        row_sum = sb("row_sum", [P, PAIRS, HS])
        inv_sum = sb("inv_sum", [P, PAIRS, HS])
        pT_hi = sb("pT_hi", [P, 2, PAIRS, 2, HP, SEQ], F32R)
        pT_lo = sb("pT_lo", [P, PAIRS, 2, HP, SEQ], F32R)
        mix_hi = sb("mix_hi", [P, RING, HP, P], F32R)
        mix_lo = sb("mix_lo", [P, RING, HP, P], F32R)
        stats = sb("stats", [P, PAIRS, 6])
        mean_var = sb("mean_var", [P, PAIRS, 2])
        rstd = sb("rstd", [P, PAIRS, 1])
        power = sb("power", [P, 1])

        stage = (stage_own[:, :], s_sb[:, :, :, :].rearrange("p n h k -> p (n h k)"),
                 y_and_res[:, :, :, :].rearrange("p w n d -> p (w n d)"))

        ps_s = ps("ps_s", [P, PAIRS, HS, SEQ])
        ps_qk = ps("ps_qk", [P, 2, 2, UNIT])
        ps_mix = ps("ps_mix", [P, 2, 512])
        ps_out = ps("ps_out", [P, PAIRS, 2, DIM])

        staged = [sem(f"staged{n}") for n in range(3)]
        xT_in = sem("xT_in")
        xd_in = sem("xd_in")
        xr_in = sem("xr_in")
        stored = sem("stored")
        w_hi = sem("w_hi")
        w_lo = sem("w_lo")
        fold_first = sem("fold_first")
        fold_filled = sem("fold_filled")
        fold_hi = sem("fold_hi")
        fold_lo = sem("fold_lo")
        consts = sem("consts")
        xT_hi_done = sem("xT_hi_done")
        xT_lo_done = sem("xT_lo_done")
        x_hi_done = sem("x_hi_done")
        x_lo_done = sem("x_lo_done")
        qk_filled = sem("qk_filled")
        qk_copied = sem("qk_copied")
        s_filled = sem("s_filled")
        masked = sem("masked")
        maxed = sem("maxed")
        shifted = sem("shifted")
        exped = sem("exped")
        summed = sem("summed")
        inverted = sem("inverted")
        normed = sem("normed")
        t_filled = sem("t_filled")
        pT_hi_done = sem("pT_hi_done")
        pT_twice = sem("pT_twice")
        pT_lo_done = sem("pT_lo_done")
        mix_filled = sem("mix_filled")
        mix_hi_done = sem("mix_hi_done")
        mix_lo_done = sem("mix_lo_done")
        proj_done = sem("proj_done")
        left_added = sem("left_added")
        right_added = sem("right_added")
        stats_done = sem("stats_done")
        stats_seen = sem("stats_seen")
        moments_done = sem("moments_done")
        var_done = sem("var_done")
        rstd_done = sem("rstd_done")
        y_done = sem("y_done")

        def staged_count(n):
            return sum(32 if m < B_LOADS else 16 for m in range(n % 3, n + 1, 3))

        def w_piece(n):
            half, i, c = n // 4, n // 2 % 2, n % 2
            return i, c, slice(half * STAGE, (half + 1) * STAGE)

        block = ctx.enter_context(nc.Block())

        xT_v = xT.rearrange("(c p) t -> p c t", p=P)
        x_pairs = x.rearrange("(n p) d -> p n d", p=P)
        x_batches = x.rearrange("(b t) d -> t b d", t=SEQ)
        out_pairs = out.rearrange("(n p) d -> p n d", p=P)
        WvT_v = WvT.rearrange("(h k) d -> k h d", k=P)
        Wo_v = Wo.rearrange("(h k) d -> k h d", k=P)

        @block.sync
        def _(sp):
            def load_xT(u):
                if not (isinstance(u, int) and u == 0):
                    sp.wait_ge(xT_lo_done, u)
                sp.dma_start(xT_raw[:, :, :], xT_v[:, :, bass.ds(u * UNIT, UNIT)]).then_inc(xT_in, 16)

            def load_xd(u):
                if not (isinstance(u, int) and u == 0):
                    sp.wait_ge(x_lo_done, 2 * u)
                for e in range(2):
                    sp.dma_start(x_raw[64 * e:64 * e + 64, :, :], x_batches[:, bass.ds(u * UB, UB), :]) \
                        .then_inc(xd_in, 16)

            def load_xres(u):
                if not (isinstance(u, int) and u == 0):
                    sp.wait_ge(left_added, PAIRS * u)
                sp.dma_start(x_res[:, :, :], x_pairs[:, bass.ds(u * PAIRS, PAIRS), :]).then_inc(xr_in, 16)

            def store(u):
                sp.wait_ge(y_done, PAIRS * (u + 1))
                sp.dma_start(out_pairs[:, bass.ds(u * PAIRS, PAIRS), :], y[:, :, :]).then_inc(stored, 16)

            for n in range(B_LOADS):
                if n >= 3:
                    sp.wait_ge(fold_filled, n - 2)
                dst = stage[n % 3].rearrange("p (h w d) -> p h w d", h=2, w=2)
                sp.dma_start(dst[:, :, 0, :], WvT_v[:, 2 * n:2 * n + 2, :]).then_inc(staged[n % 3], 16)
                sp.dma_start(dst[:, :, 1, :], Wo_v[:, 2 * n:2 * n + 2, :]).then_inc(staged[n % 3], 16)
            load_xT(0)
            for n in range(B_LOADS, B_LOADS + W_LOADS):
                if n - 3 < B_LOADS:
                    sp.wait_ge(fold_filled, n - 2)
                else:
                    sp.wait_ge(w_lo, n - 2 - B_LOADS)
                i, c, cols = w_piece(n - B_LOADS)
                sp.dma_start(stage[n % 3], (Wq, Wk)[i][c * P:(c + 1) * P, cols]).then_inc(staged[n % 3], 16)
            load_xd(0)
            sp.wait_ge(w_lo, W_LOADS)
            load_xres(0)
            load_xT(1)
            load_xd(1)
            with sp.Fori(1, UNITS - 1) as u:
                load_xT(u + 1)
                store(u - 1)
                load_xres(u)
                load_xd(u + 1)
            store(UNITS - 2)
            load_xres(UNITS - 1)
            store(UNITS - 1)
            sp.wait_ge(stored, 16 * UNITS)

        @block.gpsimd
        def _(pool):
            pool.memset(ident[:, :], 0.0).then_inc(consts, 1)
            pool.memset(power[:, :], -0.5).then_inc(consts, 1)
            pool.memset(mask[:, :], 0.0).then_inc(consts, 1)
            pool.wait_ge(consts, 3)
            pool.affine_select(out=ident[:, :], in_=ident[:, :], compare_op=ALU.not_equal, fill=1.0,
                               base=0, pattern=[[-1, P]], channel_multiplier=1).then_inc(consts, 1)
            n = 4
            for b in range(2):
                half = mask[b * SEQ:(b + 1) * SEQ, :]
                for sign in (1, -1):
                    pool.affine_select(out=half, in_=half, compare_op=ALU.is_ge, fill=MASKED,
                                       base=WINDOW // 2 - 1, pattern=[[sign, SEQ]],
                                       channel_multiplier=-sign).then_inc(consts, 1)
                    n += 1
                    pool.wait_ge(consts, n)
                pool.memset(mask[b * SEQ:(b + 1) * SEQ, 0:GLOBAL], 0.0).then_inc(consts, 1)
                pool.affine_select(out=half[:, GLOBAL:SEQ], in_=half[:, GLOBAL:SEQ], compare_op=ALU.is_ge, fill=0.0,
                                   base=-GLOBAL, pattern=[[0, SEQ - GLOBAL]],
                                   channel_multiplier=1).then_inc(consts, 1)
                n += 2
            pool.wait_ge(consts, n)

            def split_xT(u):
                pool.wait_ge(xT_hi_done, u + 1)
                pool.tensor_tensor(xT_lo[:, :, :], xT_raw[:, :, :], xT_hi[:, :, :].bitcast(F32), ALU.subtract) \
                    .then_inc(xT_lo_done, 1)

            def split_x(u):
                for e in range(2):
                    rows = slice(64 * e, 64 * e + 64)
                    pool.wait_ge(x_hi_done, 2 * u + e + 1)
                    pool.tensor_tensor(x_hl[rows, 1 - e, :, :], x_raw[rows, :, :], x_hl[rows, e, :, :].bitcast(F32),
                                       ALU.subtract).then_inc(x_lo_done, 1)
                    pool.wait_ge(x_lo_done, 2 * u + e + 1)

            def inverse_deviation(u):
                for p in range(PAIRS):
                    pool.wait_ge(var_done, PAIRS * u + p + 1)
                    pool.tensor_tensor(rstd[:, p, :], mean_var[:, p, 1:2], power[:, :], ALU.pow) \
                        .then_inc(rstd_done, 1)

            split_xT(0)
            split_x(0)
            split_xT(1)
            with pool.Fori(1, UNITS - 1) as u:
                split_x(u)
                inverse_deviation(u - 1)
                split_xT(u + 1)
            split_x(UNITS - 1)
            inverse_deviation(UNITS - 2)
            inverse_deviation(UNITS - 1)

        @block.tensor
        def _(pe):
            def scores(s):
                pe.wait_ge(qk_copied, HS * (s + 1))
                for p in range(PAIRS):
                    for hh in range(HS):
                        for b in range(2):
                            t = p * P + b * SEQ
                            last = pe.matmul(ps_s[b * SEQ:(b + 1) * SEQ, p, hh, :], qk[:, hh, 0, t:t + SEQ],
                                             qk[:, hh, 1, t:t + SEQ], start=True, stop=True)
                    last.then_inc(s_filled, 1)

            def turn(s, p):
                pe.wait_ge(normed, PAIRS * s + p + 1)
                dst = ps_s[:, p, :, :].rearrange("q h k -> q (h k)")
                for hp in range(HP):
                    last = pe.transpose(dst[:, hp * P:(hp + 1) * P], s_sb[:, p, 2 * hp:2 * hp + 2, :], ident[:, :])
                last.then_inc(t_filled, 1)

            def mix(s, unit, j, first):
                p, e, c = j // (2 * KC), j // KC % 2, j % KC
                if j == 0:
                    pe.wait_ge(x_lo_done, 2 * (unit + 1))
                if c == 0:
                    pe.wait_ge(pT_twice, 2 * (PAIRS * s + p) + e + 1)
                    pe.wait_ge(pT_lo_done, 2 * (PAIRS * s + p) + e + 1)
                if first and j < 2:
                    pe.wait_ge(fold_lo, B_LOADS * 2)
                else:
                    pe.wait_ge(mix_lo_done, JOBS * s + j - 1)
                rows = slice(64 * e, 64 * e + 64)
                for b in range(2):
                    cols = slice(c * P, (c + 1) * P)
                    dst = ps_mix[:, j % 2, b * 256:(b + 1) * 256]
                    pe.matmul(dst, x_hl[:, e, 2 * p + b, cols], pT_hi[:, e, p, b, :, :], start=True, stop=False)
                    last = pe.matmul(dst, x_hl[rows, e, 2 * p + b, cols], pT_lo[rows, p, b, :, :],
                                     start=False, stop=True)
                last.then_inc(mix_filled, 1)

            def output(s, unit, half, j, first):
                p, e, c = j // (2 * KC), j // KC % 2, j % KC
                pe.wait_ge(mix_lo_done, JOBS * s + j + 1)
                if half == 0 and j % (2 * KC) == 0 and not first:
                    pe.wait_ge(right_added, PAIRS * (unit - 1) + p + 1)
                for hp in range(HP):
                    k = (HS * half + 2 * hp + e) * KC + c
                    start = half == 0 and j % (2 * KC) == 0 and hp == 0
                    stop = half == STEPS - 1 and j % (2 * KC) == 2 * KC - 1 and hp == HP - 1
                    pe.matmul(ps_out[:, p, :, :], mix_hi[:, j % RING, hp, :], wvo[:, k, :, :],
                              start=start, stop=False)
                    last = pe.matmul(ps_out[:, p, 0, :], mix_lo[:, j % RING, hp, :], wvo[:, k, 0, :],
                                     start=False, stop=stop)
                last.then_inc(proj_done, 1)

            def step(unit, half, first, last):
                s = unit * STEPS + half
                scores(s)
                ahead = not (last and half == STEPS - 1)
                nh = (half + 1) % STEPS

                def next_projection(hh):
                    if ahead:
                        if nh == 0 and hh == 0:
                            pe.wait_ge(xT_lo_done, unit + 2)
                        if first and half == 0 and hh == 0:
                            pe.wait_ge(w_lo, W_LOADS)
                        project(s + 1, nh, hh, False)

                for hh in range(HS):
                    next_projection(hh)
                    if hh == HS - 4:
                        turn(s, 0)
                    if hh == HS - 3:
                        turn(s, 1)
                    if hh >= HS - 2:
                        mix(s, unit, hh - HS + 2, first and half == 0)
                for j in range(2, JOBS + 2):
                    if j < JOBS:
                        mix(s, unit, j, first and half == 0)
                    if j >= 2:
                        output(s, unit, half, j - 2, first)

            def project(s, half, hh, first):
                if not (first and hh < 2):
                    pe.wait_ge(qk_copied, HS * s + hh - 1)
                h = HS * half + hh
                for i in range(2):
                    dst = ps_qk[:, hh % 2, i, :]
                    n = 0
                    for c in range(KC):
                        hi = wqk_hi[:, i, c, h * P:(h + 1) * P]
                        lo = wqk_lo[:, i, c, h * P:(h + 1) * P]
                        for w, v in ((hi, xT_hi), (hi, xT_lo), (lo, xT_hi)):
                            last = pe.matmul(dst, w, v[:, c, :], start=(n == 0), stop=(n == 3 * KC - 1))
                            n += 1
                last.then_inc(qk_filled, 1)

            for g in range(B_LOADS):
                pe.wait_ge(staged[g % 3], staged_count(g))
                w = stage[g % 3].rearrange("p (h w d) -> p h w d", h=2, w=2)
                for hh in range(2):
                    if g >= 1:
                        pe.wait_ge(fold_lo, 2 * g - 1 + hh)
                    for c in range(KC):
                        last = pe.matmul(ps_mix[:, hh, c * DIM:(c + 1) * DIM], w[:, hh, 0, c * P:(c + 1) * P],
                                         w[:, hh, 1, :], start=True, stop=True)
                    last.then_inc(fold_filled if hh else fold_first, 1)
            pe.wait_ge(consts, 12)
            pe.wait_ge(xT_lo_done, 1)
            pe.wait_ge(w_lo, W_LOADS // 2)
            for hh in range(HS):
                project(0, 0, hh, True)
            for half in range(STEPS):
                step(0, half, True, False)
            with pe.Fori(1, UNITS - 1) as u:
                for half in range(STEPS):
                    step(u, half, False, False)
            for half in range(STEPS):
                step(UNITS - 1, half, False, True)

        @block.scalar
        def _(act):
            def copy_qk(s, hh, first):
                act.wait_ge(qk_filled, HS * s + hh + 1)
                if not first and hh == 0:
                    act.wait_ge(s_filled, PAIRS * s)
                nc.scalar.activation(qk[:, hh, :, :], ps_qk[:, hh % 2, :, :], ACT.Copy).then_inc(qk_copied, 1)

            def exponent(s, p):
                act.wait_ge(shifted, PAIRS * s + p + 1)
                nc.scalar.activation(s_sb[:, p, :, :], s_sb[:, p, :, :], ACT.Exp, scale=SCALE).then_inc(exped, 1)

            def probs_hi(s, p, first):
                act.wait_ge(t_filled, PAIRS * s + p + 1)
                if not first and p == 0:
                    act.wait_ge(mix_filled, JOBS * s)
                for e in range(2):
                    rows = slice(64 * e, 64 * e + 64)
                    src = ps_s[rows, p, :, :].rearrange("k h q -> k (h q)").rearrange("k (h b q) -> k b h q", h=HP, b=2)
                    nc.scalar.activation(pT_hi[rows, e, p, :, :, :], src, ACT.Copy).then_inc(pT_hi_done, 1)

            def probs_hi_again(s, p, e):
                own, other = slice(64 * e, 64 * e + 64), slice(64 - 64 * e, 128 - 64 * e)
                act.wait_ge(pT_hi_done, 2 * (PAIRS * s + p) + e + 1)
                nc.scalar.activation(pT_hi[other, e, p, :, :, :], pT_hi[own, e, p, :, :, :].bitcast(F32), ACT.Copy) \
                    .then_inc(pT_twice, 1)

            def mixed_hi(s, j, first):
                act.wait_ge(mix_filled, JOBS * s + j + 1)
                if not (first and j < RING):
                    act.wait_ge(proj_done, JOBS * s + j - RING + 1)
                src = ps_mix[:, j % 2, :].rearrange("d (b h q) -> d h b q", b=2, h=HP)
                nc.scalar.activation(mix_hi[:, j % RING, :, :].rearrange("d h (b q) -> d h b q", b=2), src,
                                     ACT.Copy).then_inc(mix_hi_done, 1)

            def xT_split(u, first=False):
                act.wait_ge(xT_in, 16 * (u + 1))
                if not first:
                    act.wait_ge(qk_filled, HEADS * u)
                nc.scalar.activation(xT_hi[:, :, :], xT_raw[:, :, :], ACT.Copy).then_inc(xT_hi_done, 1)

            def x_split(u, e, first=False):
                act.wait_ge(xd_in, 32 * (u + 1))
                if not first:
                    act.wait_ge(mix_filled, STEPS * JOBS * u)
                rows = slice(64 * e, 64 * e + 64)
                nc.scalar.activation(x_hl[rows, e, :, :], x_raw[rows, :, :], ACT.Copy).then_inc(x_hi_done, 1)

            def step(u, half, first=False, last=False):
                s = u * STEPS + half
                first, ahead = first and half == 0, not (last and half == STEPS - 1)

                def nxt(*hs):
                    for hh in hs:
                        if ahead:
                            copy_qk(s + 1, hh, False)
                for hh in range(2):
                    if half == 0 and not first:
                        x_split(u, hh)
                    nxt(hh)
                exponent(s, 0)
                nxt(2)
                exponent(s, 1)
                nxt(3, 4)
                probs_hi(s, 0, first)
                probs_hi_again(s, 0, 0)
                nxt(5)
                probs_hi_again(s, 0, 1)
                probs_hi(s, 1, first)
                nxt(6)
                mixed_hi(s, 0, first)
                probs_hi_again(s, 1, 0)
                nxt(7)
                mixed_hi(s, 1, first)
                probs_hi_again(s, 1, 1)
                for j in range(2, JOBS):
                    mixed_hi(s, j, first)
                if half == 0 and not last:
                    xT_split(u + 1)

            def weights_hi(n):
                act.wait_ge(staged[(B_LOADS + n) % 3], staged_count(B_LOADS + n))
                i, c, cols = w_piece(n)
                nc.scalar.activation(wqk_hi[:, i, c, cols], stage[(B_LOADS + n) % 3], ACT.Copy).then_inc(w_hi, 1)

            for h in range(HEADS):
                act.wait_ge((fold_first, fold_filled)[h % 2], h // 2 + 1)
                src = ps_mix[:, h % 2, :].rearrange("p (c d) -> p c d", c=KC)
                nc.scalar.activation(wvo[:, h * KC:(h + 1) * KC, 0, :], src, ACT.Copy).then_inc(fold_hi, 1)
            xT_split(0, True)
            for n in range(W_LOADS // 2):
                weights_hi(n)
            for hh in range(HS):
                copy_qk(0, hh, True)
                if hh % 2:
                    weights_hi(W_LOADS // 2 + hh // 2)
            for e in range(2):
                x_split(0, e, True)
            for half in range(STEPS):
                step(0, half, first=True)
            with act.Fori(1, UNITS - 1) as u:
                for half in range(STEPS):
                    step(u, half)
            for half in range(STEPS):
                step(UNITS - 1, half, last=True)

        @block.vector
        def _(dve):
            mask_b = mask[:, :].unsqueeze(1).to_broadcast([P, HS, SEQ])

            def softmax_start(s, p):
                n = PAIRS * s + p + 1
                dve.wait_ge(s_filled, n)
                if not (isinstance(s, int) and s == 0):
                    dve.wait_ge(t_filled, n - PAIRS)
                dve.tensor_tensor(s_sb[:, p, :, :], ps_s[:, p, :, :], mask_b, ALU.add).then_inc(masked, 1)
                dve.wait_ge(masked, n)
                dve.tensor_reduce(row_max[:, p, :], s_sb[:, p, :, :], AX.X, ALU.max).then_inc(maxed, 1)
                dve.wait_ge(maxed, n)
                dve.tensor_tensor(s_sb[:, p, :, :], s_sb[:, p, :, :],
                                  row_max[:, p, :].unsqueeze(2).to_broadcast([P, HS, SEQ]),
                                  ALU.subtract).then_inc(shifted, 1)

            def softmax_end(s, p):
                n = PAIRS * s + p + 1
                dve.wait_ge(exped, n)
                dve.tensor_reduce(row_sum[:, p, :], s_sb[:, p, :, :], AX.X, ALU.add).then_inc(summed, 1)
                dve.wait_ge(summed, n)
                dve.reciprocal(inv_sum[:, p, :], row_sum[:, p, :]).then_inc(inverted, 1)
                dve.wait_ge(inverted, n)
                dve.tensor_tensor(s_sb[:, p, :, :], s_sb[:, p, :, :],
                                  inv_sum[:, p, :].unsqueeze(2).to_broadcast([P, HS, SEQ]),
                                  ALU.mult).then_inc(normed, 1)

            def probs_lo(s, p):
                for e in range(2):
                    rows = slice(64 * e, 64 * e + 64)
                    dve.wait_ge(pT_hi_done, 2 * (PAIRS * s + p) + e + 1)
                    src = ps_s[rows, p, :, :].rearrange("k h q -> k (h q)").rearrange("k (h b q) -> k b h q", h=HP, b=2)
                    dve.tensor_tensor(pT_lo[rows, p, :, :, :], src, pT_hi[rows, e, p, :, :, :].bitcast(F32),
                                      ALU.subtract).then_inc(pT_lo_done, 1)

            def mixed_lo(s, j):
                dve.wait_ge(mix_hi_done, JOBS * s + j + 1)
                src = ps_mix[:, j % 2, :].rearrange("d (b h q) -> d h b q", b=2, h=HP)
                hi = mix_hi[:, j % RING, :, :].rearrange("d h (b q) -> d h b q", b=2).bitcast(F32)
                lo = mix_lo[:, j % RING, :, :].rearrange("d h (b q) -> d h b q", b=2)
                dve.tensor_tensor(lo, src, hi, ALU.subtract).then_inc(mix_lo_done, 1)

            def residual(unit, p, first):
                n = PAIRS * unit + p + 1
                if p == 0:
                    dve.wait_ge(xr_in, 16 * (unit + 1))
                    dve.wait_ge(proj_done, STEPS * JOBS * (unit + 1))
                    if not first:
                        dve.wait_ge(stored, 16 * unit)
                dve.tensor_tensor(y[:, p, :], ps_out[:, p, 0, :], x_res[:, p, :], ALU.add).then_inc(left_added, 1)
                dve.wait_ge(left_added, n)
                dve.tensor_tensor(y[:, p, :], ps_out[:, p, 1, :], y[:, p, :], ALU.add).then_inc(right_added, 1)

            def moments(unit, p):
                n = PAIRS * unit + p + 1
                dve.wait_ge(right_added, n)
                dve.bn_stats(stats[:, p, :], y[:, p, :]).then_inc(stats_done, 1)
                dve.wait_ge(stats_done, n)
                dve.sem_inc(stats_seen, 1)
                dve.bn_aggr(mean_var[:, p, :], stats[:, p, :]).then_inc(moments_done, 1)
                dve.wait_ge(moments_done, n)
                dve.tensor_scalar(mean_var[:, p, 1:2], mean_var[:, p, 1:2], EPS, None, ALU.add).then_inc(var_done, 1)

            def normalise(unit, p):
                dve.wait_ge(rstd_done, PAIRS * unit + p + 1)
                dve.tensor_scalar(y[:, p, :], y[:, p, :], mean_var[:, p, 0:1], rstd[:, p, 0:1],
                                  ALU.subtract, ALU.mult).then_inc(y_done, 1)

            def step(unit, half, first):
                s = unit * STEPS + half
                softmax_start(s, 0)
                softmax_start(s, 1)
                softmax_end(s, 0)
                softmax_end(s, 1)
                behind = half == 0 and not first
                probs_lo(s, 0)
                mixed_lo(s, 0)
                if behind:
                    residual(unit - 1, 0, first=isinstance(unit, int) and unit == 1)
                mixed_lo(s, 1)
                probs_lo(s, 1)
                for j in range(2, JOBS):
                    mixed_lo(s, j)
                    if behind and j == 2:
                        residual(unit - 1, 1, first=False)
                    if behind and j in (3, 4):
                        moments(unit - 1, j - 3)
                    if behind and j in (5, 6):
                        normalise(unit - 1, j - 5)

            for h in range(HEADS):
                dve.wait_ge(fold_hi, h + 1)
                src = ps_mix[:, h % 2, :].rearrange("p (c d) -> p c d", c=KC)
                dve.tensor_tensor(wvo[:, h * KC:(h + 1) * KC, 1, :], src,
                                  wvo[:, h * KC:(h + 1) * KC, 0, :].bitcast(F32), ALU.subtract).then_inc(fold_lo, 1)
            for n in range(W_LOADS):
                dve.wait_ge(w_hi, n + 1)
                i, c, cols = w_piece(n)
                dve.tensor_tensor(wqk_lo[:, i, c, cols], stage[(B_LOADS + n) % 3], wqk_hi[:, i, c, cols].bitcast(F32),
                                  ALU.subtract).then_inc(w_lo, 1)
            dve.wait_ge(consts, 12)
            dve.wait_ge(w_lo, W_LOADS)
            for half in range(STEPS):
                step(0, half, True)
            with dve.Fori(1, UNITS) as u:
                for half in range(STEPS):
                    step(u, half, False)
            for p in range(PAIRS):
                residual(UNITS - 1, p, first=False)
                moments(UNITS - 1, p)
            for p in range(PAIRS):
                normalise(UNITS - 1, p)


def latent_attention(nc, x, kv, rope, Wq, w_kc_qT, W_qrT, W_krT, w_kc_kv, WoT, out):
    LATENT, Q_RANK = 64, 192
    QR = Q_RANK - P
    HALL = HEADS // 2

    with ExitStack() as ctx:
        def sb(name, shape, dt=F32):
            return ctx.enter_context(nc.sbuf_tensor("l_" + name, shape, dt))

        def sem(name):
            return ctx.enter_context(nc.semaphore("l_" + name))

        wq = sb("wq", [P, HEADS, DIM])
        kcq_a = sb("kcq_a", [P, HEADS, P])
        kcq_b = sb("kcq_b", [QR, HEADS, P])
        qrT = sb("qrT", [64, HEADS, Q_RANK])
        krT = sb("krT", [64, HEADS, LATENT])
        kckv = sb("kckv", [P, HEADS, LATENT])
        woT = sb("woT", [P, HEADS, DIM])
        r1_a = sb("r1_a", [P, HEADS, LATENT])
        r1_b = sb("r1_b", [QR, HEADS, LATENT])
        r2 = sb("r2", [P, HEADS, LATENT])
        wm_hi = sb("wm_hi", [P, KC, HALL, P], F32R)
        wm_lo = sb("wm_lo", [P, KC, HALL, P], F32R)
        wn = sb("wn", [P, HALL, 2, DIM], F32R)
        ident = sb("ident", [P, P])
        power = sb("power", [P, 1])
        tables = sb("tables", [P, 2, LATENT])
        x_nat = sb("x_nat", [P, PAIRS, DIM])
        x_res = sb("x_res", [P, PAIRS, DIM])
        xT_hi = sb("xT_hi", [P, PAIRS, KC, P], F32R)
        xT_lo = sb("xT_lo", [P, PAIRS, KC, P], F32R)
        kv_in = sb("kv_in", [P, UB, LATENT])
        kv_cos = sb("kv_cos", [P, UB, LATENT])
        kv_sin = sb("kv_sin", [P, UB, LATENT])
        kv2 = sb("kv2", [P, UB, P])
        kv2_kept = sb("kv2_kept", [P, UB, P])
        kv2_hi = sb("kv2_hi", [P, UB, P], F32R)
        kv2_lo = sb("kv2_lo", [P, UB, P], F32R)
        kv2T = sb("kv2T", [P, UB, P])
        qm = sb("qm", [P, HP, UNIT])
        s_sb = sb("s_sb", [P, STEPS, PAIRS, HS, SEQ])
        row_max = sb("row_max", [P, STEPS, PAIRS, HS])
        row_sum = sb("row_sum", [P, STEPS, PAIRS, HS])
        inv_sum = sb("inv_sum", [P, STEPS, PAIRS, HS])
        pT_hi = sb("pT_hi", [P, PAIRS, 2, HP, SEQ], F32R)
        pT_lo = sb("pT_lo", [P, PAIRS, 2, HP, SEQ], F32R)
        mix_hi = sb("mix_hi", [P, PAIRS, HP, P], F32R)
        mix_lo = sb("mix_lo", [P, PAIRS, HP, P], F32R)
        y = sb("y", [P, PAIRS, DIM])
        stats = sb("stats", [P, PAIRS, 6])
        mean_var = sb("mean_var", [P, PAIRS, 2])
        rstd = sb("rstd", [P, PAIRS, 1])

        banks = ctx.enter_context(nc.psum_tensor("l_banks", [P, 8, 512], F32))
        ps_s = banks[:, 0:2, :].rearrange("p n (h k) -> p n h k", k=SEQ)
        ps_front = banks[:, 2:4, :]
        ps_mix = banks[:, 4:6, :]
        ps_out = banks[:, 6:8, :].rearrange("p n (w d) -> p n w d", w=2)

        r1_in = sem("r1_in")
        kcq_in = sem("kcq_in")
        wq_in = sem("wq_in")
        wn_in = sem("wn_in")
        tables_in = sem("tables_in")
        x_in = sem("x_in")
        kv_in_done = sem("kv_in_done")
        xr_in = sem("xr_in")
        stored = sem("stored")
        r1_filled = sem("r1_filled")
        r1_copied = sem("r1_copied")
        r2_filled = sem("r2_filled")
        r2_copied = sem("r2_copied")
        wm_filled = sem("wm_filled")
        wm_hi_done = sem("wm_hi_done")
        wm_lo_done = sem("wm_lo_done")
        wn_filled = sem("wn_filled")
        wn_hi_done = sem("wn_hi_done")
        wn_lo_done = sem("wn_lo_done")
        consts = sem("consts")
        xT_filled = sem("xT_filled")
        xT_hi_done = sem("xT_hi_done")
        xT_lo_done = sem("xT_lo_done")
        cos_done = sem("cos_done")
        sin_done = sem("sin_done")
        rotated = sem("rotated")
        kvT_filled = sem("kvT_filled")
        kvT_copied = sem("kvT_copied")
        kv_kept = sem("kv_kept")
        kv_hi_done = sem("kv_hi_done")
        kv_lo_done = sem("kv_lo_done")
        qm_filled = sem("qm_filled")
        qm_copied = sem("qm_copied")
        s_filled = sem("s_filled")
        maxed = sem("maxed")
        shifted = sem("shifted")
        exped = sem("exped")
        summed = sem("summed")
        inverted = sem("inverted")
        normed = sem("normed")
        t_filled = sem("t_filled")
        pT_hi_done = sem("pT_hi_done")
        pT_lo_done = sem("pT_lo_done")
        mix_filled = sem("mix_filled")
        mix_hi_done = sem("mix_hi_done")
        mix_lo_done = sem("mix_lo_done")
        proj_done = sem("proj_done")
        left_added = sem("left_added")
        right_added = sem("right_added")
        stats_done = sem("stats_done")
        stats_seen = sem("stats_seen")
        moments_done = sem("moments_done")
        var_done = sem("var_done")
        rstd_done = sem("rstd_done")
        y_done = sem("y_done")

        block = ctx.enter_context(nc.Block())

        x_pairs = x.rearrange("(n p) d -> p n d", p=P)
        kv_batches = kv.rearrange("b t d -> t b d")
        out_pairs = out.rearrange("(n p) d -> p n d", p=P)

        @block.sync
        def _(sp):
            def load_x(u, first=False):
                if not first:
                    sp.wait_ge(xT_filled, u)
                sp.dma_start(x_nat[:, :, :], x_pairs[:, bass.ds(u * PAIRS, PAIRS), :]).then_inc(x_in, 16)

            def load_kv(u, first=False):
                if not first:
                    sp.wait_ge(cos_done, u)
                    sp.wait_ge(sin_done, u)
                for e in range(2):
                    sp.dma_start(kv_in[64 * e:64 * e + 64, :, :], kv_batches[:, bass.ds(u * UB, UB), :]) \
                        .then_inc(kv_in_done, 16)

            def load_xres(u, first=False):
                if not first:
                    sp.wait_ge(left_added, PAIRS * u)
                sp.dma_start(x_res[:, :, :], x_pairs[:, bass.ds(u * PAIRS, PAIRS), :]).then_inc(xr_in, 16)

            def store(u):
                sp.wait_ge(y_done, PAIRS * (u + 1))
                sp.dma_start(out_pairs[:, bass.ds(u * PAIRS, PAIRS), :], y[:, :, :]).then_inc(stored, 16)

            sp.dma_start(qrT[:, :, :], W_qrT.rearrange("h r q -> r h q")).then_inc(r1_in, 16)
            sp.dma_start(krT[:, :, :], W_krT.rearrange("h r d -> r h d")).then_inc(r1_in, 16)
            sp.dma_start(kcq_a[:, :, :], w_kc_qT[:, 0:P, :].rearrange("h q k -> q h k")).then_inc(kcq_in, 16)
            sp.dma_start(kcq_b[:, :, :], w_kc_qT[:, P:Q_RANK, :].rearrange("h q k -> q h k")).then_inc(kcq_in, 16)
            sp.dma_start(wq[:, :, :], Wq.rearrange("(h k) d -> k h d", k=P)).then_inc(wq_in, 16)
            sp.dma_start(kckv[:, :, :], w_kc_kv.rearrange("h k d -> k h d")).then_inc(wn_in, 16)
            sp.dma_start(woT[:, :, :], WoT.rearrange("(h k) d -> k h d", k=P)).then_inc(wn_in, 16)
            for e in range(2):
                sp.dma_start(tables[64 * e:64 * e + 64, :, :], rope.rearrange("w t d -> t w d")) \
                    .then_inc(tables_in, 16)
            load_x(0, True)
            load_kv(0, True)
            load_xres(0, True)
            for u in (1, 2):
                load_kv(u)
                load_x(u)
            with sp.Fori(2, UNITS - 1) as u:
                load_kv(u + 1)
                load_x(u + 1)
                store(u - 2)
                load_xres(u - 1)
            for u in (UNITS - 3, UNITS - 2):
                store(u)
                load_xres(u + 1)
            store(UNITS - 1)
            sp.wait_ge(stored, 16 * UNITS)

        @block.gpsimd
        def _(pool):
            def rotate(u, first=False):
                pool.wait_ge(kv_in_done, 32 * (u + 1))
                pool.tensor_tensor(kv_cos[:, :, :], kv_in[:, :, :],
                                   tables[:, 0, :].unsqueeze(1).to_broadcast([P, UB, LATENT]), ALU.mult) \
                    .then_inc(cos_done, 1)
                swapped = kv_in[:, :, :].rearrange("p b (w d) -> p b w d", w=2)
                sines = tables[:, 1, :].rearrange("p (w d) -> p w d", w=2)
                turned = kv_sin[:, :, :].rearrange("p b (w d) -> p b w d", w=2)
                for w in range(2):
                    last = pool.tensor_tensor(turned[:, :, w, :], swapped[:, :, 1 - w, :],
                                              sines[:, w, :].unsqueeze(1).to_broadcast([P, UB, LATENT // 2]), ALU.mult)
                last.then_inc(sin_done, 1)
                pool.wait_ge(cos_done, u + 1)
                pool.wait_ge(sin_done, u + 1)
                if not first:
                    pool.wait_ge(kvT_filled, u)
                    pool.wait_ge(kv_kept, u)
                for e in range(2):
                    rows, cols = slice(64 * e, 64 * e + 64), slice(64 * e, 64 * e + 64)
                    pool.tensor_tensor(kv2[rows, :, cols], kv_cos[rows, :, :], kv_sin[rows, :, :], ALU.add) \
                        .then_inc(rotated, 1)
                    pool.wait_ge(rotated, 2 * u + e + 1)

            def split_kv(u):
                pool.wait_ge(kv_hi_done, u + 1)
                pool.tensor_tensor(kv2_lo[:, :, :], kv2_kept[:, :, :], kv2_hi[:, :, :].bitcast(F32), ALU.subtract) \
                    .then_inc(kv_lo_done, 1)

            def normalise_probs(s, half):
                for p in range(PAIRS):
                    pool.wait_ge(inverted, PAIRS * s + p + 1)
                    pool.tensor_tensor(s_sb[:, half, p, :, :], s_sb[:, half, p, :, :],
                                       inv_sum[:, half, p, :].unsqueeze(2).to_broadcast([P, HS, SEQ]), ALU.mult) \
                        .then_inc(normed, 1)

            def inverse_deviation(u):
                for p in range(PAIRS):
                    pool.wait_ge(var_done, PAIRS * u + p + 1)
                    pool.tensor_tensor(rstd[:, p, :], mean_var[:, p, 1:2], power[:, :], ALU.pow).then_inc(rstd_done, 1)

            pool.memset(ident[:, :], 0.0).then_inc(consts, 1)
            pool.memset(power[:, :], -0.5).then_inc(consts, 1)
            pool.memset(kv2[:, :, :], 0.0).then_inc(consts, 1)
            pool.wait_ge(consts, 3)
            pool.affine_select(out=ident[:, :], in_=ident[:, :], compare_op=ALU.not_equal, fill=1.0,
                               base=0, pattern=[[-1, P]], channel_multiplier=1).then_inc(consts, 1)
            pool.wait_ge(tables_in, 32)
            rotate(0, True)
            rotate(1)
            normalise_probs(0, 0)
            split_kv(0)
            normalise_probs(1, 1)
            rotate(2)
            normalise_probs(STEPS, 0)
            split_kv(1)
            normalise_probs(STEPS + 1, 1)
            with pool.Fori(2, UNITS - 1) as u:
                rotate(u + 1)
                inverse_deviation(u - 2)
                normalise_probs(u * STEPS, 0)
                split_kv(u)
                normalise_probs(u * STEPS + 1, 1)
            inverse_deviation(UNITS - 3)
            normalise_probs((UNITS - 1) * STEPS, 0)
            split_kv(UNITS - 1)
            normalise_probs((UNITS - 1) * STEPS + 1, 1)
            inverse_deviation(UNITS - 2)
            inverse_deviation(UNITS - 1)

        @block.tensor
        def _(pe):
            def turn_inputs(u, first=False):
                pe.wait_ge(x_in, 16 * (u + 1))
                if not first:
                    pe.wait_ge(qm_copied, 4 * u - 1)
                for p in range(PAIRS):
                    for c in range(KC):
                        k = (p * KC + c) * P
                        last = pe.transpose(ps_front[:, 0, k:k + P], x_nat[:, p, c * P:(c + 1) * P], ident[:, :])
                last.then_inc(xT_filled, 1)
                pe.wait_ge(rotated, 2 * (u + 1))
                if not first:
                    pe.wait_ge(qm_copied, 4 * u)
                for b in range(UB):
                    last = pe.transpose(ps_front[:, 1, b * P:(b + 1) * P], kv2[:, b, :], ident[:, :])
                last.then_inc(kvT_filled, 1)

            def project(s, unit, half):
                for j in range(2):
                    if half == 0 and j == 0:
                        pe.wait_ge(xT_lo_done, unit + 1)
                    elif half == 0:
                        pe.wait_ge(kvT_copied, unit + 1)
                    else:
                        pe.wait_ge(qm_copied, 2 * s - 1 + j)
                    for i in range(2):
                        dst = ps_front[:, j, i * UNIT:(i + 1) * UNIT]
                        n = 0
                        for c in range(KC):
                            hi = wm_hi[:, c, half * HP + 2 * j + i, :]
                            lo = wm_lo[:, c, half * HP + 2 * j + i, :]
                            for w, v in ((hi, xT_hi), (hi, xT_lo), (lo, xT_hi)):
                                last = pe.matmul(dst, w, v[:, :, c, :], start=(n == 0), stop=(n == 3 * KC - 1))
                                n += 1
                    last.then_inc(qm_filled, 1)

            def scores(s, first=False):
                pe.wait_ge(qm_copied, 2 * (s + 1))
                for p in range(PAIRS):
                    if not first:
                        pe.wait_ge(shifted, PAIRS * (s - 1) + p + 1)
                    for hp in range(HP):
                        for b in range(2):
                            t = p * P + b * SEQ
                            last = pe.matmul(ps_s[b * SEQ:(b + 1) * SEQ, p, 2 * hp:2 * hp + 2, :], qm[:, hp, t:t + SEQ],
                                             kv2T[:, 2 * p + b, :], start=True, stop=True)
                    last.then_inc(s_filled, 1)

            def turn(s, half, first=False):
                for p in range(PAIRS):
                    pe.wait_ge(normed, PAIRS * s + p + 1)
                    if not first:
                        pe.wait_ge(mix_lo_done, PAIRS * (s - 1) + p + 1)
                    for hp in range(HP):
                        last = pe.transpose(ps_mix[:, p, hp * P:(hp + 1) * P],
                                            s_sb[:, half, p, 2 * hp:2 * hp + 2, :], ident[:, :])
                    last.then_inc(t_filled, 1)

            def mix(s, unit, half):
                if half == 0:
                    pe.wait_ge(kv_lo_done, unit + 1)
                for p in range(PAIRS):
                    pe.wait_ge(pT_lo_done, PAIRS * s + p + 1)
                    for b in range(2):
                        hi, lo = kv2_hi[:, 2 * p + b, :], kv2_lo[:, 2 * p + b, :]
                        for n, (w, v) in enumerate(((hi, pT_hi), (hi, pT_lo), (lo, pT_hi))):
                            last = pe.matmul(ps_mix[:, p, b * 256:(b + 1) * 256], w, v[:, p, b, :, :],
                                             start=(n == 0), stop=(n == 2))
                    last.then_inc(mix_filled, 1)

            def output(s, unit, half, first=False):
                for p in range(PAIRS):
                    pe.wait_ge(mix_lo_done, PAIRS * s + p + 1)
                    if half == 0 and not first:
                        pe.wait_ge(right_added, PAIRS * (unit - 1) + p + 1)
                    for hp in range(HP):
                        k = half * HP + hp
                        pe.matmul(ps_out[:, p, :, :], mix_hi[:, p, hp, :], wn[:, k, :, :], start=(k == 0), stop=False)
                        last = pe.matmul(ps_out[:, p, 0, :], mix_lo[:, p, hp, :], wn[:, k, 0, :],
                                         start=False, stop=(k == HALL - 1))
                    last.then_inc(proj_done, 1)

            pe.wait_ge(r1_in, 32)
            pe.wait_ge(consts, 4)
            for h in range(HEADS):
                at = slice(h % 8 * LATENT, (h % 8 + 1) * LATENT)
                pe.matmul(banks[:, h // 8, at], qrT[:, h, 0:P], krT[:, h, :], start=True, stop=True)
                last = pe.matmul(banks[0:QR, 2 + h // 8, at], qrT[:, h, P:Q_RANK], krT[:, h, :], start=True, stop=True)
            last.then_inc(r1_filled, 1)
            pe.wait_ge(r1_copied, 2)
            pe.wait_ge(kcq_in, 32)
            for h in range(HEADS):
                at = slice(h % 8 * LATENT, (h % 8 + 1) * LATENT)
                pe.matmul(banks[:, 4 + h // 8, at], kcq_a[:, h, :], r1_a[:, h, :], start=True, stop=False)
                last = pe.matmul(banks[:, 4 + h // 8, at], kcq_b[:, h, :], r1_b[:, h, :], start=False, stop=True)
            last.then_inc(r2_filled, 1)
            pe.wait_ge(r2_copied, 1)
            pe.wait_ge(wq_in, 16)
            for c in range(KC):
                for h in range(HEADS):
                    at = slice(h % 8 * LATENT, (h % 8 + 1) * LATENT)
                    last = pe.matmul(banks[:, 2 * c + h // 8, at], wq[:, h, c * P:(c + 1) * P], r2[:, h, :],
                                     start=True, stop=True)
            last.then_inc(wm_filled, 1)
            pe.wait_ge(wn_in, 32)
            for h in range(HEADS):
                rows = slice(h % 2 * 64, h % 2 * 64 + 64)
                last = pe.matmul(banks[rows, 4 + h // 4, h // 2 % 2 * DIM:(h // 2 % 2 + 1) * DIM], kckv[:, h, :],
                                 woT[:, h, :], start=True, stop=True)
            last.then_inc(wn_filled, 1)
            pe.wait_ge(wm_lo_done, 1)
            pe.wait_ge(wn_lo_done, 1)

            turn_inputs(0, True)
            project(0, 0, 0)
            def first_half(u, first=False):
                s = u * STEPS
                scores(s)
                turn(s - 1, 1)
                output(s - 2, u - 1, 0, first)
                project(s + 1, u, 1)
                mix(s - 1, u - 1, 1)

            def second_half(u, ahead=True):
                s = u * STEPS
                scores(s + 1)
                if ahead:
                    turn_inputs(u + 1)
                turn(s, 0)
                output(s - 1, u - 1, 1)
                if ahead:
                    project(s + 2, u + 1, 0)
                mix(s, u, 0)

            scores(0, True)
            project(1, 0, 1)
            scores(1)
            turn_inputs(1)
            turn(0, 0, True)
            project(2, 1, 0)
            mix(0, 0, 0)
            first_half(1, first=True)
            second_half(1)
            with pe.Fori(2, UNITS - 1) as u:
                first_half(u)
                second_half(u)
            first_half(UNITS - 1)
            second_half(UNITS - 1, ahead=False)
            turn(UNITS * STEPS - 1, 1)
            output(UNITS * STEPS - 2, UNITS - 1, 0)
            mix(UNITS * STEPS - 1, UNITS - 1, 1)
            output(UNITS * STEPS - 1, UNITS - 1, 1)

        @block.scalar
        def _(act):
            def inputs_hi(u):
                act.wait_ge(xT_filled, u + 1)
                nc.scalar.activation(xT_hi[:, :, :, :], ps_front[:, 0, :], ACT.Copy).then_inc(xT_hi_done, 1)
                act.wait_ge(kvT_filled, u + 1)
                nc.scalar.activation(kv2T[:, :, :], ps_front[:, 1, :], ACT.Copy).then_inc(kvT_copied, 1)

            def copy_qm(s):
                for j in range(2):
                    act.wait_ge(qm_filled, 2 * s + j + 1)
                    nc.scalar.activation(qm[:, 2 * j:2 * j + 2, :], ps_front[:, j, :], ACT.Copy).then_inc(qm_copied, 1)

            def exponent(s, half, p):
                act.wait_ge(shifted, PAIRS * s + p + 1)
                nc.scalar.activation(s_sb[:, half, p, :, :], s_sb[:, half, p, :, :], ACT.Exp).then_inc(exped, 1)

            def probs_hi(s, p):
                act.wait_ge(t_filled, PAIRS * s + p + 1)
                src = ps_mix[:, p, :].rearrange("k (h b q) -> k b h q", h=HP, b=2)
                nc.scalar.activation(pT_hi[:, p, :, :, :], src, ACT.Copy).then_inc(pT_hi_done, 1)

            def mixed_hi(s, first=False):
                for p in range(PAIRS):
                    act.wait_ge(mix_filled, PAIRS * s + p + 1)
                    if not first:
                        act.wait_ge(proj_done, PAIRS * (s - 1) + p + 1)
                    src = ps_mix[:, p, :].rearrange("d (b h q) -> d h b q", b=2, h=HP)
                    nc.scalar.activation(mix_hi[:, p, :, :].rearrange("d h (b q) -> d h b q", b=2), src, ACT.Copy) \
                        .then_inc(mix_hi_done, 1)

            def keep_kv(u, first=False):
                act.wait_ge(rotated, 2 * (u + 1))
                if not first:
                    act.wait_ge(kv_lo_done, u)
                nc.scalar.activation(kv2_kept[:, :, :], kv2[:, :, :], ACT.Copy).then_inc(kv_kept, 1)

            def kv_split(u, first=False):
                act.wait_ge(kv_kept, u + 1)
                if not first:
                    act.wait_ge(mix_filled, STEPS * PAIRS * u)
                nc.scalar.activation(kv2_hi[:, :, :], kv2_kept[:, :, :], ACT.Copy).then_inc(kv_hi_done, 1)

            act.wait_ge(r1_filled, 1)
            nc.scalar.activation(r1_a[:, :, :], banks[:, 0:2, :], ACT.Copy).then_inc(r1_copied, 1)
            nc.scalar.activation(r1_b[:, :, :], banks[0:QR, 2:4, :], ACT.Copy).then_inc(r1_copied, 1)
            act.wait_ge(r2_filled, 1)
            nc.scalar.activation(r2[:, :, :], banks[:, 4:6, :], ACT.Copy).then_inc(r2_copied, 1)
            act.wait_ge(wm_filled, 1)
            nc.scalar.activation(wm_hi[:, :, :, :], banks[:, 0:4, :], ACT.Copy).then_inc(wm_hi_done, 1)
            act.wait_ge(wn_filled, 1)
            nc.scalar.activation(wn[:, :, 0, :], banks[:, 4:8, :].rearrange("p n (k d) -> p (n k) d", k=2),
                                 ACT.Copy).then_inc(wn_hi_done, 1)

            def first_half(u):
                s = u * STEPS
                mixed_hi(s - 2, isinstance(u, int) and u == 1)
                for p in range(PAIRS):
                    probs_hi(s - 1, p)
                    exponent(s, 0, p)
                copy_qm(s + 1)

            def second_half(u, ahead=True):
                s = u * STEPS
                mixed_hi(s - 1)
                kv_split(u)
                if ahead:
                    inputs_hi(u + 1)
                for p in range(PAIRS):
                    probs_hi(s, p)
                    exponent(s + 1, 1, p)
                if ahead:
                    keep_kv(u + 1)
                    copy_qm(s + 2)

            keep_kv(0, True)
            kv_split(0, True)
            inputs_hi(0)
            copy_qm(0)
            for p in range(PAIRS):
                exponent(0, 0, p)
            copy_qm(1)
            inputs_hi(1)
            for p in range(PAIRS):
                probs_hi(0, p)
                exponent(1, 1, p)
            keep_kv(1)
            copy_qm(2)
            first_half(1)
            second_half(1)
            with act.Fori(2, UNITS - 1) as u:
                first_half(u)
                second_half(u)
            first_half(UNITS - 1)
            second_half(UNITS - 1, ahead=False)
            mixed_hi(UNITS * STEPS - 2)
            for p in range(PAIRS):
                probs_hi(UNITS * STEPS - 1, p)
            mixed_hi(UNITS * STEPS - 1)

        @block.vector
        def _(dve):
            def inputs_lo(u):
                dve.wait_ge(xT_hi_done, u + 1)
                dve.tensor_tensor(xT_lo[:, :, :, :], ps_front[:, 0, :].rearrange("p (n c t) -> p n c t", n=PAIRS, c=KC),
                                  xT_hi[:, :, :, :].bitcast(F32), ALU.subtract).then_inc(xT_lo_done, 1)

            def softmax_start(s, half, pairs=range(PAIRS)):
                for p in pairs:
                    n = PAIRS * s + p + 1
                    dve.wait_ge(s_filled, n)
                    dve.tensor_reduce(row_max[:, half, p, :], ps_s[:, p, :, :], AX.X, ALU.max).then_inc(maxed, 1)
                    dve.wait_ge(maxed, n)
                    if not (isinstance(s, int) and s < STEPS):
                        dve.wait_ge(t_filled, n - STEPS * PAIRS)
                    dve.tensor_tensor(s_sb[:, half, p, :, :], ps_s[:, p, :, :],
                                      row_max[:, half, p, :].unsqueeze(2).to_broadcast([P, HS, SEQ]),
                                      ALU.subtract).then_inc(shifted, 1)

            def softmax_sum(s, half):
                for p in range(PAIRS):
                    n = PAIRS * s + p + 1
                    dve.wait_ge(exped, n)
                    dve.tensor_reduce(row_sum[:, half, p, :], s_sb[:, half, p, :, :], AX.X, ALU.add) \
                        .then_inc(summed, 1)
                    dve.wait_ge(summed, n)
                    dve.reciprocal(inv_sum[:, half, p, :], row_sum[:, half, p, :]).then_inc(inverted, 1)

            def probs_lo(s):
                for p in range(PAIRS):
                    dve.wait_ge(pT_hi_done, PAIRS * s + p + 1)
                    src = ps_mix[:, p, :].rearrange("k (h b q) -> k b h q", h=HP, b=2)
                    dve.tensor_tensor(pT_lo[:, p, :, :, :], src, pT_hi[:, p, :, :, :].bitcast(F32), ALU.subtract) \
                        .then_inc(pT_lo_done, 1)

            def mixed_lo(s):
                for p in range(PAIRS):
                    dve.wait_ge(mix_hi_done, PAIRS * s + p + 1)
                    src = ps_mix[:, p, :].rearrange("d (b h q) -> d h b q", b=2, h=HP)
                    hi = mix_hi[:, p, :, :].rearrange("d h (b q) -> d h b q", b=2).bitcast(F32)
                    dve.tensor_tensor(mix_lo[:, p, :, :].rearrange("d h (b q) -> d h b q", b=2), src, hi,
                                      ALU.subtract).then_inc(mix_lo_done, 1)

            def residual(unit, first=False):
                dve.wait_ge(xr_in, 16 * (unit + 1))
                dve.wait_ge(proj_done, STEPS * PAIRS * (unit + 1))
                if not first:
                    dve.wait_ge(stored, 16 * unit)
                for p in range(PAIRS):
                    dve.tensor_tensor(y[:, p, :], ps_out[:, p, 0, :], x_res[:, p, :], ALU.add).then_inc(left_added, 1)
                for p in range(PAIRS):
                    dve.wait_ge(left_added, PAIRS * unit + p + 1)
                    dve.tensor_tensor(y[:, p, :], ps_out[:, p, 1, :], y[:, p, :], ALU.add).then_inc(right_added, 1)
                for p in range(PAIRS):
                    n = PAIRS * unit + p + 1
                    dve.wait_ge(right_added, n)
                    dve.bn_stats(stats[:, p, :], y[:, p, :]).then_inc(stats_done, 1)
                    dve.wait_ge(stats_done, n)
                    dve.sem_inc(stats_seen, 1)
                    dve.bn_aggr(mean_var[:, p, :], stats[:, p, :]).then_inc(moments_done, 1)
                    dve.wait_ge(moments_done, n)
                    dve.tensor_scalar(mean_var[:, p, 1:2], mean_var[:, p, 1:2], EPS, None, ALU.add) \
                        .then_inc(var_done, 1)

            def normalise(unit):
                for p in range(PAIRS):
                    dve.wait_ge(rstd_done, PAIRS * unit + p + 1)
                    dve.tensor_scalar(y[:, p, :], y[:, p, :], mean_var[:, p, 0:1], rstd[:, p, 0:1],
                                      ALU.subtract, ALU.mult).then_inc(y_done, 1)

            dve.wait_ge(wm_hi_done, 1)
            dve.tensor_tensor(wm_lo[:, :, :, :].rearrange("p c n k -> p (c n k)"),
                              banks[:, 0:4, :].rearrange("p n k -> p (n k)"),
                              wm_hi[:, :, :, :].rearrange("p c n k -> p (c n k)").bitcast(F32), ALU.subtract) \
                .then_inc(wm_lo_done, 1)
            dve.wait_ge(wn_hi_done, 1)
            dve.tensor_tensor(wn[:, :, 1, :], banks[:, 4:8, :].rearrange("p n (k d) -> p (n k) d", k=2),
                              wn[:, :, 0, :].bitcast(F32), ALU.subtract).then_inc(wn_lo_done, 1)

            def first_half(u):
                s = u * STEPS
                mixed_lo(s - 2)
                softmax_start(s, 0)
                probs_lo(s - 1)
                softmax_sum(s, 0)
                if not (isinstance(u, int) and u == 1):
                    normalise(u - 2)

            def second_half(u, ahead=True):
                s = u * STEPS
                mixed_lo(s - 1)
                softmax_start(s + 1, 1, [0])
                if ahead:
                    inputs_lo(u + 1)
                softmax_start(s + 1, 1, [1])
                probs_lo(s)
                softmax_sum(s + 1, 1)
                residual(u - 1, isinstance(u, int) and u == 1)

            inputs_lo(0)
            softmax_start(0, 0)
            softmax_sum(0, 0)
            softmax_start(1, 1, [0])
            inputs_lo(1)
            softmax_start(1, 1, [1])
            probs_lo(0)
            softmax_sum(1, 1)
            first_half(1)
            second_half(1)
            with dve.Fori(2, UNITS - 1) as u:
                first_half(u)
                second_half(u)
            first_half(UNITS - 1)
            second_half(UNITS - 1, ahead=False)
            mixed_lo(UNITS * STEPS - 2)
            probs_lo(UNITS * STEPS - 1)
            normalise(UNITS - 2)
            mixed_lo(UNITS * STEPS - 1)
            residual(UNITS - 1)
            normalise(UNITS - 1)


def mixture(nc, x, gateT, gate_b, W1T, W3T, W2T, Ws1T, Ws3T, Ws2T, slots, slots_out, out):
    E, INNER, CAP = 16, 176, 128
    TILES = TOKENS // P
    REST = INNER - P
    W13 = KC * 2 * INNER
    WALL = W13 + 2 * DIM
    FEEDS = TILES + E
    RING = 8
    FAR = float(1 << 20)
    LOW = -1e30

    with ExitStack() as ctx:
        def sb(name, shape, dt=F32):
            return ctx.enter_context(nc.sbuf_tensor("m_" + name, shape, dt))

        def ps(name):
            return ctx.enter_context(nc.psum_tensor("m_" + name, [P, 2, 512], F32))

        def sem(name):
            return ctx.enter_context(nc.semaphore("m_" + name))

        x_all = sb("x_all", [P, TILES, DIM])
        y_all = sb("y_all", [P, TILES, DIM])
        w_raw = sb("w_raw", [P, 2, WALL])
        w_sh = sb("w_sh", [P, 2, WALL], F32R)
        w_ex = sb("w_ex", [P, 4, 2, WALL], F32R)
        gate_raw = sb("gate_raw", [P, KC, E])
        gate = sb("gate", [P, KC, 2, E], F32R)
        bias = sb("bias", [P, E])
        ident = sb("ident", [P, P])
        before = sb("before", [P, P])
        ones = sb("ones", [P, P])
        zeros = sb("zeros", [P, DIM])
        rank = sb("rank", [P, E])
        go_on = sb("go_on", [P, E, TILES])
        power = sb("power", [P, 4])
        x_in = sb("x_in", [P, 2, DIM])
        xT_hi = sb("xT_hi", [P, 2, KC, P], F32R)
        xT_lo = sb("xT_lo", [P, 2, KC, P], F32R)
        act_g = sb("act_g", [P, 2, INNER])
        h = sb("h", [P, 2, 2 * P])
        hT_hi = sb("hT_hi", [P, 2, 2, P], F32R)
        hT_lo = sb("hT_lo", [P, 2, 2, P], F32R)
        y_slot = sb("y_slot", [P, 2, DIM])
        logit = sb("logit", [P, TILES, E])
        t1 = sb("t1", [P, TILES, E])
        t2 = sb("t2", [P, TILES, E])
        t3 = sb("t3", [P, TILES, E])
        t4 = sb("t4", [P, TILES, E])
        t5 = sb("t5", [P, TILES, E])
        score = sb("score", [P, TILES, E])
        pick = sb("pick", [P, TILES, E])
        chosen = sb("chosen", [P, 2, TILES, E])
        top = sb("top", [P, 2, TILES])
        place = sb("place", [P, 2, TILES])
        raw_w = sb("raw_w", [P, 2, TILES])
        total = sb("total", [P, TILES])
        weight = sb("weight", [P, 2, TILES])
        pos = sb("pos", [P, 2, TILES])
        valid = sb("valid", [P, 2, TILES])
        slot = sb("slot", [P, 2, TILES])
        target = sb("target", [P, 2, TILES])
        counts = sb("counts", [P, E, TILES])
        running = sb("running", [P, E, TILES])
        send_at = sb("send_at", [P, 2, TILES], mybir.dt.uint32)
        fetch_at = sb("fetch_at", [P, 2, TILES], mybir.dt.uint32)
        fetched = sb("fetched", [P, RING, DIM])
        stats = sb("stats", [P, 4, 6])
        mean_var = sb("mean_var", [P, 2, 4, 2])
        rstd = sb("rstd", [P, 2, 4])

        ps_x, ps_g, ps_h, ps_y = ps("ps_x"), ps("ps_g"), ps("ps_h"), ps("ps_y")
        ps_logit = ps_y[:, :, :].rearrange("p n (t w e) -> p (n t) w e", w=2, e=E)

        gate_in = sem("gate_in")
        all_in = sem("all_in")
        cleared = sem("cleared")
        x_landed = [sem(f"x_landed{n}") for n in range(2)]
        w_landed = [sem(f"w_landed{n}") for n in range(2)]
        sent = sem("sent")
        slots_stored = [sem(f"slots_stored{n}") for n in range(2)]
        fetched_in = [sem(f"fetched_in{n}") for n in range(RING)]
        stored = sem("stored")
        consts = sem("consts")
        gate_split = sem("gate_split")
        w_hi_done = sem("w_hi_done")
        w_lo_done = sem("w_lo_done")
        x_filled = sem("x_filled")
        xT_hi_done = sem("xT_hi_done")
        xT_lo_done = sem("xT_lo_done")
        logits_filled = sem("logits_filled")
        left_logits = sem("left_logits")
        logits_read = sem("logits_read")
        chosen_done = sem("chosen_done")
        counts_read = sem("counts_read")
        targets_done = sem("targets_done")
        route_act = sem("route_act")
        route = sem("route")
        softplus_part = sem("softplus_part")
        counted = sem("counted")
        g_filled = sem("g_filled")
        g_acted = sem("g_acted")
        h_done = sem("h_done")
        hT_filled = sem("hT_filled")
        hT_hi_done = sem("hT_hi_done")
        hT_lo_done = sem("hT_lo_done")
        y_filled = sem("y_filled")
        shared_left = sem("shared_left")
        y_left = sem("y_left")
        y_right = sem("y_right")
        weighed = sem("weighed")
        stats_done = sem("stats_done")
        stats_seen = sem("stats_seen")
        moments_done = sem("moments_done")
        var_done = sem("var_done")
        rstd_done = sem("rstd_done")
        y_done = sem("y_done")


        block = ctx.enter_context(nc.Block())

        x_tiles = x.rearrange("(n p) d -> p n d", p=P)
        out_tiles = out.rearrange("(n p) d -> p n d", p=P)
        slot_tiles = slots.rearrange("(n p) d -> p n d", p=P)
        slot_out_tiles = slots_out.rearrange("(n p) d -> p n d", p=P)
        PARTS = 4
        PART = TILES // PARTS
        GROUP = 4

        def weight_parts(n, w1, w3, w2):
            w13 = w_raw[:, n, 0:W13].rearrange("p (c w i) -> p c w i", c=KC, w=2)
            return ((w13[:, :, 0, :], w1.rearrange("(c p) i -> p c i", p=P)),
                    (w13[:, :, 1, :], w3.rearrange("(c p) i -> p c i", p=P)),
                    (w_raw[:, n, W13:W13 + DIM], w2[0:P, :]),
                    (w_raw[0:REST, n, W13 + DIM:WALL], w2[P:INNER, :]))

        @block.sync
        def _(sp):
            def load_x(n, i, src, first=False):
                if not first:
                    sp.wait_ge(x_filled, n - 1)
                sp.dma_start(x_in[:, i, :], src).then_inc(x_landed[i], 16)

            def load_weights(e, i):
                if not (isinstance(e, int) and e == 0):
                    sp.wait_ge(w_lo_done, e)
                for dst, src in weight_parts(1 - i, W1T[e], W3T[e], W2T[e]):
                    sp.dma_start(dst, src).then_inc(w_landed[1 - i], 16)

            sp.dma_start(gate_raw[:, :, :], gateT.rearrange("(c p) e -> p c e", p=P)).then_inc(gate_in, 16)
            sp.dma_start(bias[:, :], gate_b.rearrange("(a e) -> a e", a=1).to_broadcast([P, E])).then_inc(gate_in, 16)
            for i in range(2):
                load_x(i, i, x_tiles[:, i, :], True)
            with sp.Fori(1, TILES // 2) as u:
                for i in range(2):
                    load_x(2 * u + i, i, x_tiles[:, 2 * u + i, :])
            for i in range(2):
                load_x(TILES + i, i, x_tiles[:, i, :])
            sp.wait_ge(consts, 7)
            for dst, src in weight_parts(0, Ws1T, Ws3T, Ws2T):
                sp.dma_start(dst, src).then_inc(w_landed[0], 16)
            for k in range(PARTS):
                part = slice(k * PART, (k + 1) * PART)
                sp.dma_start(x_all[:, part, :], x_tiles[:, part, :]).then_inc(all_in, 16)
            sp.dma_start(slot_tiles, zeros[:, :].unsqueeze(1).to_broadcast([P, E, DIM])).then_inc(cleared, 16)
            load_weights(0, 0)
            load_weights(1, 1)
            with sp.Fori(1, TILES // 2) as u:
                for i in range(2):
                    load_x(TILES + 2 * u + i, i, x_tiles[:, 2 * u + i, :])
            for e in range(2, 4):
                load_weights(e, e % 2)
            sp.wait_ge(sent, 16 * 2 * TILES)
            for e in range(3):
                load_x(2 * TILES + e, e % 2, slot_tiles[:, e, :])
            with sp.Fori(1, E // 2 - 1) as u:
                for i in (1, 2):
                    load_x(2 * TILES + 2 * u + i, i % 2, slot_tiles[:, 2 * u + i, :])
                    load_weights(2 * u + i + 1, (i + 1) % 2)
            load_x(2 * TILES + E - 1, 1, slot_tiles[:, E - 1, :])
            with sp.Fori(0, TILES // GROUP) as g:
                sp.wait_ge(y_done, GROUP * g + GROUP)
                sp.dma_start(out_tiles[:, bass.ds(GROUP * g, GROUP), :], y_all[:, bass.ds(GROUP * g, GROUP), :]) \
                    .then_inc(stored, 16)
            sp.wait_ge(stored, 16 * TILES // GROUP)

        @block.gpsimd
        def _(pool):
            pool.memset(ident[:, :], 0.0).then_inc(consts, 1)
            pool.memset(zeros[:, :], 0.0).then_inc(consts, 1)
            pool.memset(ones[:, :], 1.0).then_inc(consts, 1)
            pool.memset(w_raw[:, :, :], 0.0).then_inc(consts, 1)
            pool.memset(h[:, :, :], 0.0).then_inc(consts, 1)
            pool.memset(go_on[:, :, :], 1.0).then_inc(consts, 1)
            pool.memset(power[:, :], -0.5).then_inc(consts, 1)
            pool.wait_ge(consts, 7)
            pool.affine_select(out=ident[:, :], in_=ident[:, :], compare_op=ALU.not_equal, fill=1.0,
                               base=0, pattern=[[-1, P]], channel_multiplier=1).then_inc(consts, 1)
            pool.affine_select(out=before[:, :], in_=ones[:, :], compare_op=ALU.is_ge, fill=0.0,
                               base=-1, pattern=[[1, P]], channel_multiplier=-1).then_inc(consts, 1)
            pool.memset(go_on[:, :, 0:1], 0.0).then_inc(consts, 1)
            for e in range(E):
                pool.memset(rank[:, e:e + 1], float(E - e)).then_inc(consts, 1)

            pool.wait_ge(targets_done, 2)
            pool.wait_ge(cleared, 16)
            pool.wait_ge(all_in, 16 * PARTS)
            for t in range(TILES):
                for k in range(2):
                    pool.indirect_dma_start(
                        out=slots[:, :], out_offset=bass.IndirectOffsetOnAxis(ap=send_at[:, k, t:t + 1], axis=0),
                        in_=x_all[:, t, :], in_offset=None, bounds_check=E * CAP - 1, oob_is_err=False) \
                        .then_inc(sent, 16)

            def inverse_deviation(g):
                pool.wait_ge(var_done, g + 1)
                pool.tensor_tensor(rstd[:, g % 2, :], mean_var[:, g % 2, :, 1], power[:, :], ALU.pow) \
                    .then_inc(rstd_done, 1)

            for i in range(2):
                pool.wait_ge(slots_stored[i], 16 * E // 2)
            for g in range(TILES // GROUP):
                for k in range(2):
                    for i in range(GROUP):
                        r = k * GROUP + i
                        if g >= 1:
                            pool.wait_ge(weighed, RING * (g - 1) + r + 1)
                        pool.indirect_dma_start(
                            out=fetched[:, r, :], out_offset=None, in_=slots_out[:, :],
                            in_offset=bass.IndirectOffsetOnAxis(
                                ap=fetch_at[:, k, GROUP * g + i:GROUP * g + i + 1], axis=0)) \
                            .then_inc(fetched_in[r], 16)
                if g >= 1:
                    inverse_deviation(g - 1)
            inverse_deviation(TILES // GROUP - 1)

        @block.tensor
        def _(pe):
            def turn(n, g, k, first=False):
                i = k % 2
                pe.wait_ge(x_landed[i], 16 * (g + k // 2 + 1))
                if not first:
                    pe.wait_ge(xT_lo_done, n - 1)
                for c in range(KC):
                    last = pe.transpose(ps_x[:, i, c * P:(c + 1) * P], x_in[:, i, c * P:(c + 1) * P], ident[:, :])
                last.then_inc(x_filled, 1)

            def logits(n, i):
                pe.wait_ge(xT_lo_done, n + 1)
                for c in range(KC):
                    pe.matmul(ps_logit[:, n, :, :], xT_hi[:, i, c, :], gate[:, c, :, :], start=(c == 0), stop=False)
                    last = pe.matmul(ps_logit[:, n, 0, :], xT_lo[:, i, c, :], gate[:, c, 0, :],
                                     start=False, stop=(c == KC - 1))
                last.then_inc(logits_filled, 1)

            def up(m, k, expert, first=False):
                i = k % 2
                pe.wait_ge(xT_lo_done, TILES + m + 1)
                if expert:
                    pe.wait_ge(w_lo_done, m - TILES + 2)
                if not first:
                    pe.wait_ge(h_done, m - 1)
                w = w_ex[:, k % 4, :, :] if expert else w_sh
                dst = ps_g[:, i, 0:2 * INNER]
                n = 0
                for c in range(KC):
                    cols = slice(c * 2 * INNER, (c + 1) * 2 * INNER)
                    for v, part in ((xT_hi, 0), (xT_hi, 1), (xT_lo, 0)):
                        last = pe.matmul(dst, v[:, i, c, :], w[:, part, cols], start=(n == 0), stop=(n == 3 * KC - 1))
                        n += 1
                last.then_inc(g_filled, 1)

            def turn_inner(m, k, first=False):
                i = k % 2
                pe.wait_ge(h_done, m + 1)
                if not first:
                    pe.wait_ge(hT_lo_done, m - 1)
                for c in range(2):
                    last = pe.transpose(ps_h[:, i, c * P:(c + 1) * P], h[:, i, c * P:(c + 1) * P], ident[:, :])
                last.then_inc(hT_filled, 1)

            def down(m, k, expert, first=False):
                i = k % 2
                pe.wait_ge(hT_lo_done, m + 1)
                if first:
                    pe.wait_ge(logits_read, 1)
                else:
                    pe.wait_ge(y_right, m - 1)
                w = w_ex[:, k % 4, :, :] if expert else w_sh
                for c, rows in enumerate((P, REST)):
                    cols = slice(W13 + c * DIM, W13 + (c + 1) * DIM)
                    pe.matmul(ps_y[:, i, :], hT_hi[0:rows, i, c, :], w[0:rows, :, cols], start=(c == 0), stop=False)
                    last = pe.matmul(ps_y[:, i, 0:DIM], hT_lo[0:rows, i, c, :], w[0:rows, 0, cols],
                                     start=False, stop=(c == 1))
                last.then_inc(y_filled, 1)

            def feed_group(g, expert, first=False, last=False):
                for k in range(GROUP):
                    m = GROUP * g + k
                    if not (last and k == GROUP - 1):
                        turn(TILES + m + 1, TILES // 2 + 2 * g, k + 1)
                    up(m, k, expert, first and k < 2)
                    if not (first and k == 0):
                        turn_inner(m - 1, k + 3, first and k < 3)
                    if not (first and k < 2):
                        down(m - 2, k + 2, expert and not (first_expert(g) and k < 2), first and k < 4)

            def first_expert(g):
                return isinstance(g, int) and g == TILES // GROUP

            pe.wait_ge(consts, 10 + E)
            pe.wait_ge(gate_split, 2)
            turn(0, 0, 0, True)
            for i in range(2):
                turn(i + 1, 0, i + 1, i == 0)
                logits(i, i)
            with pe.Fori(1, TILES // 2) as u:
                for i in range(2):
                    turn(2 * u + i + 1, u, i + 1)
                    logits(2 * u + i, i)
            pe.wait_ge(chosen_done, 1)
            for n, lhs in enumerate((before, ones)):
                last = pe.matmul(ps_g[:, n, :], lhs[:, :], pick[:, :, :], start=True, stop=True)
            last.then_inc(counted, 1)
            pe.wait_ge(w_lo_done, 1)
            pe.wait_ge(counts_read, 2)
            feed_group(0, False, first=True)
            with pe.Fori(1, TILES // GROUP) as g:
                feed_group(g, False)
            feed_group(TILES // GROUP, True)
            with pe.Fori(TILES // GROUP + 1, FEEDS // GROUP - 1) as g:
                feed_group(g, True)
            feed_group(FEEDS // GROUP - 1, True, last=True)
            turn_inner(FEEDS - 1, 3)
            down(FEEDS - 2, 2, True)
            down(FEEDS - 1, 3, True)

        @block.scalar
        def _(act):
            def x_hi(n, k, routed_before, first=False):
                i = k % 2
                act.wait_ge(x_filled, n + 1)
                if not first:
                    if routed_before:
                        act.wait_ge(logits_filled, n - 1)
                    else:
                        act.wait_ge(g_filled, n - TILES - 1)
                nc.scalar.activation(xT_hi[:, i, :, :], ps_x[:, i, 0:DIM], ACT.Copy).then_inc(xT_hi_done, 1)

            def split_weights(n, i, dst, e, first=False):
                act.wait_ge(w_landed[i], n)
                if e is not None and not first:
                    act.wait_ge(y_filled, TILES + e - 3)
                nc.scalar.activation(dst, w_raw[:, i, :], ACT.Copy).then_inc(w_hi_done, 1)

            def g_act(m, k, first=False):
                i = k % 2
                act.wait_ge(g_filled, m + 1)
                if not first:
                    act.wait_ge(h_done, m - 1)
                nc.scalar.activation(act_g[:, i, :], ps_g[:, i, 0:INNER], ACT.Silu).then_inc(g_acted, 1)

            def h_hi(m, k, first=False):
                i = k % 2
                act.wait_ge(hT_filled, m + 1)
                if not first:
                    act.wait_ge(y_filled, m - 1)
                nc.scalar.activation(hT_hi[:, i, :, :], ps_h[:, i, 0:2 * P], ACT.Copy).then_inc(hT_hi_done, 1)

            def y_copy(m, k, first=False):
                i = k % 2
                act.wait_ge(y_filled, m + 1)
                if not first:
                    act.wait_ge(slots_stored[i], 8 * (m - TILES - i))
                nc.scalar.activation(y_slot[:, i, :], ps_y[:, i, 0:DIM], ACT.Copy).then_inc(y_left, 1)

            def store_expert(m, k):
                act.wait_ge(y_right, m + 1)
                act.dma_start(slot_out_tiles[:, m - TILES, :], y_slot[:, k % 2, :]).then_inc(slots_stored[k % 2], 16)

            def feed_group(g, expert, first=False, last=False):
                at = isinstance(g, int)
                for k in range(GROUP):
                    m = GROUP * g + k
                    if not (last and k == GROUP - 1):
                        x_hi(TILES + m + 1, k + 1, first and k == 0)
                    g_act(m, k, first and k < 2)
                    if not (first and k == 0):
                        h_hi(m - 1, k + 3, first and k < 3)
                    if expert:
                        boundary = at and g == TILES // GROUP
                        if not (boundary and k < 3):
                            store_expert(m - 3, k + 1)
                        if not (boundary and k < 2):
                            y_copy(m - 2, k + 2, boundary)
                        if not (last and k >= 2):
                            split_weights(32 * (m - TILES + 3 - (k + 1) % 2) + 64, (k + 1) % 2,
                                          w_ex[:, (k + 2) % 4, 0, :], m - TILES + 2, boundary and k < 2)

            act.wait_ge(gate_in, 32)
            nc.scalar.activation(gate[:, :, 0, :], gate_raw[:, :, :], ACT.Copy).then_inc(gate_split, 1)
            for n in range(2):
                x_hi(n, n, True, True)
            with act.Fori(1, TILES // 2) as u:
                for i in range(2):
                    x_hi(2 * u + i, i, True)
            act.wait_ge(logits_filled, TILES)
            nc.scalar.activation(logit[:, :, :], ps_logit[:, :, 0, :], ACT.Copy).then_inc(left_logits, 1)
            split_weights(64, 0, w_sh[:, 0, :], None)
            x_hi(TILES, 0, True)
            act.wait_ge(route, 1)
            nc.scalar.activation(t1[:, :, :], logit[:, :, :], ACT.Abs).then_inc(route_act, 1)
            act.wait_ge(route_act, 1)
            nc.scalar.activation(t2[:, :, :], t1[:, :, :], ACT.Exp, scale=-1.0).then_inc(route_act, 1)
            act.wait_ge(route, 2)
            nc.scalar.activation(t4[:, :, :], t3[:, :, :], ACT.Ln).then_inc(route_act, 1)
            split_weights(64, 1, w_ex[:, 0, 0, :], 0, True)
            act.wait_ge(route, 8)
            nc.scalar.activation(score[:, :, :], t5[:, :, :], ACT.Sqrt).then_inc(route_act, 1)
            split_weights(128, 0, w_ex[:, 1, 0, :], 1, True)
            feed_group(0, False, first=True)
            with act.Fori(1, TILES // GROUP) as g:
                feed_group(g, False)
            feed_group(TILES // GROUP, True)
            with act.Fori(TILES // GROUP + 1, FEEDS // GROUP - 1) as g:
                feed_group(g, True)
            feed_group(FEEDS // GROUP - 1, True, last=True)
            h_hi(FEEDS - 1, 3)
            store_expert(FEEDS - 3, 1)
            y_copy(FEEDS - 2, 2)
            store_expert(FEEDS - 2, 2)
            y_copy(FEEDS - 1, 3)
            store_expert(FEEDS - 1, 3)

        @block.vector
        def _(dve):
            def x_lo(n, k):
                i = k % 2
                dve.wait_ge(xT_hi_done, n + 1)
                dve.tensor_tensor(xT_lo[:, i, :, :], ps_x[:, i, 0:DIM].rearrange("p (c t) -> p c t", c=KC),
                                  xT_hi[:, i, :, :].bitcast(F32), ALU.subtract).then_inc(xT_lo_done, 1)

            def weights_lo(n, i, w):
                dve.wait_ge(w_hi_done, n)
                dve.tensor_tensor(w[:, 1, :], w_raw[:, i, :], w[:, 0, :].bitcast(F32), ALU.subtract) \
                    .then_inc(w_lo_done, 1)

            def gated(m, k, first=False):
                i = k % 2
                dve.wait_ge(g_acted, m + 1)
                if not first:
                    dve.wait_ge(hT_filled, m - 1)
                dve.tensor_tensor(h[:, i, 0:INNER], ps_g[:, i, INNER:2 * INNER], act_g[:, i, :], ALU.mult) \
                    .then_inc(h_done, 1)

            def h_lo(m, k):
                i = k % 2
                dve.wait_ge(hT_hi_done, m + 1)
                dve.tensor_tensor(hT_lo[:, i, :, :], ps_h[:, i, 0:2 * P].rearrange("p (c t) -> p c t", c=2),
                                  hT_hi[:, i, :, :].bitcast(F32), ALU.subtract).then_inc(hT_lo_done, 1)

            def add_shared(m, k):
                i = k % 2
                dve.wait_ge(y_filled, m + 1)
                dve.tensor_tensor(y_all[:, m, :], ps_y[:, i, 0:DIM], x_all[:, m, :], ALU.add).then_inc(shared_left, 1)
                dve.wait_ge(shared_left, m + 1)
                dve.tensor_tensor(y_all[:, m, :], ps_y[:, i, DIM:2 * DIM], y_all[:, m, :], ALU.add) \
                    .then_inc(y_right, 1)

            def add_expert(m, k):
                i = k % 2
                dve.wait_ge(y_left, m - TILES + 1)
                dve.tensor_tensor(y_slot[:, i, :], ps_y[:, i, DIM:2 * DIM], y_slot[:, i, :], ALU.add) \
                    .then_inc(y_right, 1)

            def feed_group(g, expert, first=False, last=False):
                boundary = isinstance(g, int) and g == TILES // GROUP
                for k in range(GROUP):
                    m = GROUP * g + k
                    if not (last and k == GROUP - 1):
                        x_lo(TILES + m + 1, k + 1)
                    gated(m, k, first and k < 2)
                    if not (first and k == 0):
                        h_lo(m - 1, k + 3)
                    if not (first and k < 2):
                        if expert and not (boundary and k < 2):
                            add_expert(m - 2, k + 2)
                        else:
                            add_shared(m - 2, k + 2)
                    if expert and not (last and k >= 2):
                        weights_lo(m - TILES + 4, (k + 1) % 2, w_ex[:, (k + 2) % 4, :, :])

            dve.wait_ge(gate_split, 1)
            dve.tensor_tensor(gate[:, :, 1, :], gate_raw[:, :, :], gate[:, :, 0, :].bitcast(F32), ALU.subtract) \
                .then_inc(gate_split, 1)
            with dve.Fori(0, TILES // 2) as u:
                for i in range(2):
                    x_lo(2 * u + i, i)

            done = 0

            def then(instruction):
                nonlocal done
                done += 1
                instruction.then_inc(route, 1)
                dve.wait_ge(route, done)

            def experts(v):
                return v.unsqueeze(2).to_broadcast([P, TILES, E])

            def tiles(v):
                return v.unsqueeze(1).to_broadcast([P, TILES, E])

            dve.wait_ge(left_logits, 1)
            dve.wait_ge(consts, 10 + E)
            then(dve.tensor_tensor(logit[:, :, :], ps_logit[:, :, 1, :], logit[:, :, :], ALU.add))
            dve.sem_inc(logits_read, 1)
            weights_lo(1, 0, w_sh)
            x_lo(TILES, 0)
            dve.wait_ge(route_act, 2)
            then(dve.tensor_scalar(t3[:, :, :], t2[:, :, :], 1.0, None, ALU.add))
            then(dve.tensor_scalar(t5[:, :, :], t3[:, :, :], -1.0, 0.0, ALU.add, ALU.is_equal))
            then(dve.scalar_tensor_tensor(t1[:, :, :], t3[:, :, :], -1.0, t5[:, :, :], ALU.add, ALU.add))
            then(dve.reciprocal(t1[:, :, :], t1[:, :, :]))
            dve.wait_ge(route_act, 3)
            then(dve.tensor_tensor(t4[:, :, :], t4[:, :, :], t1[:, :, :], ALU.mult))
            then(dve.tensor_tensor(t4[:, :, :], t4[:, :, :], t5[:, :, :], ALU.add))
            dve.tensor_tensor(t4[:, :, :], t4[:, :, :], t2[:, :, :], ALU.mult).then_inc(softplus_part, 1)
            dve.wait_ge(softplus_part, 1)
            then(dve.scalar_tensor_tensor(t5[:, :, :], logit[:, :, :], 0.0, t4[:, :, :], ALU.max, ALU.add))
            weights_lo(2, 1, w_ex[:, 0, :, :])
            dve.wait_ge(route_act, 4)
            then(dve.tensor_tensor(pick[:, :, :], score[:, :, :], tiles(bias[:, :]), ALU.add))
            for k in range(2):
                then(dve.tensor_reduce(top[:, k, :], pick[:, :, :], AX.X, ALU.max))
                then(dve.tensor_tensor(t1[:, :, :], pick[:, :, :], experts(top[:, k, :]), ALU.is_equal))
                then(dve.tensor_tensor(t1[:, :, :], t1[:, :, :], tiles(rank[:, :]), ALU.mult))
                then(dve.tensor_reduce(place[:, k, :], t1[:, :, :], AX.X, ALU.max))
                then(dve.tensor_tensor(chosen[:, k, :, :], tiles(rank[:, :]), experts(place[:, k, :]), ALU.is_equal))
                if k == 0:
                    then(dve.scalar_tensor_tensor(pick[:, :, :], chosen[:, k, :, :], LOW, pick[:, :, :],
                                                  ALU.mult, ALU.add))
            then(dve.tensor_tensor(pick[:, :, :], chosen[:, 0, :, :], chosen[:, 1, :, :], ALU.add))
            dve.sem_inc(chosen_done, 1)
            for k in range(2):
                then(dve.tensor_tensor(t1[:, :, :], score[:, :, :], chosen[:, k, :, :], ALU.mult))
                then(dve.tensor_reduce(raw_w[:, k, :], t1[:, :, :], AX.X, ALU.add))
            then(dve.tensor_tensor(total[:, :], raw_w[:, 0, :], raw_w[:, 1, :], ALU.add))
            then(dve.reciprocal(total[:, :], total[:, :]))
            dve.wait_ge(counted, 1)
            dve.tensor_copy(counts[:, :, :].rearrange("p e t -> p t e"),
                            ps_g[:, 1, :].rearrange("p (t e) -> p t e", e=E)).then_inc(counts_read, 1)
            dve.wait_ge(counts_read, 1)
            then(dve.tensor_tensor_scan(running[:, :, :].rearrange("p e t -> p (e t)"),
                                        go_on[:, :, :].rearrange("p e t -> p (e t)"),
                                        counts[:, :, :].rearrange("p e t -> p (e t)"), 0.0, ALU.mult, ALU.add))
            then(dve.tensor_tensor(running[:, :, :], running[:, :, :], counts[:, :, :], ALU.subtract))
            dve.tensor_tensor(t2[:, :, :], ps_g[:, 0, :].rearrange("p (t e) -> p t e", e=E),
                              running[:, :, :].rearrange("p e t -> p t e"), ALU.add).then_inc(counts_read, 1)
            dve.wait_ge(counts_read, 2)
            for k in range(2):
                then(dve.tensor_tensor(t1[:, :, :], t2[:, :, :], chosen[:, k, :, :], ALU.mult))
                then(dve.tensor_reduce(pos[:, k, :], t1[:, :, :], AX.X, ALU.add))
            then(dve.tensor_scalar(valid[:, :, :], pos[:, :, :], float(CAP), None, ALU.is_lt))
            for k in range(2):
                then(dve.tensor_tensor(weight[:, k, :], raw_w[:, k, :], total[:, :], ALU.mult))
            then(dve.tensor_tensor(weight[:, :, :], weight[:, :, :], valid[:, :, :], ALU.mult))
            then(dve.tensor_tensor(pos[:, :, :], pos[:, :, :], valid[:, :, :], ALU.mult))
            then(dve.tensor_scalar(slot[:, :, :], place[:, :, :], -float(CAP), float(E * CAP), ALU.mult, ALU.add))
            then(dve.tensor_tensor(slot[:, :, :], slot[:, :, :], pos[:, :, :], ALU.add))
            then(dve.tensor_scalar(target[:, :, :], valid[:, :, :], -FAR, FAR, ALU.mult, ALU.add))
            then(dve.tensor_tensor(target[:, :, :], target[:, :, :], slot[:, :, :], ALU.add))
            dve.tensor_copy(send_at[:, :, :], target[:, :, :]).then_inc(targets_done, 1)
            dve.tensor_copy(fetch_at[:, :, :], slot[:, :, :]).then_inc(targets_done, 1)

            weights_lo(3, 0, w_ex[:, 1, :, :])
            dve.wait_ge(all_in, 16 * PARTS)
            feed_group(0, False, first=True)
            with dve.Fori(1, TILES // GROUP) as g:
                feed_group(g, False)
            feed_group(TILES // GROUP, True)
            with dve.Fori(TILES // GROUP + 1, FEEDS // GROUP - 1) as g:
                feed_group(g, True)
            feed_group(FEEDS // GROUP - 1, True, last=True)
            h_lo(FEEDS - 1, 3)
            add_expert(FEEDS - 2, 2)
            add_expert(FEEDS - 1, 3)

            def combine(g, parity):
                for k in range(2):
                    for i in range(GROUP):
                        r, t = k * GROUP + i, GROUP * g + i
                        dve.wait_ge(fetched_in[r], 16 * (g + 1))
                        if k == 1:
                            dve.wait_ge(weighed, RING * g + i + 1)
                        dve.scalar_tensor_tensor(y_all[:, t, :], fetched[:, r, :], weight[:, k, bass.ds(t, 1)],
                                                 y_all[:, t, :], ALU.mult, ALU.add).then_inc(weighed, 1)
                dve.wait_ge(weighed, RING * (g + 1))
                dve.sem_inc(stats_seen, 1)
                for i in range(GROUP):
                    dve.bn_stats(stats[:, i, :], y_all[:, GROUP * g + i, :]).then_inc(stats_done, 1)
                dve.wait_ge(stats_done, GROUP * (g + 1))
                dve.sem_inc(stats_seen, 1)
                for i in range(GROUP):
                    last = dve.bn_aggr(mean_var[:, parity, i, :], stats[:, i, :])
                last.then_inc(moments_done, 1)
                dve.wait_ge(moments_done, g + 1)
                dve.tensor_scalar(mean_var[:, parity, :, 1], mean_var[:, parity, :, 1], EPS, None, ALU.add) \
                    .then_inc(var_done, 1)

            def normalise(g, parity):
                dve.wait_ge(rstd_done, g + 1)
                for i in range(GROUP):
                    t = GROUP * g + i
                    dve.tensor_scalar(y_all[:, t, :], y_all[:, t, :], mean_var[:, parity, i, 0:1],
                                      rstd[:, parity, i:i + 1], ALU.subtract, ALU.mult).then_inc(y_done, 1)

            combine(0, 0)
            with dve.Fori(0, TILES // GROUP // 2 - 1) as v:
                for i in range(2):
                    combine(2 * v + i + 1, (i + 1) % 2)
                    normalise(2 * v + i, i)
            combine(TILES // GROUP - 1, 1)
            normalise(TILES // GROUP - 2, 0)
            normalise(TILES // GROUP - 1, 1)


def decoder_layer(nc, a, out):
    def scratch(name, rows):
        return nc.dram_tensor(name, [rows, DIM], F32).ap()

    x1, x2 = scratch("x1", TOKENS), scratch("x2", TOKENS)
    slots, slots_out = scratch("slots", 16 * 128), scratch("slots_out", 16 * 128)
    local_attention(nc, a["x"], a["xT"], a["attn_Wq"], a["attn_Wk"], a["attn_WvT"], a["attn_Wo"], x1)
    latent_attention(nc, x1, a["ctx"], a["rope"], a["xattn_Wq"], a["xattn_w_kc_qT"], a["xattn_W_qrT"],
                     a["xattn_W_krT"], a["xattn_w_kc_kv"], a["xattn_WoT"], x2)
    mixture(nc, x2, a["gate_wT"], a["gate_b"], a["W1T"], a["W3T"], a["W2T"], a["Ws1T"], a["Ws3T"], a["Ws2T"],
            slots, slots_out, out)



def rope_tables():
    import numpy as np
    steps = np.arange(0, 64, 2, dtype=np.float32) / np.float32(64)
    inv_freq = (np.float32(1.0) / np.float32(10000.0) ** steps).astype(np.float32)
    freqs = np.arange(SEQ, dtype=np.float32)[:, None] * inv_freq[None, :]
    cos, sin = np.repeat(np.cos(freqs), 2, axis=-1), np.repeat(np.sin(freqs), 2, axis=-1)
    sin[:, :32] = -sin[:, :32]
    return np.stack([cos, sin]).astype(np.float32)


def kernel(x, ctx_512, L0_attn_Wq, L0_attn_Wk, L0_attn_Wv, L0_attn_Wo, L0_xattn_Wq, L0_xattn_w_kc_q,
           L0_xattn_w_kc_kv, L0_xattn_W_qr, L0_xattn_W_kr, L0_xattn_Wo, L0_ffn_input_ids, L0_ffn_gate_w,
           L0_ffn_gate_b, L0_ffn_W1, L0_ffn_W3, L0_ffn_W2, L0_ffn_Ws1, L0_ffn_Ws3, L0_ffn_Ws2):
    import numpy as np
    import concourse.bacc as bacc
    from concourse.bass_utils import run_bass_kernel_spmd

    def turned(a):
        a = np.asarray(a)
        return np.ascontiguousarray(np.swapaxes(a, -1, -2))

    rows = np.ascontiguousarray(np.asarray(x).reshape(TOKENS, DIM))
    arrays = {
        "x": rows, "xT": turned(rows), "ctx": np.ascontiguousarray(ctx_512), "rope": rope_tables(),
        "attn_Wq": np.ascontiguousarray(L0_attn_Wq), "attn_Wk": np.ascontiguousarray(L0_attn_Wk),
        "attn_WvT": turned(L0_attn_Wv), "attn_Wo": np.ascontiguousarray(L0_attn_Wo),
        "xattn_Wq": np.ascontiguousarray(L0_xattn_Wq), "xattn_w_kc_qT": turned(L0_xattn_w_kc_q),
        "xattn_W_qrT": turned(L0_xattn_W_qr), "xattn_W_krT": turned(L0_xattn_W_kr),
        "xattn_w_kc_kv": np.ascontiguousarray(L0_xattn_w_kc_kv), "xattn_WoT": turned(L0_xattn_Wo),
        "gate_wT": turned(L0_ffn_gate_w), "gate_b": np.ascontiguousarray(L0_ffn_gate_b),
        "W1T": turned(L0_ffn_W1), "W3T": turned(L0_ffn_W3), "W2T": turned(L0_ffn_W2),
        "Ws1T": turned(L0_ffn_Ws1), "Ws3T": turned(L0_ffn_Ws3), "Ws2T": turned(L0_ffn_Ws2),
    }
    nc = bacc.Bacc("TRN2", target_bir_lowering=False, num_devices=1)
    aps = {n: nc.dram_tensor(n, a.shape, mybir.dt.from_np(a.dtype), kind="ExternalInput").ap()
           for n, a in arrays.items()}
    out = nc.dram_tensor("out", [TOKENS, DIM], F32, kind="ExternalOutput").ap()
    decoder_layer(nc, aps, out)
    result = run_bass_kernel_spmd(nc, [arrays], core_ids=[0])
    return result.results[0]["out"].reshape(BATCH, SEQ, DIM)
```

```python
from contextlib import ExitStack

import concourse.bass as bass
from concourse import mybir

F32 = mybir.dt.float32
F32R = mybir.dt.float32r
ALU = mybir.AluOpType
ACT = mybir.ActivationFunctionType
AX = mybir.AxisListType

P = 128
BATCH, SEQ, DIM = 64, 64, 256
TOKENS = BATCH * SEQ
HEADS, HEAD_DIM = 16, 128
WINDOW, GLOBAL = 64, 16
KC = DIM // P
UNIT = 256
UNITS = TOKENS // UNIT
PAIRS = UNIT // P
UB = UNIT // SEQ
HS = 8
STEPS = HEADS // HS
HP = HS // 2
EPS = 1e-5
MASKED = -1e30


CARRIED = 5120


LATENT, Q_RANK = 64, 192
QR = Q_RANK - P

def first_weights(carried):
    cut = HEADS * Q_RANK
    return (carried[0:64, 0:cut].rearrange("p (h q) -> p h q", h=HEADS),
            carried[0:64, cut:cut + HEADS * LATENT].rearrange("p (h d) -> p h d", h=HEADS))


def first_fold(carried, rows_ahead):
    return (rows_ahead.rearrange("p (h d) -> p h d", h=HEADS),
            carried[0:QR, CARRIED - HEADS * LATENT:CARRIED].rearrange("p (h d) -> p h d", h=HEADS))


def local_attention(nc, x, xT, Wq, Wk, WvT, Wo, W_qrT_next, W_krT_next, carried, rows_ahead, out):
    SCALE = float(HEAD_DIM) ** -0.5
    STAGE = 1024
    W_LOADS = 2 * KC * 2048 // STAGE
    B_LOADS = HEADS // 2
    RING = 4
    JOBS = PAIRS * 2 * KC

    with ExitStack() as ctx:
        def sb(name, shape, dt=F32):
            return ctx.enter_context(nc.sbuf_tensor("a_" + name, shape, dt))

        def ps(name, shape):
            return ctx.enter_context(nc.psum_tensor("a_" + name, shape, F32))

        def sem(name):
            return ctx.enter_context(nc.semaphore("a_" + name))

        stage_own = rows_ahead
        wqk_hi = sb("wqk_hi", [P, 2, KC, 2048], F32R)
        wqk_lo = sb("wqk_lo", [P, 2, KC, 2048], F32R)
        wvo = sb("wvo", [P, HEADS * KC, 2, DIM], F32R)
        ident = sb("ident", [P, P])
        mask = sb("mask", [P, SEQ])
        y_and_res = sb("y_and_res", [P, 2, PAIRS, DIM])
        y, x_res = y_and_res[:, 0, :, :], y_and_res[:, 1, :, :]
        x_raw = carried[:, HS * 2 * UNIT:CARRIED].rearrange("p (b d) -> p b d", b=UB)
        x_hl = sb("x_hl", [P, 2, UB, DIM], F32R)
        xT_raw = sb("xT_raw", [P, KC, UNIT])
        xT_hi = sb("xT_hi", [P, KC, UNIT], F32R)
        xT_lo = sb("xT_lo", [P, KC, UNIT], F32R)
        qk = carried[:, 0:HS * 2 * UNIT].rearrange("p (h i t) -> p h i t", h=HS, i=2)
        s_sb = sb("s_sb", [P, PAIRS, HS, SEQ])
        row_max = sb("row_max", [P, PAIRS, HS])
        row_sum = sb("row_sum", [P, PAIRS, HS])
        inv_sum = sb("inv_sum", [P, PAIRS, HS])
        pT_hi = sb("pT_hi", [P, 2, PAIRS, 2, HP, SEQ], F32R)
        pT_lo = sb("pT_lo", [P, PAIRS, 2, HP, SEQ], F32R)
        mix_hi = sb("mix_hi", [P, RING, HP, P], F32R)
        mix_lo = sb("mix_lo", [P, RING, HP, P], F32R)
        stats = sb("stats", [P, PAIRS, 6])
        mean_var = sb("mean_var", [P, PAIRS, 2])
        rstd = sb("rstd", [P, PAIRS, 1])
        power = sb("power", [P, 1])

        stage = (stage_own[:, :], s_sb[:, :, :, :].rearrange("p n h k -> p (n h k)"),
                 y_and_res[:, :, :, :].rearrange("p w n d -> p (w n d)"))
        first_pieces = qk[:, :, :, :].rearrange("p h i t -> p (h i t)").rearrange("p (n k) -> p n k", k=STAGE)

        ps_s = ps("ps_s", [P, PAIRS, HS, SEQ])
        ps_qk = ps("ps_qk", [P, 2, 2, UNIT])
        r1_bank_b = ps_qk[0:QR, :, :, :].rearrange("p n i t -> p n (i t)")
        ps_mix = ps("ps_mix", [P, 2, 512])
        ps_out = ps("ps_out", [P, PAIRS, 2, DIM])

        pieces_in = sem("pieces_in")
        staged = [sem(f"staged{n}") for n in range(3)]
        xT_in = sem("xT_in")
        xd_in = sem("xd_in")
        xr_in = sem("xr_in")
        stored = sem("stored")
        next_in = sem("next_in")
        r1_filled = sem("r1_filled")
        w_hi = sem("w_hi")
        w_lo = sem("w_lo")
        fold_filled = sem("fold_filled")
        fold_hi = sem("fold_hi")
        fold_lo = sem("fold_lo")
        consts = sem("consts")
        xT_hi_done = sem("xT_hi_done")
        xT_lo_done = sem("xT_lo_done")
        x_hi_done = sem("x_hi_done")
        x_lo_done = sem("x_lo_done")
        qk_filled = sem("qk_filled")
        qk_copied = sem("qk_copied")
        s_filled = sem("s_filled")
        masked = sem("masked")
        maxed = sem("maxed")
        shifted = sem("shifted")
        exped = sem("exped")
        summed = sem("summed")
        inverted = sem("inverted")
        normed = sem("normed")
        t_filled = sem("t_filled")
        pT_hi_done = sem("pT_hi_done")
        pT_twice = sem("pT_twice")
        pT_lo_done = sem("pT_lo_done")
        mix_filled = sem("mix_filled")
        mix_hi_done = sem("mix_hi_done")
        mix_lo_done = sem("mix_lo_done")
        proj_done = sem("proj_done")
        left_added = sem("left_added")
        right_added = sem("right_added")
        stats_done = sem("stats_done")
        stats_seen = sem("stats_seen")
        moments_done = sem("moments_done")
        var_done = sem("var_done")
        rstd_done = sem("rstd_done")
        y_done = sem("y_done")

        def staged_count(n):
            return sum(32 if m < B_LOADS else 16 for m in range(n % 3, n + 1, 3))

        def w_source(n):
            if n < W_LOADS // 2:
                return first_pieces[:, n, :], (pieces_in, 16 * W_LOADS // 2)
            m = B_LOADS + n - W_LOADS // 2
            return stage[m % 3], (staged[m % 3], staged_count(m))

        def fold_bank(h):
            return ps_mix[:, h % 2, :] if h % 4 < 2 else ps_out[:, h % 2, :, :].rearrange("p w d -> p (w d)")

        def w_piece(n):
            half, i, c = n // 4, n // 2 % 2, n % 2
            return i, c, slice(half * STAGE, (half + 1) * STAGE)

        block = ctx.enter_context(nc.Block())

        xT_v = xT.rearrange("(c p) t -> p c t", p=P)
        x_pairs = x.rearrange("(n p) d -> p n d", p=P)
        x_batches = x.rearrange("(b t) d -> t b d", t=SEQ)
        out_pairs = out.rearrange("(n p) d -> p n d", p=P)
        WvT_v = WvT.rearrange("(h k) d -> k h d", k=P)
        Wo_v = Wo.rearrange("(h k) d -> k h d", k=P)

        @block.sync
        def _(sp):
            def load_xT(u):
                if not (isinstance(u, int) and u == 0):
                    sp.wait_ge(xT_lo_done, u)
                sp.dma_start(xT_raw[:, :, :], xT_v[:, :, bass.ds(u * UNIT, UNIT)]).then_inc(xT_in, 16)

            def load_xd(u):
                if not (isinstance(u, int) and u == 0):
                    sp.wait_ge(x_lo_done, 2 * u)
                for e in range(2):
                    sp.dma_start(x_raw[64 * e:64 * e + 64, :, :], x_batches[:, bass.ds(u * UB, UB), :]) \
                        .then_inc(xd_in, 16)

            def load_xres(u):
                if not (isinstance(u, int) and u == 0):
                    sp.wait_ge(left_added, PAIRS * u)
                sp.dma_start(x_res[:, :, :], x_pairs[:, bass.ds(u * PAIRS, PAIRS), :]).then_inc(xr_in, 16)

            def store(u):
                sp.wait_ge(y_done, PAIRS * (u + 1))
                sp.dma_start(out_pairs[:, bass.ds(u * PAIRS, PAIRS), :], y[:, :, :]).then_inc(stored, 16)

            for n in range(B_LOADS):
                if n >= 3:
                    sp.wait_ge(fold_filled, 2 * (n - 2))
                dst = stage[n % 3].rearrange("p (h w d) -> p h w d", h=2, w=2)
                sp.dma_start(dst[:, :, 0, :], WvT_v[:, 2 * n:2 * n + 2, :]).then_inc(staged[n % 3], 16)
                sp.dma_start(dst[:, :, 1, :], Wo_v[:, 2 * n:2 * n + 2, :]).then_inc(staged[n % 3], 16)
                if n == 2:
                    for piece in range(W_LOADS // 2):
                        i, c, cols = w_piece(piece)
                        sp.dma_start(first_pieces[:, piece, :], (Wq, Wk)[i][c * P:(c + 1) * P, cols]) \
                            .then_inc(pieces_in, 16)
                    load_xT(0)
            for piece in range(W_LOADS // 2, W_LOADS):
                n = B_LOADS + piece - W_LOADS // 2
                if n - 3 < B_LOADS:
                    sp.wait_ge(fold_filled, 2 * (n - 2))
                else:
                    sp.wait_ge(w_lo, piece - 2)
                i, c, cols = w_piece(piece)
                sp.dma_start(stage[n % 3], (Wq, Wk)[i][c * P:(c + 1) * P, cols]).then_inc(staged[n % 3], 16)
            load_xd(0)
            sp.wait_ge(w_lo, W_LOADS)
            load_xres(0)
            load_xT(1)
            load_xd(1)
            with sp.Fori(1, UNITS - 1) as u:
                load_xT(u + 1)
                store(u - 1)
                load_xres(u)
                load_xd(u + 1)
            store(UNITS - 2)
            load_xres(UNITS - 1)
            sp.wait_ge(s_filled, PAIRS * STEPS * UNITS)
            qrT, krT = first_weights(carried)
            sp.dma_start(qrT, W_qrT_next.rearrange("h r q -> r h q")).then_inc(next_in, 16)
            sp.dma_start(krT, W_krT_next.rearrange("h r d -> r h d")).then_inc(next_in, 16)
            store(UNITS - 1)
            sp.wait_ge(stored, 16 * UNITS)

        @block.gpsimd
        def _(pool):
            pool.memset(ident[:, :], 0.0).then_inc(consts, 1)
            pool.memset(power[:, :], -0.5).then_inc(consts, 1)
            pool.memset(mask[:, :], 0.0).then_inc(consts, 1)
            pool.wait_ge(consts, 3)
            pool.affine_select(out=ident[:, :], in_=ident[:, :], compare_op=ALU.not_equal, fill=1.0,
                               base=0, pattern=[[-1, P]], channel_multiplier=1).then_inc(consts, 1)
            n = 4
            for b in range(2):
                half = mask[b * SEQ:(b + 1) * SEQ, :]
                for sign in (1, -1):
                    pool.affine_select(out=half, in_=half, compare_op=ALU.is_ge, fill=MASKED,
                                       base=WINDOW // 2 - 1, pattern=[[sign, SEQ]],
                                       channel_multiplier=-sign).then_inc(consts, 1)
                    n += 1
                    pool.wait_ge(consts, n)
                pool.memset(mask[b * SEQ:(b + 1) * SEQ, 0:GLOBAL], 0.0).then_inc(consts, 1)
                pool.affine_select(out=half[:, GLOBAL:SEQ], in_=half[:, GLOBAL:SEQ], compare_op=ALU.is_ge, fill=0.0,
                                   base=-GLOBAL, pattern=[[0, SEQ - GLOBAL]],
                                   channel_multiplier=1).then_inc(consts, 1)
                n += 2
            pool.wait_ge(consts, n)

            def split_xT(u):
                pool.wait_ge(xT_hi_done, u + 1)
                pool.tensor_tensor(xT_lo[:, :, :], xT_raw[:, :, :], xT_hi[:, :, :].bitcast(F32), ALU.subtract) \
                    .then_inc(xT_lo_done, 1)

            def split_x(u):
                for e in range(2):
                    rows = slice(64 * e, 64 * e + 64)
                    pool.wait_ge(x_hi_done, 2 * u + e + 1)
                    pool.tensor_tensor(x_hl[rows, 1 - e, :, :], x_raw[rows, :, :], x_hl[rows, e, :, :].bitcast(F32),
                                       ALU.subtract).then_inc(x_lo_done, 1)
                    pool.wait_ge(x_lo_done, 2 * u + e + 1)

            def inverse_deviation(u):
                for p in range(PAIRS):
                    pool.wait_ge(var_done, PAIRS * u + p + 1)
                    pool.tensor_tensor(rstd[:, p, :], mean_var[:, p, 1:2], power[:, :], ALU.pow) \
                        .then_inc(rstd_done, 1)

            split_xT(0)
            split_x(0)
            split_xT(1)
            with pool.Fori(1, UNITS - 1) as u:
                split_x(u)
                inverse_deviation(u - 1)
                split_xT(u + 1)
            split_x(UNITS - 1)
            inverse_deviation(UNITS - 2)
            inverse_deviation(UNITS - 1)

        @block.tensor
        def _(pe):
            def scores(s):
                pe.wait_ge(qk_copied, HS * (s + 1))
                for p in range(PAIRS):
                    for hh in range(HS):
                        for b in range(2):
                            t = p * P + b * SEQ
                            last = pe.matmul(ps_s[b * SEQ:(b + 1) * SEQ, p, hh, :], qk[:, hh, 0, t:t + SEQ],
                                             qk[:, hh, 1, t:t + SEQ], start=True, stop=True)
                    last.then_inc(s_filled, 1)

            def turn(s, p):
                pe.wait_ge(normed, PAIRS * s + p + 1)
                dst = ps_s[:, p, :, :].rearrange("q h k -> q (h k)")
                for hp in range(HP):
                    last = pe.transpose(dst[:, hp * P:(hp + 1) * P], s_sb[:, p, 2 * hp:2 * hp + 2, :], ident[:, :])
                last.then_inc(t_filled, 1)

            def mix(s, unit, j, first):
                p, e, c = j // (2 * KC), j // KC % 2, j % KC
                if j == 0:
                    pe.wait_ge(x_lo_done, 2 * (unit + 1))
                if c == 0:
                    pe.wait_ge(pT_twice, 2 * (PAIRS * s + p) + e + 1)
                    pe.wait_ge(pT_lo_done, 2 * (PAIRS * s + p) + e + 1)
                if first and j < 2:
                    pe.wait_ge(fold_lo, B_LOADS * 2)
                else:
                    pe.wait_ge(mix_lo_done, JOBS * s + j - 1)
                rows = slice(64 * e, 64 * e + 64)
                for b in range(2):
                    cols = slice(c * P, (c + 1) * P)
                    dst = ps_mix[:, j % 2, b * 256:(b + 1) * 256]
                    pe.matmul(dst, x_hl[:, e, 2 * p + b, cols], pT_hi[:, e, p, b, :, :], start=True, stop=False)
                    last = pe.matmul(dst, x_hl[rows, e, 2 * p + b, cols], pT_lo[rows, p, b, :, :],
                                     start=False, stop=True)
                last.then_inc(mix_filled, 1)

            def output(s, unit, half, j, first):
                p, e, c = j // (2 * KC), j // KC % 2, j % KC
                pe.wait_ge(mix_lo_done, JOBS * s + j + 1)
                if half == 0 and j % (2 * KC) == 0 and not first:
                    pe.wait_ge(right_added, PAIRS * (unit - 1) + p + 1)
                for hp in range(HP):
                    k = (HS * half + 2 * hp + e) * KC + c
                    start = half == 0 and j % (2 * KC) == 0 and hp == 0
                    stop = half == STEPS - 1 and j % (2 * KC) == 2 * KC - 1 and hp == HP - 1
                    pe.matmul(ps_out[:, p, :, :], mix_hi[:, j % RING, hp, :], wvo[:, k, :, :],
                              start=start, stop=False)
                    last = pe.matmul(ps_out[:, p, 0, :], mix_lo[:, j % RING, hp, :], wvo[:, k, 0, :],
                                     start=False, stop=stop)
                last.then_inc(proj_done, 1)

            def step(unit, half, first, last):
                s = unit * STEPS + half
                scores(s)
                ahead = not (last and half == STEPS - 1)
                nh = (half + 1) % STEPS

                def next_projection(hh):
                    if ahead:
                        if nh == 0 and hh == 0:
                            pe.wait_ge(xT_lo_done, unit + 2)
                        if first and half == 0 and hh == 0:
                            pe.wait_ge(w_lo, W_LOADS)
                        project(s + 1, nh, hh, False)

                for hh in range(HS):
                    next_projection(hh)
                    if hh == HS - 4:
                        turn(s, 0)
                    if hh == HS - 3:
                        turn(s, 1)
                    if hh >= HS - 2:
                        mix(s, unit, hh - HS + 2, first and half == 0)
                for j in range(2, JOBS + 2):
                    if j < JOBS:
                        mix(s, unit, j, first and half == 0)
                    if j >= 2:
                        output(s, unit, half, j - 2, first)

            def project(s, half, hh, first):
                if not (first and hh < 2):
                    pe.wait_ge(qk_copied, HS * s + hh - 1)
                h = HS * half + hh
                for i in range(2):
                    dst = ps_qk[:, hh % 2, i, :]
                    n = 0
                    for c in range(KC):
                        hi = wqk_hi[:, i, c, h * P:(h + 1) * P]
                        lo = wqk_lo[:, i, c, h * P:(h + 1) * P]
                        for w, v in ((hi, xT_hi), (hi, xT_lo), (lo, xT_hi)):
                            last = pe.matmul(dst, w, v[:, c, :], start=(n == 0), stop=(n == 3 * KC - 1))
                            n += 1
                last.then_inc(qk_filled, 1)

            for g in range(B_LOADS):
                pe.wait_ge(staged[g % 3], staged_count(g))
                w = stage[g % 3].rearrange("p (h w d) -> p h w d", h=2, w=2)
                for hh in range(2):
                    h = 2 * g + hh
                    if g >= 2:
                        pe.wait_ge(fold_lo, h - 3)
                    for c in range(KC):
                        last = pe.matmul(fold_bank(h)[:, c * DIM:(c + 1) * DIM], w[:, hh, 0, c * P:(c + 1) * P],
                                         w[:, hh, 1, :], start=True, stop=True)
                    last.then_inc(fold_filled, 1)
            pe.wait_ge(consts, 12)
            pe.wait_ge(xT_lo_done, 1)
            pe.wait_ge(w_lo, W_LOADS // 2)
            for hh in range(HS):
                project(0, 0, hh, True)
            for half in range(STEPS):
                step(0, half, True, False)
            with pe.Fori(1, UNITS - 1) as u:
                for half in range(STEPS):
                    step(u, half, False, False)
            for half in range(STEPS):
                step(UNITS - 1, half, False, True)
            qrT, krT = first_weights(carried)
            pe.wait_ge(next_in, 32)
            for h in range(HEADS):
                for rows in (slice(0, 64), slice(64, P)):
                    pe.matmul(ps_s[rows, h // HS, h % HS, :], qrT[:, h, rows], krT[:, h, :], start=True, stop=True)
                at = slice(h % HS * LATENT, (h % HS + 1) * LATENT)
                last = pe.matmul(r1_bank_b[:, h // HS, at], qrT[:, h, P:Q_RANK], krT[:, h, :], start=True, stop=True)
            last.then_inc(r1_filled, 1)

        @block.scalar
        def _(act):
            def copy_qk(s, hh, first):
                act.wait_ge(qk_filled, HS * s + hh + 1)
                if first and hh == 0:
                    act.wait_ge(w_lo, W_LOADS // 2)
                if not first and hh == 0:
                    act.wait_ge(s_filled, PAIRS * s)
                nc.scalar.activation(qk[:, hh, :, :], ps_qk[:, hh % 2, :, :], ACT.Copy).then_inc(qk_copied, 1)

            def exponent(s, p):
                act.wait_ge(shifted, PAIRS * s + p + 1)
                nc.scalar.activation(s_sb[:, p, :, :], s_sb[:, p, :, :], ACT.Exp, scale=SCALE).then_inc(exped, 1)

            def probs_hi(s, p, first):
                act.wait_ge(t_filled, PAIRS * s + p + 1)
                if not first and p == 0:
                    act.wait_ge(mix_filled, JOBS * s)
                for e in range(2):
                    rows = slice(64 * e, 64 * e + 64)
                    src = ps_s[rows, p, :, :].rearrange("k h q -> k (h q)").rearrange("k (h b q) -> k b h q", h=HP, b=2)
                    nc.scalar.activation(pT_hi[rows, e, p, :, :, :], src, ACT.Copy).then_inc(pT_hi_done, 1)

            def probs_hi_again(s, p, e):
                own, other = slice(64 * e, 64 * e + 64), slice(64 - 64 * e, 128 - 64 * e)
                act.wait_ge(pT_hi_done, 2 * (PAIRS * s + p) + e + 1)
                nc.scalar.activation(pT_hi[other, e, p, :, :, :], pT_hi[own, e, p, :, :, :].bitcast(F32), ACT.Copy) \
                    .then_inc(pT_twice, 1)

            def mixed_hi(s, j, first):
                act.wait_ge(mix_filled, JOBS * s + j + 1)
                if not (first and j < RING):
                    act.wait_ge(proj_done, JOBS * s + j - RING + 1)
                src = ps_mix[:, j % 2, :].rearrange("d (b h q) -> d h b q", b=2, h=HP)
                nc.scalar.activation(mix_hi[:, j % RING, :, :].rearrange("d h (b q) -> d h b q", b=2), src,
                                     ACT.Copy).then_inc(mix_hi_done, 1)

            def xT_split(u, first=False):
                act.wait_ge(xT_in, 16 * (u + 1))
                if not first:
                    act.wait_ge(qk_filled, HEADS * u)
                nc.scalar.activation(xT_hi[:, :, :], xT_raw[:, :, :], ACT.Copy).then_inc(xT_hi_done, 1)

            def x_split(u, e, first=False):
                act.wait_ge(xd_in, 32 * (u + 1))
                if not first:
                    act.wait_ge(mix_filled, STEPS * JOBS * u)
                rows = slice(64 * e, 64 * e + 64)
                nc.scalar.activation(x_hl[rows, e, :, :], x_raw[rows, :, :], ACT.Copy).then_inc(x_hi_done, 1)

            def step(u, half, first=False, last=False):
                s = u * STEPS + half
                first, ahead = first and half == 0, not (last and half == STEPS - 1)

                def nxt(*hs):
                    for hh in hs:
                        if ahead:
                            copy_qk(s + 1, hh, False)
                for hh in range(2):
                    if half == 0 and not first:
                        x_split(u, hh)
                    nxt(hh)
                exponent(s, 0)
                nxt(2)
                exponent(s, 1)
                nxt(3, 4)
                probs_hi(s, 0, first)
                probs_hi_again(s, 0, 0)
                nxt(5)
                probs_hi_again(s, 0, 1)
                probs_hi(s, 1, first)
                nxt(6)
                mixed_hi(s, 0, first)
                probs_hi_again(s, 1, 0)
                nxt(7)
                mixed_hi(s, 1, first)
                probs_hi_again(s, 1, 1)
                for j in range(2, JOBS):
                    mixed_hi(s, j, first)
                if half == 0 and not last:
                    xT_split(u + 1)

            def weights_hi(n):
                src, landed = w_source(n)
                act.wait_ge(*landed)
                i, c, cols = w_piece(n)
                nc.scalar.activation(wqk_hi[:, i, c, cols], src, ACT.Copy).then_inc(w_hi, 1)

            for h in range(HEADS):
                act.wait_ge(fold_filled, h + 1)
                src = fold_bank(h).rearrange("p (c d) -> p c d", c=KC)
                nc.scalar.activation(wvo[:, h * KC:(h + 1) * KC, 0, :], src, ACT.Copy).then_inc(fold_hi, 1)
                if h % 3 == 1 and h > 1:
                    weights_hi(h // 3 - 1)
                if h == HEADS - 2:
                    xT_split(0, True)
            for hh in range(HS):
                copy_qk(0, hh, True)
                if hh % 2:
                    weights_hi(W_LOADS // 2 + hh // 2)
            for e in range(2):
                x_split(0, e, True)
            for half in range(STEPS):
                step(0, half, first=True)
            with act.Fori(1, UNITS - 1) as u:
                for half in range(STEPS):
                    step(u, half)
            for half in range(STEPS):
                step(UNITS - 1, half, last=True)
            r1_a, r1_b = first_fold(carried, rows_ahead)
            act.wait_ge(r1_filled, 1)
            nc.scalar.activation(r1_a, ps_s[:, :, :, :].rearrange("p n h d -> p (n h) d"), ACT.Copy)
            nc.scalar.activation(r1_b, r1_bank_b.rearrange("p n (h d) -> p (n h) d", d=LATENT), ACT.Copy)

        @block.vector
        def _(dve):
            mask_b = mask[:, :].unsqueeze(1).to_broadcast([P, HS, SEQ])

            def softmax_start(s, p):
                n = PAIRS * s + p + 1
                dve.wait_ge(s_filled, n)
                if not (isinstance(s, int) and s == 0):
                    dve.wait_ge(t_filled, n - PAIRS)
                dve.tensor_tensor(s_sb[:, p, :, :], ps_s[:, p, :, :], mask_b, ALU.add).then_inc(masked, 1)
                dve.wait_ge(masked, n)
                dve.tensor_reduce(row_max[:, p, :], s_sb[:, p, :, :], AX.X, ALU.max).then_inc(maxed, 1)
                dve.wait_ge(maxed, n)
                dve.tensor_tensor(s_sb[:, p, :, :], s_sb[:, p, :, :],
                                  row_max[:, p, :].unsqueeze(2).to_broadcast([P, HS, SEQ]),
                                  ALU.subtract).then_inc(shifted, 1)

            def softmax_end(s, p):
                n = PAIRS * s + p + 1
                dve.wait_ge(exped, n)
                dve.tensor_reduce(row_sum[:, p, :], s_sb[:, p, :, :], AX.X, ALU.add).then_inc(summed, 1)
                dve.wait_ge(summed, n)
                dve.reciprocal(inv_sum[:, p, :], row_sum[:, p, :]).then_inc(inverted, 1)
                dve.wait_ge(inverted, n)
                dve.tensor_tensor(s_sb[:, p, :, :], s_sb[:, p, :, :],
                                  inv_sum[:, p, :].unsqueeze(2).to_broadcast([P, HS, SEQ]),
                                  ALU.mult).then_inc(normed, 1)

            def probs_lo(s, p):
                for e in range(2):
                    rows = slice(64 * e, 64 * e + 64)
                    dve.wait_ge(pT_hi_done, 2 * (PAIRS * s + p) + e + 1)
                    src = ps_s[rows, p, :, :].rearrange("k h q -> k (h q)").rearrange("k (h b q) -> k b h q", h=HP, b=2)
                    dve.tensor_tensor(pT_lo[rows, p, :, :, :], src, pT_hi[rows, e, p, :, :, :].bitcast(F32),
                                      ALU.subtract).then_inc(pT_lo_done, 1)

            def mixed_lo(s, j):
                dve.wait_ge(mix_hi_done, JOBS * s + j + 1)
                src = ps_mix[:, j % 2, :].rearrange("d (b h q) -> d h b q", b=2, h=HP)
                hi = mix_hi[:, j % RING, :, :].rearrange("d h (b q) -> d h b q", b=2).bitcast(F32)
                lo = mix_lo[:, j % RING, :, :].rearrange("d h (b q) -> d h b q", b=2)
                dve.tensor_tensor(lo, src, hi, ALU.subtract).then_inc(mix_lo_done, 1)

            def residual(unit, p, first):
                n = PAIRS * unit + p + 1
                if p == 0:
                    dve.wait_ge(xr_in, 16 * (unit + 1))
                    dve.wait_ge(proj_done, STEPS * JOBS * (unit + 1))
                    if not first:
                        dve.wait_ge(stored, 16 * unit)
                dve.tensor_tensor(y[:, p, :], ps_out[:, p, 0, :], x_res[:, p, :], ALU.add).then_inc(left_added, 1)
                dve.wait_ge(left_added, n)
                dve.tensor_tensor(y[:, p, :], ps_out[:, p, 1, :], y[:, p, :], ALU.add).then_inc(right_added, 1)

            def moments(unit, p):
                n = PAIRS * unit + p + 1
                dve.wait_ge(right_added, n)
                dve.bn_stats(stats[:, p, :], y[:, p, :]).then_inc(stats_done, 1)
                dve.wait_ge(stats_done, n)
                dve.sem_inc(stats_seen, 1)
                dve.bn_aggr(mean_var[:, p, :], stats[:, p, :]).then_inc(moments_done, 1)
                dve.wait_ge(moments_done, n)
                dve.tensor_scalar(mean_var[:, p, 1:2], mean_var[:, p, 1:2], EPS, None, ALU.add).then_inc(var_done, 1)

            def normalise(unit, p):
                dve.wait_ge(rstd_done, PAIRS * unit + p + 1)
                dve.tensor_scalar(y[:, p, :], y[:, p, :], mean_var[:, p, 0:1], rstd[:, p, 0:1],
                                  ALU.subtract, ALU.mult).then_inc(y_done, 1)

            def step(unit, half, first):
                s = unit * STEPS + half
                softmax_start(s, 0)
                softmax_start(s, 1)
                softmax_end(s, 0)
                softmax_end(s, 1)
                behind = half == 0 and not first
                probs_lo(s, 0)
                mixed_lo(s, 0)
                if behind:
                    residual(unit - 1, 0, first=isinstance(unit, int) and unit == 1)
                mixed_lo(s, 1)
                probs_lo(s, 1)
                for j in range(2, JOBS):
                    mixed_lo(s, j)
                    if behind and j == 2:
                        residual(unit - 1, 1, first=False)
                    if behind and j in (3, 4):
                        moments(unit - 1, j - 3)
                    if behind and j in (5, 6):
                        normalise(unit - 1, j - 5)

            def weights_lo(n):
                dve.wait_ge(w_hi, n + 1)
                i, c, cols = w_piece(n)
                dve.tensor_tensor(wqk_lo[:, i, c, cols], w_source(n)[0], wqk_hi[:, i, c, cols].bitcast(F32),
                                  ALU.subtract).then_inc(w_lo, 1)

            for h in range(HEADS):
                dve.wait_ge(fold_hi, h + 1)
                src = fold_bank(h).rearrange("p (c d) -> p c d", c=KC)
                dve.tensor_tensor(wvo[:, h * KC:(h + 1) * KC, 1, :], src,
                                  wvo[:, h * KC:(h + 1) * KC, 0, :].bitcast(F32), ALU.subtract).then_inc(fold_lo, 1)
                if h % 3 == 1 and h > 1:
                    weights_lo(h // 3 - 1)
            for n in range(W_LOADS // 2, W_LOADS):
                weights_lo(n)
            dve.wait_ge(consts, 12)
            dve.wait_ge(w_lo, W_LOADS)
            for half in range(STEPS):
                step(0, half, True)
            with dve.Fori(1, UNITS) as u:
                for half in range(STEPS):
                    step(u, half, False)
            for p in range(PAIRS):
                residual(UNITS - 1, p, first=False)
                moments(UNITS - 1, p)
            for p in range(PAIRS):
                normalise(UNITS - 1, p)


INNER = 176
REST = INNER - P
W13 = KC * 2 * INNER
WALL = W13 + 2 * DIM
RAWS = 4
GROUP = 4


def raw_weights(carried):
    return carried[:, 0:RAWS * WALL].rearrange("p (n w) -> p n w", n=RAWS)


def weight_parts(w_raw, n, w1, w3, w2):
    w13 = w_raw[:, n, 0:W13].rearrange("p (c w i) -> p c w i", c=KC, w=2)
    return ((w13[:, :, 0, :], w1.rearrange("(c p) i -> p c i", p=P)),
            (w13[:, :, 1, :], w3.rearrange("(c p) i -> p c i", p=P)),
            (w_raw[:, n, W13:W13 + DIM], w2[0:P, :]),
            (w_raw[0:REST, n, W13 + DIM:WALL], w2[P:INNER, :]))


def latent_attention(nc, x, kv, rope, Wq, w_kc_qT, w_kc_kv, WoT, Ws_next, carried, rows_ahead, to_clear, out):
    HALL = HEADS // 2

    with ExitStack() as ctx:
        def sb(name, shape, dt=F32):
            return ctx.enter_context(nc.sbuf_tensor("l_" + name, shape, dt))

        def sem(name):
            return ctx.enter_context(nc.semaphore("l_" + name))

        wq = sb("wq", [P, HEADS, DIM])
        kcq_a = sb("kcq_a", [P, HEADS, P])
        kcq_b = sb("kcq_b", [QR, HEADS, P])
        kckv = sb("kckv", [P, HEADS, LATENT])
        woT = sb("woT", [P, HEADS, DIM])
        r1_a, r1_b = first_fold(carried, rows_ahead)
        r2 = sb("r2", [P, HEADS, LATENT])
        wm_hi = sb("wm_hi", [P, KC, HALL, P], F32R)
        wm_lo = sb("wm_lo", [P, KC, HALL, P], F32R)
        wn = sb("wn", [P, HALL, 2, DIM], F32R)
        ident = sb("ident", [P, P])
        power = sb("power", [P, 1])
        zeros = sb("zeros", [P, DIM])
        tables = sb("tables", [P, 2, LATENT])
        x_nat = sb("x_nat", [P, PAIRS, DIM])
        x_res = sb("x_res", [P, PAIRS, DIM])
        xT_hi = sb("xT_hi", [P, PAIRS, KC, P], F32R)
        xT_lo = sb("xT_lo", [P, PAIRS, KC, P], F32R)
        kv_in = sb("kv_in", [P, UB, LATENT])
        kv_cos = sb("kv_cos", [P, UB, LATENT])
        kv_sin = sb("kv_sin", [P, UB, LATENT])
        kv2 = sb("kv2", [P, UB, P])
        kv2_kept = sb("kv2_kept", [P, UB, P])
        kv2_hi = sb("kv2_hi", [P, UB, P], F32R)
        kv2_lo = sb("kv2_lo", [P, UB, P], F32R)
        kv2T = sb("kv2T", [P, UB, P])
        qm = sb("qm", [P, HP, UNIT])
        s_sb = sb("s_sb", [P, STEPS, PAIRS, HS, SEQ])
        row_max = sb("row_max", [P, STEPS, PAIRS, HS])
        row_sum = sb("row_sum", [P, STEPS, PAIRS, HS])
        inv_sum = sb("inv_sum", [P, STEPS, PAIRS, HS])
        pT_hi = sb("pT_hi", [P, PAIRS, 2, HP, SEQ], F32R)
        pT_lo = sb("pT_lo", [P, PAIRS, 2, HP, SEQ], F32R)
        mix_hi = sb("mix_hi", [P, PAIRS, HP, P], F32R)
        mix_lo = sb("mix_lo", [P, PAIRS, HP, P], F32R)
        y = sb("y", [P, PAIRS, DIM])
        stats = sb("stats", [P, PAIRS, 6])
        mean_var = sb("mean_var", [P, PAIRS, 2])
        rstd = sb("rstd", [P, PAIRS, 1])

        banks = ctx.enter_context(nc.psum_tensor("l_banks", [P, 8, 512], F32))
        ps_s = banks[:, 0:2, :].rearrange("p n (h k) -> p n h k", k=SEQ)
        ps_front = banks[:, 2:4, :]
        ps_mix = banks[:, 4:6, :]
        ps_out = banks[:, 6:8, :].rearrange("p n (w d) -> p n w d", w=2)

        next_in = sem("next_in")
        kcq_in = [sem(f"kcq_in{n}") for n in range(2)]
        wq_in = sem("wq_in")
        wn_in = sem("wn_in")
        tables_in = sem("tables_in")
        x_in = sem("x_in")
        kv_in_done = sem("kv_in_done")
        xr_in = sem("xr_in")
        stored = sem("stored")
        cleared = sem("cleared")
        r2_filled = sem("r2_filled")
        r2_copied = sem("r2_copied")
        wm_filled = sem("wm_filled")
        wm_hi_done = sem("wm_hi_done")
        wm_lo_done = sem("wm_lo_done")
        wn_filled = sem("wn_filled")
        wn_hi_done = sem("wn_hi_done")
        wn_lo_done = sem("wn_lo_done")
        consts = sem("consts")
        xT_filled = sem("xT_filled")
        xT_hi_done = sem("xT_hi_done")
        xT_lo_done = sem("xT_lo_done")
        cos_done = sem("cos_done")
        sin_done = sem("sin_done")
        rotated = sem("rotated")
        kvT_filled = sem("kvT_filled")
        kvT_copied = sem("kvT_copied")
        kv_kept = sem("kv_kept")
        kv_hi_done = sem("kv_hi_done")
        kv_lo_done = sem("kv_lo_done")
        qm_filled = sem("qm_filled")
        qm_copied = sem("qm_copied")
        s_filled = sem("s_filled")
        maxed = sem("maxed")
        shifted = sem("shifted")
        exped = sem("exped")
        summed = sem("summed")
        inverted = sem("inverted")
        normed = sem("normed")
        t_filled = sem("t_filled")
        pT_hi_done = sem("pT_hi_done")
        pT_lo_done = sem("pT_lo_done")
        mix_filled = sem("mix_filled")
        mix_hi_done = sem("mix_hi_done")
        mix_lo_done = sem("mix_lo_done")
        proj_done = sem("proj_done")
        left_added = sem("left_added")
        right_added = sem("right_added")
        stats_done = sem("stats_done")
        stats_seen = sem("stats_seen")
        moments_done = sem("moments_done")
        var_done = sem("var_done")
        rstd_done = sem("rstd_done")
        y_done = sem("y_done")

        block = ctx.enter_context(nc.Block())

        x_pairs = x.rearrange("(n p) d -> p n d", p=P)
        clear_tiles = to_clear.rearrange("(n p) d -> p n d", p=P)
        CLEAR = 2 * TOKENS // P // UNITS
        kv_batches = kv.rearrange("b t d -> t b d")
        out_pairs = out.rearrange("(n p) d -> p n d", p=P)

        @block.sync
        def _(sp):
            def load_x(u, first=False):
                if not first:
                    sp.wait_ge(xT_filled, u)
                sp.dma_start(x_nat[:, :, :], x_pairs[:, bass.ds(u * PAIRS, PAIRS), :]).then_inc(x_in, 16)

            def load_kv(u, first=False):
                if not first:
                    sp.wait_ge(cos_done, u)
                    sp.wait_ge(sin_done, u)
                for e in range(2):
                    sp.dma_start(kv_in[64 * e:64 * e + 64, :, :], kv_batches[:, bass.ds(u * UB, UB), :]) \
                        .then_inc(kv_in_done, 16)

            def clear(u):
                sp.dma_start(clear_tiles[:, bass.ds(u * CLEAR, CLEAR), :],
                             zeros[:, :].unsqueeze(1).to_broadcast([P, CLEAR, DIM])).then_inc(cleared, 16)

            def load_xres(u, first=False):
                if not first:
                    sp.wait_ge(left_added, PAIRS * u)
                sp.dma_start(x_res[:, :, :], x_pairs[:, bass.ds(u * PAIRS, PAIRS), :]).then_inc(xr_in, 16)

            def store(u):
                sp.wait_ge(y_done, PAIRS * (u + 1))
                sp.dma_start(out_pairs[:, bass.ds(u * PAIRS, PAIRS), :], y[:, :, :]).then_inc(stored, 16)

            for n in range(2):
                some = slice(8 * n, 8 * n + 8)
                sp.dma_start(kcq_a[:, some, :], w_kc_qT[some, 0:P, :].rearrange("h q k -> q h k")).then_inc(kcq_in[n], 16)
                sp.dma_start(kcq_b[:, some, :], w_kc_qT[some, P:Q_RANK, :].rearrange("h q k -> q h k")) \
                    .then_inc(kcq_in[n], 16)
            sp.dma_start(wq[:, :, :], Wq.rearrange("(h k) d -> k h d", k=P)).then_inc(wq_in, 16)
            sp.dma_start(kckv[:, :, :], w_kc_kv.rearrange("h k d -> k h d")).then_inc(wn_in, 16)
            sp.dma_start(woT[:, :, :], WoT.rearrange("(h k) d -> k h d", k=P)).then_inc(wn_in, 16)
            for e in range(2):
                sp.dma_start(tables[64 * e:64 * e + 64, :, :], rope.rearrange("w t d -> t w d")) \
                    .then_inc(tables_in, 16)
            load_x(0, True)
            load_kv(0, True)
            load_xres(0, True)
            for u in (1, 2):
                load_kv(u)
                load_x(u)
            sp.wait_ge(consts, 5)
            for u in (0, 1, UNITS - 1):
                clear(u)
            with sp.Fori(2, UNITS - 1) as u:
                load_kv(u + 1)
                load_x(u + 1)
                clear(u)
                store(u - 2)
                load_xres(u - 1)
            store(UNITS - 3)
            load_xres(UNITS - 2)
            sp.wait_ge(consts, 6)
            for dst, src in weight_parts(raw_weights(carried), 0, *Ws_next):
                sp.dma_start(dst, src).then_inc(next_in, 16)
            sp.wait_ge(stored, 16 * (UNITS - 2))
            sp.dma_start(rows_ahead.rearrange("p (n d) -> p n d", d=DIM), out_pairs[:, 0:GROUP, :]).then_inc(next_in, 16)
            store(UNITS - 2)
            load_xres(UNITS - 1)
            store(UNITS - 1)
            sp.wait_ge(next_in, 16 * 5)
            sp.wait_ge(cleared, 16 * UNITS)
            sp.wait_ge(stored, 16 * UNITS)

        @block.gpsimd
        def _(pool):
            def rotate(u, first=False):
                pool.wait_ge(kv_in_done, 32 * (u + 1))
                pool.tensor_tensor(kv_cos[:, :, :], kv_in[:, :, :],
                                   tables[:, 0, :].unsqueeze(1).to_broadcast([P, UB, LATENT]), ALU.mult) \
                    .then_inc(cos_done, 1)
                swapped = kv_in[:, :, :].rearrange("p b (w d) -> p b w d", w=2)
                sines = tables[:, 1, :].rearrange("p (w d) -> p w d", w=2)
                turned = kv_sin[:, :, :].rearrange("p b (w d) -> p b w d", w=2)
                for w in range(2):
                    last = pool.tensor_tensor(turned[:, :, w, :], swapped[:, :, 1 - w, :],
                                              sines[:, w, :].unsqueeze(1).to_broadcast([P, UB, LATENT // 2]), ALU.mult)
                last.then_inc(sin_done, 1)
                pool.wait_ge(cos_done, u + 1)
                pool.wait_ge(sin_done, u + 1)
                if not first:
                    pool.wait_ge(kvT_filled, u)
                    pool.wait_ge(kv_kept, u)
                for e in range(2):
                    rows, cols = slice(64 * e, 64 * e + 64), slice(64 * e, 64 * e + 64)
                    pool.tensor_tensor(kv2[rows, :, cols], kv_cos[rows, :, :], kv_sin[rows, :, :], ALU.add) \
                        .then_inc(rotated, 1)
                    pool.wait_ge(rotated, 2 * u + e + 1)

            def split_kv(u):
                pool.wait_ge(kv_hi_done, u + 1)
                pool.tensor_tensor(kv2_lo[:, :, :], kv2_kept[:, :, :], kv2_hi[:, :, :].bitcast(F32), ALU.subtract) \
                    .then_inc(kv_lo_done, 1)

            def normalise_probs(s, half):
                for p in range(PAIRS):
                    pool.wait_ge(inverted, PAIRS * s + p + 1)
                    pool.tensor_tensor(s_sb[:, half, p, :, :], s_sb[:, half, p, :, :],
                                       inv_sum[:, half, p, :].unsqueeze(2).to_broadcast([P, HS, SEQ]), ALU.mult) \
                        .then_inc(normed, 1)

            def inverse_deviation(u):
                for p in range(PAIRS):
                    pool.wait_ge(var_done, PAIRS * u + p + 1)
                    pool.tensor_tensor(rstd[:, p, :], mean_var[:, p, 1:2], power[:, :], ALU.pow).then_inc(rstd_done, 1)

            pool.memset(ident[:, :], 0.0).then_inc(consts, 1)
            pool.memset(power[:, :], -0.5).then_inc(consts, 1)
            pool.memset(kv2[:, :, :], 0.0).then_inc(consts, 1)
            pool.memset(zeros[:, :], 0.0).then_inc(consts, 1)
            pool.wait_ge(consts, 4)
            pool.affine_select(out=ident[:, :], in_=ident[:, :], compare_op=ALU.not_equal, fill=1.0,
                               base=0, pattern=[[-1, P]], channel_multiplier=1).then_inc(consts, 1)
            pool.wait_ge(tables_in, 32)
            rotate(0, True)
            rotate(1)
            normalise_probs(0, 0)
            split_kv(0)
            normalise_probs(1, 1)
            rotate(2)
            normalise_probs(STEPS, 0)
            split_kv(1)
            normalise_probs(STEPS + 1, 1)
            with pool.Fori(2, UNITS - 1) as u:
                rotate(u + 1)
                inverse_deviation(u - 2)
                normalise_probs(u * STEPS, 0)
                split_kv(u)
                normalise_probs(u * STEPS + 1, 1)
            inverse_deviation(UNITS - 3)
            normalise_probs((UNITS - 1) * STEPS, 0)
            split_kv(UNITS - 1)
            pool.wait_ge(wm_filled, 1)
            pool.memset(raw_weights(carried)[:, :, W13 + DIM:WALL], 0.0).then_inc(consts, 1)
            normalise_probs((UNITS - 1) * STEPS + 1, 1)
            inverse_deviation(UNITS - 2)
            inverse_deviation(UNITS - 1)

        @block.tensor
        def _(pe):
            def turn_inputs(u, first=False):
                pe.wait_ge(x_in, 16 * (u + 1))
                if not first:
                    pe.wait_ge(qm_copied, 4 * u - 1)
                for p in range(PAIRS):
                    for c in range(KC):
                        k = (p * KC + c) * P
                        last = pe.transpose(ps_front[:, 0, k:k + P], x_nat[:, p, c * P:(c + 1) * P], ident[:, :])
                last.then_inc(xT_filled, 1)
                pe.wait_ge(rotated, 2 * (u + 1))
                if not first:
                    pe.wait_ge(qm_copied, 4 * u)
                for b in range(UB):
                    last = pe.transpose(ps_front[:, 1, b * P:(b + 1) * P], kv2[:, b, :], ident[:, :])
                last.then_inc(kvT_filled, 1)

            def project(s, unit, half):
                for j in range(2):
                    if half == 0 and j == 0:
                        pe.wait_ge(xT_lo_done, unit + 1)
                    elif half == 0:
                        pe.wait_ge(kvT_copied, unit + 1)
                    else:
                        pe.wait_ge(qm_copied, 2 * s - 1 + j)
                    for i in range(2):
                        dst = ps_front[:, j, i * UNIT:(i + 1) * UNIT]
                        n = 0
                        for c in range(KC):
                            hi = wm_hi[:, c, half * HP + 2 * j + i, :]
                            lo = wm_lo[:, c, half * HP + 2 * j + i, :]
                            for w, v in ((hi, xT_hi), (hi, xT_lo), (lo, xT_hi)):
                                last = pe.matmul(dst, w, v[:, :, c, :], start=(n == 0), stop=(n == 3 * KC - 1))
                                n += 1
                    last.then_inc(qm_filled, 1)

            def scores(s, first=False):
                pe.wait_ge(qm_copied, 2 * (s + 1))
                for p in range(PAIRS):
                    if not first:
                        pe.wait_ge(shifted, PAIRS * (s - 1) + p + 1)
                    for hp in range(HP):
                        for b in range(2):
                            t = p * P + b * SEQ
                            last = pe.matmul(ps_s[b * SEQ:(b + 1) * SEQ, p, 2 * hp:2 * hp + 2, :], qm[:, hp, t:t + SEQ],
                                             kv2T[:, 2 * p + b, :], start=True, stop=True)
                    last.then_inc(s_filled, 1)

            def turn(s, half, first=False):
                for p in range(PAIRS):
                    pe.wait_ge(normed, PAIRS * s + p + 1)
                    if not first:
                        pe.wait_ge(mix_lo_done, PAIRS * (s - 1) + p + 1)
                    for hp in range(HP):
                        last = pe.transpose(ps_mix[:, p, hp * P:(hp + 1) * P],
                                            s_sb[:, half, p, 2 * hp:2 * hp + 2, :], ident[:, :])
                    last.then_inc(t_filled, 1)

            def mix(s, unit, half):
                if half == 0:
                    pe.wait_ge(kv_lo_done, unit + 1)
                for p in range(PAIRS):
                    pe.wait_ge(pT_lo_done, PAIRS * s + p + 1)
                    for b in range(2):
                        hi, lo = kv2_hi[:, 2 * p + b, :], kv2_lo[:, 2 * p + b, :]
                        for n, (w, v) in enumerate(((hi, pT_hi), (hi, pT_lo), (lo, pT_hi))):
                            last = pe.matmul(ps_mix[:, p, b * 256:(b + 1) * 256], w, v[:, p, b, :, :],
                                             start=(n == 0), stop=(n == 2))
                    last.then_inc(mix_filled, 1)

            def output(s, unit, half, first=False):
                for p in range(PAIRS):
                    pe.wait_ge(mix_lo_done, PAIRS * s + p + 1)
                    if half == 0 and not first:
                        pe.wait_ge(right_added, PAIRS * (unit - 1) + p + 1)
                    for hp in range(HP):
                        k = half * HP + hp
                        pe.matmul(ps_out[:, p, :, :], mix_hi[:, p, hp, :], wn[:, k, :, :], start=(k == 0), stop=False)
                        last = pe.matmul(ps_out[:, p, 0, :], mix_lo[:, p, hp, :], wn[:, k, 0, :],
                                         start=False, stop=(k == HALL - 1))
                    last.then_inc(proj_done, 1)

            halves = (slice(0, 64), slice(64, P))
            for h in range(HEADS):
                if h % 8 == 0:
                    pe.wait_ge(kcq_in[h // 8], 32)
                at = slice(h % 8 * LATENT, (h % 8 + 1) * LATENT)
                for rows in halves:
                    pe.matmul(banks[rows, 4 + h // 8, at], kcq_a[:, h, rows], r1_a[:, h, :], start=True, stop=False)
                for rows in halves:
                    last = pe.matmul(banks[rows, 4 + h // 8, at], kcq_b[:, h, rows], r1_b[:, h, :],
                                     start=False, stop=True)
            last.then_inc(r2_filled, 1)
            pe.wait_ge(r2_copied, 1)
            pe.wait_ge(wq_in, 16)
            for c in range(KC):
                for h in range(HEADS):
                    at = slice(h % 8 * LATENT, (h % 8 + 1) * LATENT)
                    for e in range(2):
                        last = pe.matmul(banks[halves[e], 2 * c + h // 8, at], wq[:, h, c * P + e * 64:c * P + e * 64 + 64],
                                         r2[:, h, :], start=True, stop=True)
            last.then_inc(wm_filled, 1)
            pe.wait_ge(wn_in, 32)
            for h in range(HEADS):
                if h == HEADS // 2:
                    pe.wait_ge(wm_lo_done, 1)
                    pe.wait_ge(consts, 5)
                    turn_inputs(0, True)
                rows = slice(h % 2 * 64, h % 2 * 64 + 64)
                last = pe.matmul(banks[rows, 4 + h // 4, h // 2 % 2 * DIM:(h // 2 % 2 + 1) * DIM], kckv[:, h, :],
                                 woT[:, h, :], start=True, stop=True)
            last.then_inc(wn_filled, 1)
            project(0, 0, 0)
            def first_half(u, first=False):
                s = u * STEPS
                scores(s)
                turn(s - 1, 1)
                output(s - 2, u - 1, 0, first)
                project(s + 1, u, 1)
                mix(s - 1, u - 1, 1)

            def second_half(u, ahead=True):
                s = u * STEPS
                scores(s + 1)
                if ahead:
                    turn_inputs(u + 1)
                turn(s, 0)
                output(s - 1, u - 1, 1)
                if ahead:
                    project(s + 2, u + 1, 0)
                mix(s, u, 0)

            scores(0, True)
            project(1, 0, 1)
            scores(1)
            turn_inputs(1)
            pe.wait_ge(wn_lo_done, 1)
            turn(0, 0, True)
            project(2, 1, 0)
            mix(0, 0, 0)
            first_half(1, first=True)
            second_half(1)
            with pe.Fori(2, UNITS - 1) as u:
                first_half(u)
                second_half(u)
            first_half(UNITS - 1)
            second_half(UNITS - 1, ahead=False)
            turn(UNITS * STEPS - 1, 1)
            output(UNITS * STEPS - 2, UNITS - 1, 0)
            mix(UNITS * STEPS - 1, UNITS - 1, 1)
            output(UNITS * STEPS - 1, UNITS - 1, 1)

        @block.scalar
        def _(act):
            def inputs_hi(u):
                act.wait_ge(xT_filled, u + 1)
                nc.scalar.activation(xT_hi[:, :, :, :], ps_front[:, 0, :], ACT.Copy).then_inc(xT_hi_done, 1)
                act.wait_ge(kvT_filled, u + 1)
                nc.scalar.activation(kv2T[:, :, :], ps_front[:, 1, :], ACT.Copy).then_inc(kvT_copied, 1)

            def copy_qm(s):
                for j in range(2):
                    act.wait_ge(qm_filled, 2 * s + j + 1)
                    nc.scalar.activation(qm[:, 2 * j:2 * j + 2, :], ps_front[:, j, :], ACT.Copy).then_inc(qm_copied, 1)

            def exponent(s, half, p):
                act.wait_ge(shifted, PAIRS * s + p + 1)
                nc.scalar.activation(s_sb[:, half, p, :, :], s_sb[:, half, p, :, :], ACT.Exp).then_inc(exped, 1)

            def probs_hi(s, p):
                act.wait_ge(t_filled, PAIRS * s + p + 1)
                src = ps_mix[:, p, :].rearrange("k (h b q) -> k b h q", h=HP, b=2)
                nc.scalar.activation(pT_hi[:, p, :, :, :], src, ACT.Copy).then_inc(pT_hi_done, 1)

            def mixed_hi(s, first=False):
                for p in range(PAIRS):
                    act.wait_ge(mix_filled, PAIRS * s + p + 1)
                    if not first:
                        act.wait_ge(proj_done, PAIRS * (s - 1) + p + 1)
                    src = ps_mix[:, p, :].rearrange("d (b h q) -> d h b q", b=2, h=HP)
                    nc.scalar.activation(mix_hi[:, p, :, :].rearrange("d h (b q) -> d h b q", b=2), src, ACT.Copy) \
                        .then_inc(mix_hi_done, 1)

            def keep_kv(u, first=False):
                act.wait_ge(rotated, 2 * (u + 1))
                if not first:
                    act.wait_ge(kv_lo_done, u)
                nc.scalar.activation(kv2_kept[:, :, :], kv2[:, :, :], ACT.Copy).then_inc(kv_kept, 1)

            def kv_split(u, first=False):
                act.wait_ge(kv_kept, u + 1)
                if not first:
                    act.wait_ge(mix_filled, STEPS * PAIRS * u)
                nc.scalar.activation(kv2_hi[:, :, :], kv2_kept[:, :, :], ACT.Copy).then_inc(kv_hi_done, 1)

            act.wait_ge(r2_filled, 1)
            nc.scalar.activation(r2[:, :, :], banks[:, 4:6, :], ACT.Copy).then_inc(r2_copied, 1)
            act.wait_ge(wm_filled, 1)
            nc.scalar.activation(wm_hi[:, :, :, :], banks[:, 0:4, :], ACT.Copy).then_inc(wm_hi_done, 1)
            inputs_hi(0)
            keep_kv(0, True)
            kv_split(0, True)
            act.wait_ge(wn_filled, 1)
            nc.scalar.activation(wn[:, :, 0, :], banks[:, 4:8, :].rearrange("p n (k d) -> p (n k) d", k=2),
                                 ACT.Copy).then_inc(wn_hi_done, 1)

            def first_half(u):
                s = u * STEPS
                mixed_hi(s - 2, isinstance(u, int) and u == 1)
                for p in range(PAIRS):
                    probs_hi(s - 1, p)
                    exponent(s, 0, p)
                copy_qm(s + 1)

            def second_half(u, ahead=True):
                s = u * STEPS
                mixed_hi(s - 1)
                kv_split(u)
                if ahead:
                    inputs_hi(u + 1)
                for p in range(PAIRS):
                    probs_hi(s, p)
                    exponent(s + 1, 1, p)
                if ahead:
                    keep_kv(u + 1)
                    copy_qm(s + 2)

            copy_qm(0)
            for p in range(PAIRS):
                exponent(0, 0, p)
            copy_qm(1)
            inputs_hi(1)
            for p in range(PAIRS):
                probs_hi(0, p)
                exponent(1, 1, p)
            keep_kv(1)
            copy_qm(2)
            first_half(1)
            second_half(1)
            with act.Fori(2, UNITS - 1) as u:
                first_half(u)
                second_half(u)
            first_half(UNITS - 1)
            second_half(UNITS - 1, ahead=False)
            mixed_hi(UNITS * STEPS - 2)
            for p in range(PAIRS):
                probs_hi(UNITS * STEPS - 1, p)
            mixed_hi(UNITS * STEPS - 1)

        @block.vector
        def _(dve):
            def inputs_lo(u):
                dve.wait_ge(xT_hi_done, u + 1)
                dve.tensor_tensor(xT_lo[:, :, :, :], ps_front[:, 0, :].rearrange("p (n c t) -> p n c t", n=PAIRS, c=KC),
                                  xT_hi[:, :, :, :].bitcast(F32), ALU.subtract).then_inc(xT_lo_done, 1)

            def softmax_start(s, half, pairs=range(PAIRS)):
                for p in pairs:
                    n = PAIRS * s + p + 1
                    dve.wait_ge(s_filled, n)
                    dve.tensor_reduce(row_max[:, half, p, :], ps_s[:, p, :, :], AX.X, ALU.max).then_inc(maxed, 1)
                    dve.wait_ge(maxed, n)
                    if not (isinstance(s, int) and s < STEPS):
                        dve.wait_ge(t_filled, n - STEPS * PAIRS)
                    dve.tensor_tensor(s_sb[:, half, p, :, :], ps_s[:, p, :, :],
                                      row_max[:, half, p, :].unsqueeze(2).to_broadcast([P, HS, SEQ]),
                                      ALU.subtract).then_inc(shifted, 1)

            def softmax_sum(s, half):
                for p in range(PAIRS):
                    n = PAIRS * s + p + 1
                    dve.wait_ge(exped, n)
                    dve.tensor_reduce(row_sum[:, half, p, :], s_sb[:, half, p, :, :], AX.X, ALU.add) \
                        .then_inc(summed, 1)
                    dve.wait_ge(summed, n)
                    dve.reciprocal(inv_sum[:, half, p, :], row_sum[:, half, p, :]).then_inc(inverted, 1)

            def probs_lo(s):
                for p in range(PAIRS):
                    dve.wait_ge(pT_hi_done, PAIRS * s + p + 1)
                    src = ps_mix[:, p, :].rearrange("k (h b q) -> k b h q", h=HP, b=2)
                    dve.tensor_tensor(pT_lo[:, p, :, :, :], src, pT_hi[:, p, :, :, :].bitcast(F32), ALU.subtract) \
                        .then_inc(pT_lo_done, 1)

            def mixed_lo(s):
                for p in range(PAIRS):
                    dve.wait_ge(mix_hi_done, PAIRS * s + p + 1)
                    src = ps_mix[:, p, :].rearrange("d (b h q) -> d h b q", b=2, h=HP)
                    hi = mix_hi[:, p, :, :].rearrange("d h (b q) -> d h b q", b=2).bitcast(F32)
                    dve.tensor_tensor(mix_lo[:, p, :, :].rearrange("d h (b q) -> d h b q", b=2), src, hi,
                                      ALU.subtract).then_inc(mix_lo_done, 1)

            def residual(unit, first=False):
                dve.wait_ge(xr_in, 16 * (unit + 1))
                dve.wait_ge(proj_done, STEPS * PAIRS * (unit + 1))
                if not first:
                    dve.wait_ge(stored, 16 * unit)
                for p in range(PAIRS):
                    dve.tensor_tensor(y[:, p, :], ps_out[:, p, 0, :], x_res[:, p, :], ALU.add).then_inc(left_added, 1)
                for p in range(PAIRS):
                    dve.wait_ge(left_added, PAIRS * unit + p + 1)
                    dve.tensor_tensor(y[:, p, :], ps_out[:, p, 1, :], y[:, p, :], ALU.add).then_inc(right_added, 1)
                for p in range(PAIRS):
                    n = PAIRS * unit + p + 1
                    dve.wait_ge(right_added, n)
                    dve.bn_stats(stats[:, p, :], y[:, p, :]).then_inc(stats_done, 1)
                    dve.wait_ge(stats_done, n)
                    dve.sem_inc(stats_seen, 1)
                    dve.bn_aggr(mean_var[:, p, :], stats[:, p, :]).then_inc(moments_done, 1)
                    dve.wait_ge(moments_done, n)
                    dve.tensor_scalar(mean_var[:, p, 1:2], mean_var[:, p, 1:2], EPS, None, ALU.add) \
                        .then_inc(var_done, 1)

            def normalise(unit):
                for p in range(PAIRS):
                    dve.wait_ge(rstd_done, PAIRS * unit + p + 1)
                    dve.tensor_scalar(y[:, p, :], y[:, p, :], mean_var[:, p, 0:1], rstd[:, p, 0:1],
                                      ALU.subtract, ALU.mult).then_inc(y_done, 1)

            dve.wait_ge(wm_hi_done, 1)
            dve.tensor_tensor(wm_lo[:, :, :, :].rearrange("p c n k -> p (c n k)"),
                              banks[:, 0:4, :].rearrange("p n k -> p (n k)"),
                              wm_hi[:, :, :, :].rearrange("p c n k -> p (c n k)").bitcast(F32), ALU.subtract) \
                .then_inc(wm_lo_done, 1)
            inputs_lo(0)
            dve.wait_ge(wn_hi_done, 1)
            dve.tensor_tensor(wn[:, :, 1, :], banks[:, 4:8, :].rearrange("p n (k d) -> p (n k) d", k=2),
                              wn[:, :, 0, :].bitcast(F32), ALU.subtract).then_inc(wn_lo_done, 1)

            def first_half(u):
                s = u * STEPS
                mixed_lo(s - 2)
                softmax_start(s, 0)
                probs_lo(s - 1)
                softmax_sum(s, 0)
                if not (isinstance(u, int) and u == 1):
                    normalise(u - 2)

            def second_half(u, ahead=True):
                s = u * STEPS
                mixed_lo(s - 1)
                softmax_start(s + 1, 1, [0])
                if ahead:
                    inputs_lo(u + 1)
                softmax_start(s + 1, 1, [1])
                probs_lo(s)
                softmax_sum(s + 1, 1)
                residual(u - 1, isinstance(u, int) and u == 1)

            softmax_start(0, 0)
            softmax_sum(0, 0)
            softmax_start(1, 1, [0])
            inputs_lo(1)
            softmax_start(1, 1, [1])
            probs_lo(0)
            softmax_sum(1, 1)
            first_half(1)
            second_half(1)
            with dve.Fori(2, UNITS - 1) as u:
                first_half(u)
                second_half(u)
            first_half(UNITS - 1)
            second_half(UNITS - 1, ahead=False)
            mixed_lo(UNITS * STEPS - 2)
            probs_lo(UNITS * STEPS - 1)
            normalise(UNITS - 2)
            mixed_lo(UNITS * STEPS - 1)
            residual(UNITS - 1)
            normalise(UNITS - 1)


def mixture(nc, x, gateT, gate_b, W1T, W3T, W2T, carried, rows_ahead, results, out):
    E, CAP = 16, 128
    TILES = TOKENS // P
    HOTS = 8
    RING = 4
    FEEDS = TILES + E
    FIELDS = 4
    FAR = float(1 << 20)
    LOW = -1e30

    with ExitStack() as ctx:
        def sb(name, shape, dt=F32):
            return ctx.enter_context(nc.sbuf_tensor("m_" + name, shape, dt))

        def ps(name):
            return ctx.enter_context(nc.psum_tensor("m_" + name, [P, 2, 512], F32))

        def sem(name):
            return ctx.enter_context(nc.semaphore("m_" + name))

        y_all = sb("y_all", [P, TILES, DIM])
        w_raw = raw_weights(carried)
        w_sh = sb("w_sh", [P, 2, WALL], F32R)
        w_ex = sb("w_ex", [P, 4, 2, WALL], F32R)
        gate_raw = sb("gate_raw", [P, KC, E])
        gate = sb("gate", [P, KC, 2, E], F32R)
        bias = sb("bias", [P, E])
        ident = sb("ident", [P, P])
        before = sb("before", [P, P])
        ones = sb("ones", [P, P])
        choice = sb("choice", [P, 2])
        token = sb("token", [P, TILES])
        place_no = sb("place_no", [P, CAP])
        rank = sb("rank", [P, E])
        go_on = sb("go_on", [P, E, TILES])
        power = sb("power", [P, 4])
        x_in = rows_ahead.rearrange("p (n d) -> p n d", d=DIM)
        x_ex = sb("x_ex", [P, 4, DIM])
        xT_hi = sb("xT_hi", [P, 4, KC, P], F32R)
        xT_lo = sb("xT_lo", [P, 4, KC, P], F32R)
        act_g = sb("act_g", [P, 2, INNER])
        h_all = sb("h_all", [P, TILES, INNER])
        h = sb("h", [P, 2, 2 * P])
        hT_hi = sb("hT_hi", [P, 2, 2, P], F32R)
        hT_lo = sb("hT_lo", [P, 2, 2, P], F32R)
        y_slot = sb("y_slot", [P, 2, DIM])
        logit = sb("logit", [P, TILES, E])
        routing = sb("routing", [P, 8, TILES, E])
        t1, t2, t3, t4, score, pick = (routing[:, n, :, :] for n in range(6))
        chosen = routing[:, 6:8, :, :]
        t5 = sb("t5", [P, TILES, E])
        tree = sb("tree", [P, TILES, E // 2])
        top = sb("top", [P, 2, TILES])
        place = sb("place", [P, 2, TILES])
        raw_w = sb("raw_w", [P, 2, TILES])
        total = sb("total", [P, TILES])
        inv_total = sb("inv_total", [P, TILES])
        w_hi = sb("w_hi", [P, 2, TILES], F32R)
        pos = sb("pos", [P, 2, TILES])
        counts = sb("counts", [P, E, TILES])
        running = sb("running", [P, E, TILES])
        queue = sb("queue", [P, TILES, E])
        fields = sb("fields", [P, 2, TILES, FIELDS, E], F32R)
        one_hot = sb("one_hot", [P, 2, HOTS, CAP], F32R)
        plan = sb("plan", [P, FIELDS, E])
        unfilled = sb("unfilled", [P, E])
        target = sb("target", [P, E])
        w_slot = sb("w_slot", [P, E])
        fetch_at = sb("fetch_at", [P, E], mybir.dt.uint32)
        send_at = sb("send_at", [P, E], mybir.dt.uint32)
        back = [v.rearrange("p (k n d) -> p k n d", k=2, d=DIM) for v in (
            routing[:, 0:4, :, :].rearrange("p n t e -> p (n t e)"),
            routing[:, 4:8, :, :].rearrange("p n t e -> p (n t e)"),
            carried[:, 0:2 * GROUP * DIM], carried[:, 2 * GROUP * DIM:4 * GROUP * DIM])]
        stats = sb("stats", [P, 4, 6])
        mean_var = sb("mean_var", [P, 2, 4, 2])
        rstd = sb("rstd", [P, 2, 4])
        shift = sb("shift", [P, 2, 4])

        ps_x, ps_g, ps_h, ps_y = ps("ps_x"), ps("ps_g"), ps("ps_h"), ps("ps_y")
        ps_logit = ps_y[:, :, :].rearrange("p n (t w e) -> p (n t) w e", w=2, e=E)

        gate_in = sem("gate_in")
        x_landed = [sem(f"x_landed{n}") for n in range(2)]
        w_landed = [sem(f"w_landed{n}") for n in range(RAWS)]
        ex_landed = [sem(f"ex_landed{n}") for n in range(4)]
        sent = [sem(f"sent{n}") for n in range(2)]
        back_in = [sem(f"back_in{n}") for n in range(RING)]
        stored = sem("stored")
        consts = sem("consts")
        gate_split = sem("gate_split")
        w_hi_done = sem("w_hi_done")
        w_lo_done = sem("w_lo_done")
        w2_lo_done = sem("w2_lo_done")
        x_filled = sem("x_filled")
        xT_hi_done = sem("xT_hi_done")
        xT_lo_done = sem("xT_lo_done")
        logits_filled = sem("logits_filled")
        chosen_done = sem("chosen_done")
        queue_done = sem("queue_done")
        routed = sem("routed")
        route_parts = sem("route_parts")
        hot_done = sem("hot_done")
        planned = sem("planned")
        targets_done = sem("targets_done")
        choices_added = sem("choices_added")
        all_added = sem("all_added")
        route_act = sem("route_act")
        route = sem("route")
        counted = sem("counted")
        g_filled = sem("g_filled")
        g_acted = sem("g_acted")
        h_done = sem("h_done")
        h_copied = sem("h_copied")
        hT_filled = sem("hT_filled")
        hT_hi_done = sem("hT_hi_done")
        hT_lo_done = sem("hT_lo_done")
        y_filled = sem("y_filled")
        shared_added = sem("shared_added")
        y_copied = sem("y_copied")
        stats_done = sem("stats_done")
        stats_seen = sem("stats_seen")
        moments_done = sem("moments_done")
        var_done = sem("var_done")
        rstd_done = sem("rstd_done")
        y_done = sem("y_done")


        block = ctx.enter_context(nc.Block())

        x_tiles = x.rearrange("(n p) d -> p n d", p=P)
        out_tiles = out.rearrange("(n p) d -> p n d", p=P)
        result_tiles = results.rearrange("(k n p) d -> p k n d", p=P, k=2)
        CONSTS = 12 + E
        CHUNKS = TILES // HOTS
        COUNT_AT = 4

        def pass_bank(k):
            return (ps_x, ps_h)[k % GROUP // 2][:, k % 2, :]

        @block.sync
        def _(sp):
            def load_pair(g, q, first=False):
                rows = x_tiles[:, bass.ds(GROUP * g + 2 * q, 2), :]
                if not first:
                    sp.wait_ge(x_filled, GROUP * (g - 1) + 2 * q + 2)
                    sp.dma_start(x_in[:, 2 * q:2 * q + 2, :], rows).then_inc(x_landed[q], 16)
                sp.dma_start(y_all[:, bass.ds(GROUP * g + 2 * q, 2), :], rows).then_inc(x_landed[q], 16)

            def load_weights(e, i):
                if not isinstance(e, int) or e >= 6:
                    sp.wait_ge(w2_lo_done, e - 5)
                elif e >= 3:
                    sp.wait_ge(w_lo_done, e - 2)
                for dst, src in weight_parts(w_raw, i % RAWS, W1T[e], W3T[e], W2T[e]):
                    sp.dma_start(dst, src).then_inc(w_landed[i % RAWS], 16)

            sp.dma_start(gate_raw[:, :, :], gateT.rearrange("(c p) e -> p c e", p=P)).then_inc(gate_in, 16)
            sp.dma_start(bias[:, :], gate_b.rearrange("(a e) -> a e", a=1).to_broadcast([P, E])).then_inc(gate_in, 16)
            load_pair(0, 0, True)
            load_pair(0, 1, True)
            with sp.Fori(1, TILES // GROUP) as g:
                for q in range(2):
                    load_pair(g, q)
            for e in range(4):
                load_weights(e, e + 1)
            for e in range(4, 8):
                load_weights(e, e + 1)
            with sp.Fori(2, E // RAWS) as u:
                for i in range(RAWS):
                    load_weights(RAWS * u + i, i + 1)

            for i in range(2):
                sp.wait_ge(sent[i], 16 * E // 2)

            def load_results(g, i):
                for k in range(2):
                    sp.dma_start(back[i][:, k, :, :], result_tiles[:, k, bass.ds(GROUP * g, GROUP), :]) \
                        .then_inc(back_in[i], 16)

            def store(g):
                sp.wait_ge(y_done, GROUP * g + GROUP)
                sp.dma_start(out_tiles[:, bass.ds(GROUP * g, GROUP), :], y_all[:, bass.ds(GROUP * g, GROUP), :]) \
                    .then_inc(stored, 16)

            for i in range(RING):
                load_results(i, i)
            with sp.Fori(1, TILES // GROUP // RING) as v:
                for i in range(RING):
                    sp.wait_ge(all_added, RING * (v - 1) + i + 1)
                    load_results(RING * v + i, i)
                    store(RING * (v - 1) + i)
            for i in range(RING):
                store(TILES // GROUP - RING + i)
            sp.wait_ge(stored, 16 * TILES // GROUP)

        @block.gpsimd
        def _(pool):
            pool.memset(ident[:, :], 0.0).then_inc(consts, 1)
            pool.wait_ge(consts, 1)
            pool.affine_select(out=ident[:, :], in_=ident[:, :], compare_op=ALU.not_equal, fill=1.0,
                               base=0, pattern=[[-1, P]], channel_multiplier=1).then_inc(consts, 1)
            pool.memset(ones[:, :], 1.0).then_inc(consts, 1)
            pool.memset(h[:, :, :], 0.0).then_inc(consts, 1)
            pool.memset(go_on[:, :, :], 1.0).then_inc(consts, 1)
            pool.memset(power[:, :], -0.5).then_inc(consts, 1)
            pool.wait_ge(consts, 6)
            pool.affine_select(out=before[:, :], in_=ones[:, :], compare_op=ALU.is_ge, fill=0.0,
                               base=-1, pattern=[[1, P]], channel_multiplier=-1).then_inc(consts, 1)
            pool.memset(go_on[:, :, 0:1], 0.0).then_inc(consts, 1)
            for e in range(E):
                pool.memset(rank[:, e:e + 1], float(E - e)).then_inc(consts, 1)

            for k in range(2):
                pool.memset(choice[:, k:k + 1], float(k + 1)).then_inc(consts, 1)
            pool.iota(token[:, :], pattern=[[P, TILES]], base=0, channel_multiplier=1,
                      allow_small_or_imprecise_dtypes=True).then_inc(consts, 1)
            pool.iota(place_no[:, :], pattern=[[1, CAP]], base=0, channel_multiplier=0,
                      allow_small_or_imprecise_dtypes=True).then_inc(consts, 1)
            pool.wait_ge(consts, CONSTS)

            done = 0

            def then(out, a, b, op):
                nonlocal done
                done += 1
                pool.tensor_tensor(out, a, b, op).then_inc(routed, 1)
                pool.wait_ge(routed, done)

            def experts(v):
                return v.unsqueeze(2).to_broadcast([P, TILES, E])

            def over_experts(out, v):
                n = E // 2
                then(tree[:, :, 0:n], v[:, :, 0:n], v[:, :, n:2 * n], ALU.add)
                while n > 2:
                    n //= 2
                    then(tree[:, :, 0:n], tree[:, :, 0:n], tree[:, :, n:2 * n], ALU.add)
                then(out.unsqueeze(2), tree[:, :, 0:1], tree[:, :, 1:2], ALU.add)

            for e in range(2):
                pool.wait_ge(w_hi_done, e + 2)
                pool.wait_ge(w_lo_done, e + 1)
                pool.tensor_tensor(w_ex[:, e, 1, :], w_raw[:, e + 1, :], w_ex[:, e, 0, :].bitcast(F32), ALU.subtract) \
                    .then_inc(w_lo_done, 1)
            pool.wait_ge(chosen_done, 1)
            for k in range(2):
                then(t1[:, :, :], score[:, :, :], chosen[:, k, :, :], ALU.mult)
                over_experts(raw_w[:, k, :], t1[:, :, :])
            pool.tensor_tensor(total[:, :], raw_w[:, 0, :], raw_w[:, 1, :], ALU.add).then_inc(route_parts, 1)

            def field(k, n, value):
                then(fields[:, k, :, n, :], chosen[:, k, :, :], experts(value), ALU.mult)

            def names(k):
                field(k, 0, token[:, :])
                field(k, 1, choice[:, k:k + 1].to_broadcast([P, TILES]))

            def weights(k):
                then(raw_w[:, k, :], raw_w[:, k, :], inv_total[:, :], ALU.mult)
                then(w_hi[:, k, :], raw_w[:, k, :], ones[:, 0:TILES], ALU.mult)
                then(raw_w[:, k, :], raw_w[:, k, :], w_hi[:, k, :].bitcast(F32), ALU.subtract)
                field(k, 2, w_hi[:, k, :].bitcast(F32))
                field(k, 3, raw_w[:, k, :])
                pool.sem_inc(route_parts, 1)

            names(0)
            pool.wait_ge(queue_done, 1)
            for k in range(2):
                then(t1[:, :, :], queue[:, :, :], chosen[:, k, :, :], ALU.mult)
                over_experts(pos[:, k, :], t1[:, :, :])
                pool.sem_inc(route_parts, 1)
            weights(0)
            names(1)
            weights(1)

            def fetch(e):
                if e >= 4:
                    pool.wait_ge(x_filled, TILES + e - 3)
                pool.indirect_dma_start(
                    out=x_ex[:, e % 4, :], out_offset=None, in_=x[:, :],
                    in_offset=bass.IndirectOffsetOnAxis(ap=fetch_at[:, e:e + 1], axis=0)).then_inc(ex_landed[e % 4], 16)

            pool.wait_ge(targets_done, 2)
            for e in range(4):
                fetch(e)
            for e in range(E):
                if e + 4 < E:
                    fetch(e + 4)
                if e + 2 < E:
                    pool.wait_ge(w_lo_done, e + 4)
                    pool.tensor_tensor(w_ex[:, (e + 2) % 4, 1, W13:WALL], w_raw[:, (e + 3) % RAWS, W13:WALL],
                                       w_ex[:, (e + 2) % 4, 0, W13:WALL].bitcast(F32), ALU.subtract) \
                        .then_inc(w2_lo_done, 1)
                pool.wait_ge(y_copied, e + 1)
                pool.indirect_dma_start(
                    out=results[:, :], out_offset=bass.IndirectOffsetOnAxis(ap=send_at[:, e:e + 1], axis=0),
                    in_=y_slot[:, e % 2, :], in_offset=None, bounds_check=2 * TOKENS - 1, oob_is_err=False) \
                    .then_inc(sent[e % 2], 16)

            def add_choices(v, i):
                pool.wait_ge(back_in[i], 32 * (v + 1))
                pool.tensor_tensor(back[i][:, 0, :, :], back[i][:, 0, :, :], back[i][:, 1, :, :], ALU.add) \
                    .then_inc(choices_added, 1)

            def inverse_deviation(g, i):
                pool.wait_ge(var_done, g + 1)
                pool.tensor_tensor(rstd[:, i, :], mean_var[:, i, :, 1], power[:, :], ALU.pow).then_inc(rstd_done, 1)
                pool.wait_ge(rstd_done, 2 * g + 1)
                pool.tensor_tensor(shift[:, i, :], mean_var[:, i, :, 0], rstd[:, i, :], ALU.mult).then_inc(rstd_done, 1)

            for i in range(RING):
                add_choices(0, i)
                if i:
                    inverse_deviation(i - 1, (i - 1) % 2)
            with pool.Fori(1, TILES // GROUP // RING) as v:
                for i in range(RING):
                    add_choices(v, i)
                    inverse_deviation(RING * v + i - 1, (i - 1) % 2)
            inverse_deviation(TILES // GROUP - 1, 1)

        @block.tensor
        def _(pe):
            def turn(bank, landed, src, left=None):
                if landed is not None:
                    pe.wait_ge(*landed)
                if left is not None:
                    pe.wait_ge(xT_lo_done, left)
                for c in range(KC):
                    last = pe.transpose(bank[:, c * P:(c + 1) * P], src[:, c * P:(c + 1) * P], ident[:, :])
                last.then_inc(x_filled, 1)

            def turn_tile(g, k, first=False):
                ahead = isinstance(g, int) and g * GROUP + k < GROUP
                turn(pass_bank(k), None if ahead else (x_landed[k % GROUP // 2], 32 * (g + k // GROUP) + 16), x_in[:, k % GROUP, :],
                     None if first else GROUP * g + k - 3)

            def turn_expert(g, k):
                turn(ps_x[:, k % 2, :], (ex_landed[k % 4], 16 * (g + k // 4 + 1)), x_ex[:, k % 4, :],
                     TILES + GROUP * g + k - 1)

            def logits(n, i):
                pe.wait_ge(xT_lo_done, n + 1)
                for c in range(KC):
                    pe.matmul(ps_logit[:, n, :, :], xT_hi[:, i, c, :], gate[:, c, :, :], start=(c == 0), stop=False)
                    last = pe.matmul(ps_logit[:, n, 0, :], xT_lo[:, i, c, :], gate[:, c, 0, :],
                                     start=False, stop=(c == KC - 1))
                last.then_inc(logits_filled, 1)

            def up(m, k, expert, first=False):
                i = k % 2
                t = i if expert else k % GROUP
                pe.wait_ge(xT_lo_done, m + 1)
                if expert:
                    pe.wait_ge(w_lo_done, m - TILES + 2)
                if not first:
                    pe.wait_ge(h_done, m - 1)
                w = w_ex[:, k % 4, :, :] if expert else w_sh
                dst = ps_g[:, i, 0:2 * INNER]
                n = 0
                for c in range(KC):
                    cols = slice(c * 2 * INNER, (c + 1) * 2 * INNER)
                    for v, part in ((xT_hi, 0), (xT_hi, 1), (xT_lo, 0)):
                        last = pe.matmul(dst, v[:, t, c, :], w[:, part, cols], start=(n == 0), stop=(n == 3 * KC - 1))
                        n += 1
                last.then_inc(g_filled, 1)

            def turn_inner(m, k, first=False, expert=True):
                i = k % 2
                pe.wait_ge(h_done if expert else h_copied, m + 1)
                if not first:
                    pe.wait_ge(hT_lo_done, m - 1)
                for c in range(2):
                    last = pe.transpose(ps_h[:, i, c * P:(c + 1) * P], h[:, i, c * P:(c + 1) * P], ident[:, :])
                last.then_inc(hT_filled, 1)

            def down(m, k, expert, first=False, chunk=None):
                i = k % 2
                pe.wait_ge(hT_lo_done, m + 1)
                if first:
                    pe.wait_ge(route, 1)
                elif expert == "later":
                    pe.wait_ge(y_copied, m - TILES - 1)
                else:
                    pe.wait_ge(shared_added, m - 1)
                if expert == "later":
                    pe.wait_ge(w2_lo_done, m - TILES - 1)
                if chunk is not None:
                    plan_part(chunk, 0)
                w = w_ex[:, k % 4, :, :] if expert else w_sh
                n = 0
                for c, rows in enumerate((P, REST)):
                    cols = slice(W13 + c * DIM, W13 + (c + 1) * DIM)
                    for v, part in ((hT_hi, 0), (hT_hi, 1), (hT_lo, 0)):
                        last = pe.matmul(ps_y[:, i, 0:DIM], v[0:rows, i, c, :], w[0:rows, part, cols],
                                         start=(n == 0), stop=(n == 5))
                        n += 1
                        if n == 6:
                            last.then_inc(y_filled, 1)
                        if chunk is not None:
                            plan_part(chunk, n)
                if chunk is not None:
                    plan_part(chunk, HOTS - 1).then_inc(planned, 1)

            def expert_group(g, first=False, last=False):
                for k in range(GROUP):
                    m = TILES + GROUP * g + k
                    if not (last and k == GROUP - 1):
                        turn_expert(g, k + 1)
                    up(m, k, True)
                    if not (first and k == 0):
                        turn_inner(m - 1, k + 3)
                    if not (first and k < 2):
                        down(m - 2, k + 2, "first" if first else "later")

            pe.wait_ge(consts, 2)
            for k in range(2):
                turn_tile(0, k, True)
            pe.wait_ge(consts, CONSTS)
            pe.wait_ge(gate_split, 2)
            pe.wait_ge(w_lo_done, 1)
            for k in range(GROUP):
                turn_tile(0, k + 2, k < 2)
                logits(k, k)
                up(k, k, False, k < 2)
            with pe.Fori(1, TILES // GROUP - 1) as g:
                for k in range(GROUP):
                    turn_tile(g, k + 2)
                    logits(GROUP * g + k, k)
                    up(GROUP * g + k, k, False)
            for k in range(GROUP):
                if k < 2:
                    turn_tile(TILES // GROUP - 1, k + 2)
                logits(TILES - GROUP + k, k)
                up(TILES - GROUP + k, k, False)

            def shared_job(m, k, chunk=None):
                turn_inner(m, k, False, expert=False)
                down(m - 1, k + 1, None, False, chunk)

            pe.wait_ge(xT_lo_done, TILES)
            for k in range(GROUP):
                turn_inner(k, k, k < 2, expert=False)
                if k >= 1:
                    down(k - 1, k - 1, None, k < 3)
            with pe.Fori(1, COUNT_AT) as g:
                for k in range(GROUP):
                    shared_job(GROUP * g + k, k)
            pe.wait_ge(chosen_done, 1)
            for n, lhs in enumerate((before, ones)):
                last = pe.matmul(ps_x[:, n, :], lhs[:, :], pick[:, :, :], start=True, stop=True)
            last.then_inc(counted, 1)
            with pe.Fori(COUNT_AT, TILES // GROUP - 2) as g:
                for k in range(GROUP):
                    shared_job(GROUP * g + k, k)
            pe.wait_ge(h_done, TILES)
            def plan_part(c, n):
                if n == 0 and c % CHUNKS == 0:
                    pe.wait_ge(route_parts, 4 + c // CHUNKS)
                if n == 0:
                    pe.wait_ge(hot_done, c + 1)
                return pe.matmul(ps_g[:, 0, 0:FIELDS * E], one_hot[:, c % 2, n, :],
                                 fields[:, c // CHUNKS, c % CHUNKS * HOTS + n, :, :],
                                 start=(c == 0 and n == 0), stop=(c == 2 * CHUNKS - 1 and n == HOTS - 1))

            for c in range(2 * CHUNKS):
                shared_job(TILES - 2 * CHUNKS + c, c % GROUP, c - 1 if c else None)
            down(TILES - 1, TILES - 1, None, chunk=2 * CHUNKS - 1)

            turn_expert(0, 0)
            expert_group(0, first=True)
            with pe.Fori(1, E // GROUP - 1) as g:
                expert_group(g)
            expert_group(E // GROUP - 1, last=True)
            turn_inner(FEEDS - 1, 3)
            down(FEEDS - 2, 2, "later")
            down(FEEDS - 1, 3, "later")

        @block.scalar
        def _(act):
            def x_hi_tile(g, k, first=False):
                act.wait_ge(x_filled, GROUP * g + k + 1)
                if not first:
                    act.wait_ge(g_filled, GROUP * (g - 1) + k + 1)
                nc.scalar.activation(xT_hi[:, k % GROUP, :, :], pass_bank(k)[:, 0:DIM], ACT.Copy) \
                    .then_inc(xT_hi_done, 1)

            def x_hi_expert(g, k):
                n = TILES + GROUP * g + k
                act.wait_ge(x_filled, n + 1)
                act.wait_ge(g_filled, n - 1)
                nc.scalar.activation(xT_hi[:, k % 2, :, :], ps_x[:, k % 2, 0:DIM], ACT.Copy).then_inc(xT_hi_done, 1)

            def split_weights(n, i, dst, e, first=False):
                if n is not None:
                    act.wait_ge(w_landed[i], n)
                if e is not None and not first:
                    act.wait_ge(y_filled, TILES + e - 3)
                nc.scalar.activation(dst, w_raw[:, i, :], ACT.Copy).then_inc(w_hi_done, 1)

            def g_act(m, k, first=False):
                i = k % 2
                act.wait_ge(g_filled, m + 1)
                if not first:
                    act.wait_ge(h_done, m - 1)
                nc.scalar.activation(act_g[:, i, :], ps_g[:, i, 0:INNER], ACT.Silu).then_inc(g_acted, 1)

            def h_hi(m, k, first=False):
                i = k % 2
                act.wait_ge(hT_filled, m + 1)
                if not first:
                    act.wait_ge(y_filled, m - 1)
                nc.scalar.activation(hT_hi[:, i, :, :], ps_h[:, i, 0:2 * P], ACT.Copy).then_inc(hT_hi_done, 1)

            def y_copy(m, k, first=False):
                i = k % 2
                act.wait_ge(y_filled, m + 1)
                if not first:
                    act.wait_ge(sent[i], 8 * (m - TILES - i))
                nc.scalar.activation(y_slot[:, i, :], ps_y[:, i, 0:DIM], ACT.Copy).then_inc(y_copied, 1)

            def h_copy(m, k, first=False):
                act.wait_ge(h_done, m + 1)
                if not first:
                    act.wait_ge(hT_filled, m - 1)
                nc.scalar.activation(h[:, k % 2, 0:INNER], h_all[:, m, :], ACT.Copy).then_inc(h_copied, 1)

            def shared_job(m, k, last=False):
                if not last:
                    h_copy(m + 1, k + 1)
                h_hi(m, k)

            def expert_group(g, first=False, last=False):
                for k in range(GROUP):
                    m = TILES + GROUP * g + k
                    if not (last and k == GROUP - 1):
                        x_hi_expert(g, k + 1)
                    g_act(m, k)
                    if not (first and k == 0):
                        h_hi(m - 1, k + 3)
                    if not (first and k < 2):
                        y_copy(m - 2, k + 2, first)
                    if not (last and k >= 2):
                        split_weights(64 * (g + 1 if k < 2 else g + 2), (k + 3) % RAWS, w_ex[:, (k + 2) % 4, 0, :],
                                      m - TILES + 2, first and k < 2)

            act.wait_ge(gate_in, 32)
            nc.scalar.activation(gate[:, :, 0, :], gate_raw[:, :, :], ACT.Copy).then_inc(gate_split, 1)
            x_hi_tile(0, 0, True)
            x_hi_tile(0, 1, True)
            split_weights(None, 0, w_sh[:, 0, :], None)
            for k in range(GROUP):
                x_hi_tile(0, k + 2, k < 2)
                g_act(k, k, k < 2)
            with act.Fori(1, TILES // GROUP - 1) as g:
                for k in range(GROUP):
                    x_hi_tile(g, k + 2)
                    g_act(GROUP * g + k, k)
            for k in range(GROUP):
                if k < 2:
                    x_hi_tile(TILES // GROUP - 1, k + 2)
                g_act(TILES - GROUP + k, k)

            act.wait_ge(logits_filled, TILES)
            nc.scalar.activation(logit[:, :, :], ps_logit[:, :, 0, :], ACT.Copy).then_inc(route_act, 1)
            for k in range(2):
                h_copy(k, k, True)
            h_hi(0, 0, True)
            act.wait_ge(route, 2)
            nc.scalar.activation(t2[:, :, :], t1[:, :, :], ACT.Exp, scale=-1.0).then_inc(route_act, 1)
            h_copy(2, 2)
            h_hi(1, 1, True)
            act.wait_ge(route, 3)
            nc.scalar.activation(t4[:, :, :], t3[:, :, :], ACT.Ln).then_inc(route_act, 1)
            for k in (2, 3):
                shared_job(k, k)
            act.wait_ge(route, 6)
            nc.scalar.activation(score[:, :, :], t5[:, :, :], ACT.Sqrt).then_inc(route_act, 1)
            for e in range(2):
                for k in (2 * e, 2 * e + 1):
                    shared_job(GROUP + k, k)
                split_weights(64, e + 1, w_ex[:, e, 0, :], e, True)
            with act.Fori(2, COUNT_AT) as g:
                for k in range(GROUP):
                    shared_job(GROUP * g + k, k)
            act.wait_ge(counted, 1)
            nc.scalar.activation(queue[:, :, :], ps_x[:, 0, :], ACT.Copy).then_inc(route_act, 1)
            nc.scalar.activation(counts[:, :, :].rearrange("p e t -> p t e"),
                                 ps_x[:, 1, :].rearrange("p (t e) -> p t e", e=E), ACT.Copy).then_inc(route_act, 1)
            with act.Fori(COUNT_AT, TILES // GROUP - 1) as g:
                for k in range(GROUP):
                    shared_job(GROUP * g + k, k)
            for k in range(GROUP):
                shared_job(TILES - GROUP + k, k, k == GROUP - 1)
            act.wait_ge(planned, 2 * CHUNKS)
            nc.scalar.activation(plan[:, :, :], ps_g[:, 0, 0:FIELDS * E], ACT.Copy).then_inc(route_act, 1)
            x_hi_expert(0, 0)
            expert_group(0, first=True)
            with act.Fori(1, E // GROUP - 1) as g:
                expert_group(g)
            expert_group(E // GROUP - 1, last=True)
            h_hi(FEEDS - 1, 3)
            y_copy(FEEDS - 2, 2)
            y_copy(FEEDS - 1, 3)

            def normalise(g, i):
                act.wait_ge(rstd_done, 2 * g + 2)
                for n in range(GROUP):
                    t = GROUP * g + n
                    nc.scalar.activation(y_all[:, t, :], y_all[:, t, :], ACT.Identity, bias=shift[:, i, n:n + 1],
                                         scale=rstd[:, i, n:n + 1]).then_inc(y_done, 1)

            for g in range(2):
                normalise(g, g)
            with act.Fori(1, TILES // GROUP // 2) as v:
                for i in range(2):
                    normalise(2 * v + i, i)

        @block.vector
        def _(dve):
            def x_lo(n, t, bank):
                dve.wait_ge(xT_hi_done, n + 1)
                dve.tensor_tensor(xT_lo[:, t, :, :], bank[:, 0:DIM].rearrange("p (c t) -> p c t", c=KC),
                                  xT_hi[:, t, :, :].bitcast(F32), ALU.subtract).then_inc(xT_lo_done, 1)

            def weights_lo(n, i, w, width=WALL):
                dve.wait_ge(w_hi_done, n)
                dve.tensor_tensor(w[:, 1, 0:width], w_raw[:, i, 0:width], w[:, 0, 0:width].bitcast(F32), ALU.subtract) \
                    .then_inc(w_lo_done, 1)

            def gated(m, k, expert, first=False):
                i = k % 2
                dve.wait_ge(g_acted, m + 1)
                if expert:
                    dve.wait_ge(hT_filled, m - 1)
                    dve.scalar_tensor_tensor(h[:, i, 0:INNER], ps_g[:, i, INNER:2 * INNER],
                                             w_slot[:, bass.ds(m - TILES, 1)], act_g[:, i, :],
                                             ALU.mult, ALU.mult).then_inc(h_done, 1)
                else:
                    dve.tensor_tensor(h_all[:, m, :], ps_g[:, i, INNER:2 * INNER], act_g[:, i, :], ALU.mult) \
                        .then_inc(h_done, 1)

            def h_lo(m, k):
                i = k % 2
                dve.wait_ge(hT_hi_done, m + 1)
                dve.tensor_tensor(hT_lo[:, i, :, :], ps_h[:, i, 0:2 * P].rearrange("p (c t) -> p c t", c=2),
                                  hT_hi[:, i, :, :].bitcast(F32), ALU.subtract).then_inc(hT_lo_done, 1)

            def add_shared(m, k):
                i = k % 2
                dve.wait_ge(y_filled, m + 1)
                dve.tensor_tensor(y_all[:, m, :], ps_y[:, i, 0:DIM], y_all[:, m, :], ALU.add).then_inc(shared_added, 1)

            def shared_job(m, k, first=False):
                h_lo(m, k)
                if not first:
                    add_shared(m - 1, k + 1)

            def expert_group(g, first=False, last=False):
                for k in range(GROUP):
                    m = TILES + GROUP * g + k
                    if not (last and k == GROUP - 1):
                        x_lo(m + 1, (k + 1) % 2, ps_x[:, (k + 1) % 2, :])
                    gated(m, k, True)
                    if not (first and k == 0):
                        h_lo(m - 1, k + 3)
                    if not (last and k >= 2):
                        weights_lo(m - TILES + 4, (k + 3) % RAWS, w_ex[:, (k + 2) % 4, :, :], W13)

            dve.wait_ge(gate_split, 1)
            dve.tensor_tensor(gate[:, :, 1, :], gate_raw[:, :, :], gate[:, :, 0, :].bitcast(F32), ALU.subtract) \
                .then_inc(gate_split, 1)
            for k in range(2):
                x_lo(k, k, pass_bank(k))
            weights_lo(1, 0, w_sh)
            with dve.Fori(0, TILES // GROUP - 1) as g:
                for k in range(GROUP):
                    x_lo(GROUP * g + k + 2, (k + 2) % GROUP, pass_bank(k + 2))
                    gated(GROUP * g + k, k, False)
            for k in range(GROUP):
                if k < 2:
                    x_lo(TILES - GROUP + k + 2, k + 2, pass_bank(k + 2))
                gated(TILES - GROUP + k, k, False)

            done = 0

            def then(instruction):
                nonlocal done
                done += 1
                instruction.then_inc(route, 1)
                dve.wait_ge(route, done)

            def experts(v):
                return v.unsqueeze(2).to_broadcast([P, TILES, E])

            def tiles(v):
                return v.unsqueeze(1).to_broadcast([P, TILES, E])

            dve.wait_ge(route_act, 1)
            then(dve.tensor_tensor(logit[:, :, :], ps_logit[:, :, 1, :], logit[:, :, :], ALU.add))
            then(dve.scalar_tensor_tensor(t1[:, :, :], logit[:, :, :], -1.0, logit[:, :, :], ALU.mult, ALU.max))
            for m in range(2):
                shared_job(m, m, m == 0)
            dve.wait_ge(route_act, 2)
            then(dve.tensor_scalar(t3[:, :, :], t2[:, :, :], 1.0, None, ALU.add))
            then(dve.scalar_tensor_tensor(t5[:, :, :], t3[:, :, :], -1.0, t2[:, :, :], ALU.add, ALU.subtract))
            for m in range(2, 4):
                shared_job(m, m)
            dve.wait_ge(route_act, 3)
            then(dve.tensor_tensor(t4[:, :, :], t4[:, :, :], t5[:, :, :], ALU.subtract))
            then(dve.scalar_tensor_tensor(t5[:, :, :], logit[:, :, :], 0.0, t4[:, :, :], ALU.max, ALU.add))
            for m in range(4, 6):
                shared_job(m, m)
            dve.wait_ge(consts, CONSTS)
            dve.wait_ge(route_act, 4)
            then(dve.tensor_tensor(pick[:, :, :], score[:, :, :], tiles(bias[:, :]), ALU.add))
            for k in range(2):
                then(dve.tensor_reduce(top[:, k, :], pick[:, :, :], AX.X, ALU.max))
                then(dve.tensor_tensor(t5[:, :, :], pick[:, :, :], experts(top[:, k, :]), ALU.is_equal))
                shared_job(6 + 3 * k, 3 * k)
                then(dve.tensor_tensor(t5[:, :, :], t5[:, :, :], tiles(rank[:, :]), ALU.mult))
                then(dve.tensor_reduce(place[:, k, :], t5[:, :, :], AX.X, ALU.max))
                shared_job(7 + 3 * k, 1 + 3 * k)
                then(dve.tensor_tensor(chosen[:, k, :, :], tiles(rank[:, :]), experts(place[:, k, :]), ALU.is_equal))
                if k == 0:
                    then(dve.scalar_tensor_tensor(pick[:, :, :], chosen[:, k, :, :], LOW, pick[:, :, :],
                                                  ALU.mult, ALU.add))
                    shared_job(8, 0)
            dve.tensor_tensor(pick[:, :, :], chosen[:, 0, :, :], chosen[:, 1, :, :], ALU.add).then_inc(chosen_done, 1)
            for m in range(11, GROUP * COUNT_AT):
                shared_job(m, m)
            dve.wait_ge(route_parts, 1)
            then(dve.reciprocal(inv_total[:, :], total[:, :]))
            dve.wait_ge(route_act, 6)
            then(dve.tensor_tensor_scan(running[:, :, :].rearrange("p e t -> p (e t)"),
                                        go_on[:, :, :].rearrange("p e t -> p (e t)"),
                                        counts[:, :, :].rearrange("p e t -> p (e t)"), 0.0, ALU.mult, ALU.add))
            then(dve.tensor_tensor(running[:, :, :], running[:, :, :], counts[:, :, :], ALU.subtract))
            dve.tensor_tensor(queue[:, :, :], queue[:, :, :], running[:, :, :].rearrange("p e t -> p t e"),
                              ALU.add).then_inc(queue_done, 1)
            with dve.Fori(COUNT_AT, TILES // GROUP - 2) as g:
                for k in range(GROUP):
                    shared_job(GROUP * g + k, k)
            for c in range(2 * CHUNKS):
                k, some = c // CHUNKS, slice(c % CHUNKS * HOTS, (c % CHUNKS + 1) * HOTS)
                if c % CHUNKS == 0:
                    dve.wait_ge(route_parts, k + 2)
                if c >= 2:
                    dve.wait_ge(planned, c - 1)
                dve.tensor_tensor(one_hot[:, c % 2, :, :], place_no[:, :].unsqueeze(1).to_broadcast([P, HOTS, CAP]),
                                  pos[:, k, some].unsqueeze(2).to_broadcast([P, HOTS, CAP]),
                                  ALU.is_equal).then_inc(hot_done, 1)
                shared_job(TILES - 2 * CHUNKS + c, c % GROUP)
            add_shared(TILES - 1, TILES - 1)
            dve.wait_ge(route_act, 7)
            dve.tensor_copy(fetch_at[:, :], plan[:, 0, :]).then_inc(targets_done, 1)
            then(dve.tensor_scalar(unfilled[:, :], plan[:, 1, :], 0.0, FAR, ALU.is_equal, ALU.mult))
            then(dve.scalar_tensor_tensor(target[:, :], plan[:, 1, :], float(TOKENS), plan[:, 0, :],
                                          ALU.mult, ALU.add))
            then(dve.scalar_tensor_tensor(target[:, :], target[:, :], -float(TOKENS), unfilled[:, :],
                                          ALU.add, ALU.add))
            dve.wait_ge(targets_done, 1)
            dve.tensor_copy(send_at[:, :], target[:, :]).then_inc(targets_done, 1)
            then(dve.tensor_tensor(w_slot[:, :], plan[:, 2, :], plan[:, 3, :], ALU.add))
            x_lo(TILES, 0, ps_x[:, 0, :])
            expert_group(0, first=True)
            with dve.Fori(1, E // GROUP - 1) as g:
                expert_group(g)
            expert_group(E // GROUP - 1, last=True)
            h_lo(FEEDS - 1, 3)
            def combine(g, r):
                i = r % 2
                dve.wait_ge(choices_added, g + 1)
                group = y_all[:, bass.ds(GROUP * g, GROUP), :]
                dve.tensor_tensor(group, group, back[r][:, 0, :, :], ALU.add).then_inc(all_added, 1)
                dve.wait_ge(all_added, g + 1)
                if not (isinstance(g, int) and g < 2):
                    dve.sem_inc(stats_seen, 1)
                    dve.wait_ge(y_done, GROUP * (g - 1))
                dve.sem_inc(stats_seen, 1)
                for n in range(GROUP):
                    dve.bn_stats(stats[:, n, :], y_all[:, GROUP * g + n, :]).then_inc(stats_done, 1)
                dve.wait_ge(stats_done, GROUP * (g + 1))
                dve.sem_inc(stats_seen, 1)
                for n in range(GROUP):
                    last = dve.bn_aggr(mean_var[:, i, n, :], stats[:, n, :])
                last.then_inc(moments_done, 1)
                dve.wait_ge(moments_done, 2 * g + 1)
                dve.tensor_scalar(mean_var[:, i, :, 1], mean_var[:, i, :, 1], EPS, None, ALU.add) \
                    .then_inc(moments_done, 1)
                dve.tensor_scalar(mean_var[:, i, :, 0], mean_var[:, i, :, 0], -1.0, None, ALU.mult) \
                    .then_inc(var_done, 1)

            for i in range(RING):
                combine(i, i)
            with dve.Fori(1, TILES // GROUP // RING) as v:
                for i in range(RING):
                    combine(RING * v + i, i)


def decoder_layer(nc, a, out):
    def scratch(name, rows):
        return nc.dram_tensor(name, [rows, DIM], F32).ap()

    x1, x2 = scratch("x1", TOKENS), scratch("x2", TOKENS)
    results = scratch("results", 2 * TOKENS)
    with ExitStack() as ctx:
        carried = ctx.enter_context(nc.sbuf_tensor("carried", [P, CARRIED], F32))[:, :]
        rows_ahead = ctx.enter_context(nc.sbuf_tensor("rows_ahead", [P, GROUP * DIM], F32))[:, :]
        local_attention(nc, a["x"], a["xT"], a["attn_Wq"], a["attn_Wk"], a["attn_WvT"], a["attn_Wo"],
                        a["xattn_W_qrT"], a["xattn_W_krT"], carried, rows_ahead, x1)
        latent_attention(nc, x1, a["ctx"], a["rope"], a["xattn_Wq"], a["xattn_w_kc_qT"], a["xattn_w_kc_kv"],
                         a["xattn_WoT"], (a["Ws1T"], a["Ws3T"], a["Ws2T"]), carried, rows_ahead, results, x2)
        mixture(nc, x2, a["gate_wT"], a["gate_b"], a["W1T"], a["W3T"], a["W2T"], carried, rows_ahead,
                results, out)



def rope_tables():
    import numpy as np
    steps = np.arange(0, 64, 2, dtype=np.float32) / np.float32(64)
    inv_freq = (np.float32(1.0) / np.float32(10000.0) ** steps).astype(np.float32)
    freqs = np.arange(SEQ, dtype=np.float32)[:, None] * inv_freq[None, :]
    cos, sin = np.repeat(np.cos(freqs), 2, axis=-1), np.repeat(np.sin(freqs), 2, axis=-1)
    sin[:, :32] = -sin[:, :32]
    return np.stack([cos, sin]).astype(np.float32)


def kernel(x, ctx_512, L0_attn_Wq, L0_attn_Wk, L0_attn_Wv, L0_attn_Wo, L0_xattn_Wq, L0_xattn_w_kc_q,
           L0_xattn_w_kc_kv, L0_xattn_W_qr, L0_xattn_W_kr, L0_xattn_Wo, L0_ffn_input_ids, L0_ffn_gate_w,
           L0_ffn_gate_b, L0_ffn_W1, L0_ffn_W3, L0_ffn_W2, L0_ffn_Ws1, L0_ffn_Ws3, L0_ffn_Ws2):
    import numpy as np
    import concourse.bacc as bacc
    from concourse.bass_utils import run_bass_kernel_spmd

    def turned(a):
        a = np.asarray(a)
        return np.ascontiguousarray(np.swapaxes(a, -1, -2))

    rows = np.ascontiguousarray(np.asarray(x).reshape(TOKENS, DIM))
    arrays = {
        "x": rows, "xT": turned(rows), "ctx": np.ascontiguousarray(ctx_512), "rope": rope_tables(),
        "attn_Wq": np.ascontiguousarray(L0_attn_Wq), "attn_Wk": np.ascontiguousarray(L0_attn_Wk),
        "attn_WvT": turned(L0_attn_Wv), "attn_Wo": np.ascontiguousarray(L0_attn_Wo),
        "xattn_Wq": np.ascontiguousarray(L0_xattn_Wq), "xattn_w_kc_qT": turned(L0_xattn_w_kc_q),
        "xattn_W_qrT": turned(L0_xattn_W_qr), "xattn_W_krT": turned(L0_xattn_W_kr),
        "xattn_w_kc_kv": np.ascontiguousarray(L0_xattn_w_kc_kv), "xattn_WoT": turned(L0_xattn_Wo),
        "gate_wT": turned(L0_ffn_gate_w), "gate_b": np.ascontiguousarray(L0_ffn_gate_b),
        "W1T": turned(L0_ffn_W1), "W3T": turned(L0_ffn_W3), "W2T": turned(L0_ffn_W2),
        "Ws1T": turned(L0_ffn_Ws1), "Ws3T": turned(L0_ffn_Ws3), "Ws2T": turned(L0_ffn_Ws2),
    }
    nc = bacc.Bacc("TRN2", target_bir_lowering=False, num_devices=1)
    aps = {n: nc.dram_tensor(n, a.shape, mybir.dt.from_np(a.dtype), kind="ExternalInput").ap()
           for n, a in arrays.items()}
    out = nc.dram_tensor("out", [TOKENS, DIM], F32, kind="ExternalOutput").ap()
    decoder_layer(nc, aps, out)
    result = run_bass_kernel_spmd(nc, [arrays], core_ids=[0])
    return result.results[0]["out"].reshape(BATCH, SEQ, DIM)
```
